# Optimizing a Trainium2 kernel written in Bass

```python
import numpy as np
import jax
import jax.numpy as jnp

def _softmax(x, axis=-1):
    return jax.nn.softmax(x, axis=axis)

def _gelu(x):
    return jax.nn.gelu(x, approximate=True)

def _silu(x):
    return jax.nn.silu(x)

def _sigmoid(x):
    return jax.nn.sigmoid(x)

def _layernorm(x, axis=-1, eps=1e-05):
    m = jnp.mean(x, axis=axis, keepdims=True)
    v = jnp.var(x, axis=axis, keepdims=True)
    return (x - m) / jnp.sqrt(v + eps)

def _scatter_add(tgt, idx, src, axis=0):
    return tgt.at[idx].add(src)

def _segment_sum(src, seg, n):
    return jax.ops.segment_sum(src, seg, n)
kernel_name = 'mk_adaln_d1_jaxref_r4_f0587b'

def setup_inputs(seed: int=0):
    np.random.seed(seed)
    _w = jnp.asarray

    def _L0_attn_setup():
        import jax, jax.numpy as jnp
        import numpy as np
        B, S, E, H, P = (2, 512, 256, 16, 512)
        HD = E // H
        key = jax.random.key(seed)
        ks = jax.random.split(key, 10)
        std = E ** (-0.5)
        x = jax.random.normal(ks[0], (B, S, E), jnp.float32)
        Wq = jax.random.normal(ks[1], (E, E), jnp.float32) * std
        Wk = jax.random.normal(ks[2], (E, E), jnp.float32) * std
        Wv = jax.random.normal(ks[3], (E, E), jnp.float32) * std
        Wo = jax.random.normal(ks[4], (E, E), jnp.float32) * std
        rel_key = jax.random.normal(ks[5], (P, HD), jnp.float32) * 0.02
        z = jnp.zeros((E,), jnp.float32)
        return {'x': x, 'Wq': Wq, 'bq': z, 'Wk': Wk, 'bk': z, 'Wv': Wv, 'bv': z, 'Wo': Wo, 'bo': z, 'rel_key': rel_key}
    _L0_attn_in = _L0_attn_setup()

    def _L0_ffn_setup():
        import jax, jax.numpy as jnp
        import numpy as np
        B, S, D, O, E, K = (2, 512, 256, 256, 8, 2)
        key = jax.random.key(seed)
        ks = jax.random.split(key, 6)

        def w(k, shape, fan_in):
            return jax.random.normal(k, shape, jnp.float32) * fan_in ** (-0.5)
        return {'x': jax.random.normal(ks[0], (B, S, D), jnp.float32), 'gate_w': w(ks[1], (E, D), D), 'gate_b': jnp.zeros((E,), jnp.float32), 'w1': w(ks[2], (E, D, O), D), 'b1': jnp.zeros((E, O), jnp.float32), 'w2': w(ks[3], (E, O, O), O), 'b2': jnp.zeros((E, O), jnp.float32), 'w3': w(ks[4], (E, O, O), O), 'b3': jnp.zeros((E, O), jnp.float32)}
    _L0_ffn_in = _L0_ffn_setup()
    _L0_c = _w((lambda *s: np.random.randn(*s).astype(np.float32) * 0.05)(4, 256))
    _L0_wmod = _w((lambda *s: np.random.randn(*s).astype(np.float32) * 0.05)(256, 6 * 256) * 256 ** (-0.5))
    _d = {'L0_attn_x': _L0_attn_in['x'], 'L0_attn_Wq': _L0_attn_in['Wq'], 'L0_attn_bq': _L0_attn_in['bq'], 'L0_attn_Wk': _L0_attn_in['Wk'], 'L0_attn_bk': _L0_attn_in['bk'], 'L0_attn_Wv': _L0_attn_in['Wv'], 'L0_attn_bv': _L0_attn_in['bv'], 'L0_attn_Wo': _L0_attn_in['Wo'], 'L0_attn_bo': _L0_attn_in['bo'], 'L0_attn_rel_key': _L0_attn_in['rel_key'], 'L0_ffn_gate_w': _L0_ffn_in['gate_w'], 'L0_ffn_gate_b': _L0_ffn_in['gate_b'], 'L0_ffn_w1': _L0_ffn_in['w1'], 'L0_ffn_b1': _L0_ffn_in['b1'], 'L0_ffn_w2': _L0_ffn_in['w2'], 'L0_ffn_b2': _L0_ffn_in['b2'], 'L0_ffn_w3': _L0_ffn_in['w3'], 'L0_ffn_b3': _L0_ffn_in['b3'], 'L0_c': _L0_c, 'L0_wmod': _L0_wmod}
    _x0 = _d['L0_attn_x']
    _d['L0_attn_x'] = jax.random.normal(jax.random.fold_in(jax.random.key(seed), 1), (4, 2048, 256), dtype=_x0.dtype)
    del _x0
    return _d

def reference(L0_attn_x, L0_attn_Wq, L0_attn_bq, L0_attn_Wk, L0_attn_bk, L0_attn_Wv, L0_attn_bv, L0_attn_Wo, L0_attn_bo, L0_attn_rel_key, L0_ffn_gate_w, L0_ffn_gate_b, L0_ffn_w1, L0_ffn_b1, L0_ffn_w2, L0_ffn_b2, L0_ffn_w3, L0_ffn_b3, L0_c, L0_wmod):

    def _L0_attn_ref(x, Wq, bq, Wk, bk, Wv, bv, Wo, bo, rel_key):
        import jax, jax.numpy as jnp
        import numpy as np
        B, S, E, H, P = (2, 512, 256, 16, 512)
        HD = E // H
        b, s, e = x.shape
        p, hd = rel_key.shape
        h = e // hd
        scale = hd ** (-0.5)

        def split_heads(t):
            return t.reshape(b, s, h, hd).transpose(0, 2, 1, 3)
        q = split_heads(x @ Wq + bq)
        k = split_heads(x @ Wk + bk)
        v = split_heads(x @ Wv + bv)
        scores = jnp.einsum('bhid,bhjd->bhij', q, k)
        rel = jnp.einsum('bhid,pd->bhip', q, rel_key)
        i = jnp.arange(s)[:, None]
        j = jnp.arange(s)[None, :]
        rel_idx = jnp.clip(j - i + p - 1, 0, p - 1)
        bias = jnp.take_along_axis(rel, jnp.broadcast_to(rel_idx[None, None], (b, h, s, s)), axis=3)
        causal = j <= i
        logits = jnp.where(causal[None, None], (scores + bias) * scale, -jnp.inf)
        attn = jax.nn.softmax(logits, axis=-1)
        out = jnp.einsum('bhij,bhjd->bhid', attn, v)
        out = out.transpose(0, 2, 1, 3).reshape(b, s, e)
        return out @ Wo + bo

    def _L0_ffn_ref(x, gate_w, gate_b, w1, b1, w2, b2, w3, b3):
        import jax, jax.numpy as jnp
        import numpy as np
        B, S, D, O, E, K = (2, 512, 256, 256, 8, 2)
        probs = jax.nn.softmax(x @ gate_w.T + gate_b, axis=-1)
        _, topi = jax.lax.top_k(probs, K)
        onehot = jax.nn.one_hot(topi, E, dtype=probs.dtype)
        cw = jnp.einsum('bske,bsk->bse', onehot, probs[..., :K])
        out = jnp.zeros(x.shape[:2] + (O,), x.dtype)
        for e in range(E):
            h = jax.nn.relu(x @ w1[e] + b1[e])
            h = jax.nn.relu(h @ w2[e] + b2[e])
            h = h @ w3[e] + b3[e]
            out = out + cw[..., e:e + 1] * h
        return out
    x = L0_attn_x
    mod = (_silu(L0_c) @ L0_wmod).reshape(L0_c.shape[0], 6, 1, -1)
    sa, ca, ga, sb, cb, gb = (mod[:, 0], mod[:, 1], mod[:, 2], mod[:, 3], mod[:, 4], mod[:, 5])
    ga = (2 * (ga >= 0) - 1) * jnp.maximum(jnp.abs(ga), 0.25)
    gb = (2 * (gb >= 0) - 1) * jnp.maximum(jnp.abs(gb), 0.25)
    h = _layernorm(x, axis=-1) * (1 + ca) + sa
    x = x + ga * _L0_attn_ref(h, L0_attn_Wq, L0_attn_bq, L0_attn_Wk, L0_attn_bk, L0_attn_Wv, L0_attn_bv, L0_attn_Wo, L0_attn_bo, L0_attn_rel_key)
    h = _layernorm(x, axis=-1) * (1 + cb) + sb
    x = x + gb * _L0_ffn_ref(h, L0_ffn_gate_w, L0_ffn_gate_b, L0_ffn_w1, L0_ffn_b1, L0_ffn_w2, L0_ffn_b2, L0_ffn_w3, L0_ffn_b3)
    return x

_drawn_inputs = setup_inputs


def setup_inputs(seed=0):
    import zlib

    import numpy as np

    out = dict(_drawn_inputs(seed))
    spreads = {'L0_attn_bq': (0.0, 2.0),
     'L0_attn_bk': (0.0, 2.0),
     'L0_attn_bv': (0.0, 0.305),
     'L0_attn_bo': (0.0, 0.323),
     'L0_ffn_gate_b': (0.0, 0.611),
     'L0_ffn_b1': (0.0, 2.0),
     'L0_ffn_b2': (0.0, 2.0),
     'L0_ffn_b3': (0.0, 0.8)}
    factors = {'L0_attn_rel_key': 53.731, 'L0_ffn_w1': 2.689}
    for name, (base, spread) in spreads.items():
        noise = np.random.default_rng([zlib.crc32(name.encode()), seed]).standard_normal(out[name].shape)
        drawn = base * np.exp(spread * noise) if base else spread * noise
        out[name] = jnp.asarray(drawn.astype(out[name].dtype))
    for name, factor in factors.items():
        out[name] = (out[name] * factor).astype(out[name].dtype)
    return out
```

```python
from contextlib import ExitStack

import concourse.bass as bass
from concourse import mybir

ALU = mybir.AluOpType
ACT = mybir.ActivationFunctionType
AX = mybir.AxisListType
F32 = mybir.dt.float32
F16 = mybir.dt.float16
U32 = mybir.dt.uint32

B, S, E = 4, 2048, 256
H, D, W = 16, 16, 512
P = 128
NB = S // P
EH = E // P
HH = 8
CH = 512
CPB = S // CH
NX, TOP = 8, 2
G = 8
EPS = 1e-5
SCALE = D ** -0.5
KR = 4 * D + 1
NJ = W // P + 1
TAB = 760
TAB0 = 632
FARI = NJ
MASK = 30000.0


class PhaseMemory:

    def __init__(self, nc, tag):
        self.nc, self.tag, self.ctx, self.taken = nc, tag, ExitStack(), []

    def __enter__(self):
        return self

    def __exit__(self, *a):
        self.nc.clear_and_free_semaphores(self.taken)
        self.nc.all_engine_barrier()
        return self.ctx.__exit__(*a)

    def sb(self, name, shape, dt=F32):
        return self.ctx.enter_context(self.nc.sbuf_tensor(f"{self.tag}_{name}", shape, dt))

    def ps(self, name, shape):
        return self.ctx.enter_context(self.nc.psum_tensor(f"{self.tag}_{name}", shape, F32))

    def sem(self, name):
        self.taken.append(self.nc.alloc_semaphore(name=f"{self.tag}_{name}"))
        return self.taken[-1]

    def sems(self, name, n):
        return [self.sem(f"{name}{i}") for i in range(n)]


def phase_modulation(nc, io, keep):
    with PhaseMemory(nc, "mod") as a:
        cT = a.sb("cT", [P, EH, B])
        e_c = a.sb("e_c", [P, EH, B])
        den = a.sb("den", [P, EH, B])
        rec = a.sb("rec", [P, EH, B])
        silu = a.sb("silu", [P, EH, B])
        silu_b = a.sb("silu_b", [P, EH, B, P])
        wmod = a.sb("wmod", [P, EH, 6 * E])
        mag = a.sb("mag", [P, 2, B, E])
        raw = a.sb("raw", [P, 2, B, E])
        sgn = a.sb("sgn", [P, 2, B, E])
        relT = a.sb("relT", [D, W])
        relx = a.sb("relx", [D, TAB + 2 * G])
        relh = a.sb("relh", [D, TAB + 2 * G], F16)
        rell = a.sb("rell", [D, TAB + 2 * G], F16)
        mask_dh = a.sb("mask_dh", [P, D, HH])
        pm = a.ps("pm", [P, 12, B])
        pg = [a.ps(f"pg{i}", [P, 2, E]) for i in range(4)]
        loaded, wloaded = a.sem("loaded"), a.sem("wloaded")
        pool_step, act_exp, dve_step = a.sem("pool_step"), a.sem("act_exp"), a.sem("dve_step")
        silu_ready, mod_ready, gate_ready = a.sem("silu_ready"), a.sem("mod_ready"), a.sem("gate_ready")
        rel_ready, table_out, table_in = a.sem("rel_ready"), a.sem("table_out"), a.sem("table_in")
        rel_step = a.sem("rel_step")
        with nc.Block() as block:

            @block.sync
            def _(sp):
                sp.dma_start(cT[:, :, :], io["cT"].rearrange("(e p) b -> p e b", p=P)).then_inc(loaded, 16)
                sp.dma_start(relT[:, :], io["relT"]).then_inc(loaded, 16)
                sp.dma_start(wmod[:, :, :], io["wmod"].rearrange("(e p) n -> p e n", p=P)).then_inc(wloaded, 16)
                sp.wait_ge(rel_ready, 1)
                sp.dma_start(io["s_rel"][0], relh[:, :]).then_inc(table_out, 16)
                sp.dma_start(io["s_rel"][1], rell[:, :]).then_inc(table_out, 16)
                sp.wait_ge(table_out, 32)
                for part in range(2):
                    for i in range(G):
                        sp.dma_start(keep["table"][i * D:(i + 1) * D, part, :],
                                     io["s_rel"][part][:, G - 1 - i:G - 1 - i + TAB]).then_inc(table_in, 16)
                sp.wait_ge(table_in, 32 * G)

            @block.gpsimd
            def _(pool):
                pool.memset(keep["ident"][:, :], 0.0)
                pool.memset(mask_dh[:, :, :], 1.0)
                pool.memset(keep["mask_i"][:, :], 1.0)
                pool.memset(keep["ident_s"][:, :, :], MASK)
                pool.memset(keep["mask_f"][:, :], -MASK)
                pool.memset(keep["iota8"][:, :], 0.0)
                pool.memset(keep["spread"][:, :], 0.0).then_inc(pool_step, 1)
                pool.wait_ge(pool_step, 1)
                pool.affine_select(out=keep["ident"][:, :], in_=keep["ident"][:, :], compare_op=ALU.not_equal,
                                   fill=1.0, base=0, pattern=[[-1, P]], channel_multiplier=1)
                pool.affine_select(out=keep["mask_i"][:, :], in_=keep["mask_i"][:, :], compare_op=ALU.is_ge,
                                   fill=0.0, base=0, pattern=[[-D, G]], channel_multiplier=1)
                pool.affine_select(out=keep["ident_s"][:, :, :], in_=keep["ident_s"][:, :, :], compare_op=ALU.is_equal,
                                   fill=0.0, base=0, pattern=[[0, H], [-1, G]], channel_multiplier=1)
                pool.affine_select(out=keep["mask_f"][:, :], in_=keep["mask_f"][:, :], compare_op=ALU.is_ge,
                                   fill=0.0, base=-1, pattern=[[1, G]], channel_multiplier=-1)
                pool.affine_select(out=mask_dh[:, :, :], in_=mask_dh[:, :, :], compare_op=ALU.is_equal,
                                   fill=0.0, base=0, pattern=[[-HH, D], [-1, HH]], channel_multiplier=1)
                for n in range(1, NX):
                    pool.memset(keep["iota8"][:, n:n + 1], float(n))
                for q in range(4):
                    v = keep["spread"][:, 32 * q:32 * q + 32]
                    last = pool.affine_select(out=v, in_=v, compare_op=ALU.not_equal, fill=1.0,
                                              base=-(32 * q + D), pattern=[[0, 32]], channel_multiplier=1)
                last.then_inc(pool_step, 1)
                pool.wait_ge(pool_step, 2)
                pool.affine_select(out=keep["mask_i"][:, :], in_=keep["mask_i"][:, :], compare_op=ALU.is_ge,
                                   fill=0.0, base=D - 1, pattern=[[D, G]], channel_multiplier=-1).then_inc(pool_step, 1)
                pool.wait_ge(pool_step, 3)

            @block.scalar
            def _(act):
                act.wait_ge(loaded, 32)
                act.activation(e_c[:, :, :], cT[:, :, :], ACT.Exp, scale=-1.0).then_inc(act_exp, 1)

            @block.vector
            def _(dve):
                n = [0]

                def link(ins):
                    n[0] += 1
                    ins.then_inc(dve_step, 1)
                    dve.wait_ge(dve_step, n[0])

                dve.wait_ge(act_exp, 1)
                link(dve.tensor_scalar(den[:, :, :], e_c[:, :, :], 1.0, None, ALU.add))
                link(dve.reciprocal(rec[:, :, :], den[:, :, :]))
                dve.wait_ge(loaded, 32)
                link(dve.tensor_tensor(silu[:, :, :], cT[:, :, :], rec[:, :, :], ALU.mult))
                dve.tensor_copy(silu_b[:, :, :, :], silu[:, :, :].unsqueeze(3).broadcast_to([P, EH, B, P])).then_inc(silu_ready, 1)
                link(dve.tensor_scalar(relx[:, P:P + W], relT[:, :], relT[:, 0:1], None, ALU.subtract))
                dve.memset(relx[:, 0:P], 0.0)
                link(dve.tensor_copy(relx[:, P + W:], relx[:, P + W - 1:P + W].broadcast_to([D, TAB + 2 * G - P - W])))
                link(dve.tensor_copy(relh[:, :], relx[:, :]))
                dve.tensor_tensor(rell[:, :], relx[:, :], relh[:, :], ALU.subtract).then_inc(rel_ready, 1)
                dve.wait_ge(pool_step, 2)
                with nc.allow_low_precision("zeros and one one"):
                    dve.tensor_reduce(keep["mask_h"][:, :], mask_dh[:, :, :].rearrange("p d h -> p h d"), AX.X, ALU.add)
                dve.wait_ge(mod_ready, 1)
                for kind, dst in ((0, "shift_a"), (3, "shift_b")):
                    dve.tensor_copy(keep[dst][:, :, :], pm[:, 2 * kind:2 * kind + 2, :])
                for kind, dst in ((1, "scale_a"), (4, "scale_b")):
                    dve.tensor_scalar(keep[dst][:, :, :], pm[:, 2 * kind:2 * kind + 2, :], 1.0, None, ALU.add)
                for b in range(B):
                    dve.wait_ge(gate_ready, b + 1)
                    dve.tensor_copy(raw[:, :, b, :], pg[b][:, :, :])
                    link(dve.tensor_scalar(sgn[:, :, b, :], pg[b][:, :, :], 0.0, 2.0, ALU.is_ge, ALU.mult))
                flat = lambda t: t[:, :, :, :].rearrange("p k b e -> p (k b e)")
                link(dve.scalar_tensor_tensor(out=flat(mag), in0=flat(raw), scalar=-1.0, in1=flat(raw),
                                              op0=ALU.mult, op1=ALU.max))
                link(dve.tensor_scalar(flat(raw), flat(mag), 0.25, None, ALU.max))
                link(dve.scalar_tensor_tensor(out=keep["gates"][:, :, :, :].rearrange("p k b e -> p (k b e)"),
                                              in0=sgn[:, :, :, :].rearrange("p k b e -> p (k b e)"), scalar=-1.0,
                                              in1=flat(raw),
                                              op0=ALU.add, op1=ALU.mult))

            @block.tensor
            def _(pe):
                pe.wait_ge(silu_ready, 1)
                pe.wait_ge(wloaded, 16)
                for n in range(12):
                    for eh in range(EH):
                        last = pe.matmul(pm[:, n, :], wmod[:, eh, n * P:(n + 1) * P], silu[:, eh, :],
                                         start=(eh == 0), stop=(eh == EH - 1))
                last.then_inc(mod_ready, 1)
                for b in range(B):
                    for k, kind in enumerate((2, 5)):
                        for eh in range(EH):
                            last = pe.matmul(pg[b][:, k, :], silu_b[:, eh, b, :],
                                             wmod[:, eh, kind * E:(kind + 1) * E],
                                             start=(eh == 0), stop=(eh == EH - 1))
                    last.then_inc(gate_ready, 1)


def inverse_root(dve, out, sd, ve, t1, t2, step, n):
    dve.reciprocal(t1, sd).then_inc(step, 1)
    dve.wait_ge(step, n + 1)
    dve.tensor_tensor(t2, t1, ve, ALU.mult).then_inc(step, 1)
    dve.wait_ge(step, n + 2)
    dve.scalar_tensor_tensor(out=t2, in0=t2, scalar=-0.5, in1=t1, op0=ALU.mult, op1=ALU.mult).then_inc(step, 1)
    dve.wait_ge(step, n + 3)
    dve.scalar_tensor_tensor(out=out, in0=t2, scalar=1.5, in1=t1, op0=ALU.add, op1=ALU.mult).then_inc(step, 1)
    dve.wait_ge(step, n + 4)


def phase_project(nc, io, keep):
    with PhaseMemory(nc, "prj") as a:
        JT = CH // P
        wq, wk, wv = (a.sb(n, [P, EH, E]) for n in ("wq", "wk", "wv"))
        bq, bk, r0, bkr = (a.sb(n, [P, EH]) for n in ("bq", "bk", "r0", "bkr"))
        bv = a.sb("bv", [P, E])
        x = a.sb("x", [P, 2, JT, E])
        stats = a.sb("stats", [P, 2, JT, 6])
        tick = a.sb("tick", [P, 1])
        mod_now = a.sb("mod_now", [P, 2, EH])
        mv = a.sb("mv", [P, 2, JT, 2])
        ve, sd, r1, r2, rstd = (a.sb(n, [P, 2, JT]) for n in ("ve", "sd", "r1", "r2", "rstd"))
        xn = a.sb("xn", [P, 2, JT, E])
        hT = a.sb("hT", [P, 2, EH, CH])
        qf = a.sb("qf", [P, 4, CH])
        hi = a.sb("hi", [P, 4, CH], F16)
        lo = a.sb("lo", [P, 4, CH], F16)
        vx = a.sb("vx", [P, JT, H, 2 * D])
        tp = [a.ps(f"tp{i}", [P, CH]) for i in range(EH)]
        qp = [a.ps(f"qp{i}", [P, CH]) for i in range(4)]
        vp = [a.ps(f"vp{i}", [P, 2, E]) for i in range(2)]
        weights, biases = a.sem("weights"), a.sem("biases")
        x_in = a.sems("x_in", 2)
        xn_done, tp_done, hT_done, proj_done = (a.sems(n, 2) for n in ("xn_done", "tp_done", "hT_done", "proj_done"))
        ln_step, once = a.sem("ln_step"), a.sem("once")
        mod_set = a.sem("mod_set")
        var_done, sd_done = a.sems("var_done", 2), a.sems("sd_done", 2)
        LN = 6
        qp_done, qf_done, hi_done, lo_done, hi_out, lo_out = (
            a.sems(n, 4) for n in ("qp_done", "qf_done", "hi_done", "lo_done", "hi_out", "lo_out"))
        vp_done, vx_done, vx_out = (a.sems(n, 2) for n in ("vp_done", "vx_done", "vx_out"))
        xv = io["x"].rearrange("b (c j p) e -> (b c) p j e", j=JT, p=P)
        NI = B * CPB // 2

        with nc.Block() as block:

            def low(dve, it, n):
                dve.wait_ge(hi_done[n], it + 1)
                dve.wait_ge(lo_out[n], it * 16)
                dve.tensor_tensor(lo[:, n, :], qf[:, n, :], hi[:, n, :], ALU.subtract).then_inc(lo_done[n], 1)

            @block.gpsimd
            def _(pool):
                for w, name in ((wq, "wq"), (wk, "wk"), (wv, "wv")):
                    pool.dma_start(w[:, :, :], io[name].rearrange("(e p) n -> p e n", p=P)).then_inc(weights, 16)
                for w, name in ((bq, "bq"), (bk, "bk"), (r0, "r0")):
                    pool.dma_start(w[:, :], io[name]).then_inc(biases, 16)
                pool.dma_start(bv[:, :], io["bv"].partition_broadcast(P)).then_inc(biases, 16)
                with pool.Fori(0, NI) as t:
                    for s in range(2):
                        pool.wait_ge(xn_done[s], t)
                        pool.dma_start(x[:, s], xv[bass.ds(t * 2 + s, 1)].rearrange("o p j e -> p (o j) e")).then_inc(x_in[s], 16)

            @block.vector
            def _(dve):
                dve.memset(vx[:, :, :, D:], 1.0)
                dve.wait_ge(biases, 64)
                dve.tensor_tensor(bkr[:, :], bk[:, :], r0[:, :], ALU.add).then_inc(once, 1)
                dve.wait_ge(once, 1)
                with dve.Fori(0, NI) as t:
                    for s in range(2):
                        it = t * 2 + s
                        dve.wait_ge(x_in[s], t * 16 + 16)
                        for j in range(JT):
                            last = dve.bn_stats(stats[:, s, j, :], x[:, s, j, :])
                        last.then_inc(ln_step, 1)
                        dve.wait_ge(ln_step, it * LN + 1)
                        dve.memset(tick[:, :], 0.0)
                        for j in range(JT):
                            last = dve.bn_aggr(mv[:, s, j, :], stats[:, s, j, :])
                        last.then_inc(ln_step, 1)
                        dve.wait_ge(ln_step, it * LN + 2)
                        dve.tensor_scalar(ve[:, s, :], mv[:, s, :, 1], EPS, None, ALU.add).then_inc(var_done[s], 1)
                        dve.wait_ge(sd_done[s], t + 1)
                        inverse_root(dve, rstd[:, s, :], sd[:, s, :], ve[:, s, :], r1[:, s, :], r2[:, s, :], ln_step, it * LN + 2)
                        dve.wait_ge(tp_done[s], t)
                        for j in range(JT):
                            last = dve.tensor_scalar(xn[:, s, j, :], x[:, s, j, :], mv[:, s, j, 0:1], rstd[:, s, j:j + 1],
                                                     ALU.subtract, ALU.mult)
                        last.then_inc(xn_done[s], 1)
                        for n in range(4):
                            dve.wait_ge(qp_done[n], it + 1)
                            dve.wait_ge(lo_done[n], it)
                            bias = bq[:, n:n + 1] if n < 2 else bkr[:, n - 2:n - 1]
                            dve.tensor_scalar(qf[:, n, :], qp[n][:, :], bias, None, ALU.add).then_inc(qf_done[n], 1)
                            if n:
                                low(dve, it, n - 1)
                        low(dve, it, 3)
                        for n in range(2):
                            dve.wait_ge(vp_done[n], it + 1)
                            dve.wait_ge(vx_out[n], it * 16)
                            for j in range(2):
                                last = dve.tensor_tensor(vx[:, 2 * n + j, :, 0:D],
                                                         vp[n][:, j, :].rearrange("p (h d) -> p h d", d=D),
                                                         bv[:, :].rearrange("p (h d) -> p h d", d=D), ALU.add)
                            last.then_inc(vx_done[n], 1)

            @block.scalar
            def _(act):
                with act.Fori(0, B) as b:
                    for k, name in enumerate(("shift_a", "scale_a")):
                        act.activation(mod_now[:, k, :].unsqueeze(2), keep[name][:, :, bass.ds(b, 1)], ACT.Copy).then_inc(mod_set, 1)
                    act.wait_ge(mod_set, b * 2 + 2)
                    with act.Fori(0, CPB // 2) as u:
                        t = b * (CPB // 2) + u
                        for s in range(2):
                            it = t * 2 + s
                            act.wait_ge(var_done[s], t + 1)
                            act.activation(sd[:, s, :], ve[:, s, :], ACT.Sqrt).then_inc(sd_done[s], 1)
                            act.wait_ge(tp_done[s], t + 1)
                            act.wait_ge(proj_done[s], t)
                            for eh in range(EH):
                                last = act.activation(hT[:, s, eh, :], tp[eh][:, :], ACT.Identity,
                                                      bias=mod_now[:, 0, eh:eh + 1],
                                                      scale=mod_now[:, 1, eh:eh + 1])
                            last.then_inc(hT_done[s], 1)
                            for n in range(4):
                                act.wait_ge(qf_done[n], it + 1)
                                act.wait_ge(hi_out[n], it * 16)
                                act.wait_ge(lo_done[n], it)
                                act.activation(hi[:, n, :], qf[:, n, :], ACT.Copy).then_inc(hi_done[n], 1)

            @block.tensor
            def _(pe):
                pe.wait_ge(weights, 48)
                with pe.Fori(0, NI) as t:
                    for s in range(2):
                        it = t * 2 + s
                        pe.wait_ge(xn_done[s], t + 1)
                        pe.wait_ge(hT_done[1 - s], t + s)
                        for eh in range(EH):
                            for j in range(JT):
                                last = pe.transpose(tp[eh][:, j * P:(j + 1) * P], xn[:, s, j, eh * P:(eh + 1) * P],
                                                    keep["ident"][:, :])
                        last.then_inc(tp_done[s], 1)
                        pe.wait_ge(hT_done[s], t + 1)
                        for n in range(4):
                            w = wq if n < 2 else wk
                            pe.wait_ge(qf_done[n], it)
                            for eh in range(EH):
                                last = pe.matmul(qp[n][:, :], w[:, eh, (n % 2) * P:(n % 2 + 1) * P], hT[:, s, eh, :],
                                                 start=(eh == 0), stop=(eh == EH - 1))
                            last.then_inc(qp_done[n], 1)
                        for n in range(2):
                            pe.wait_ge(vx_done[n], it)
                            for j in range(2):
                                for eh in range(EH):
                                    last = pe.matmul(vp[n][:, j, :], hT[:, s, eh, (2 * n + j) * P:(2 * n + j + 1) * P],
                                                     wv[:, eh, :], start=(eh == 0), stop=(eh == EH - 1))
                            last.then_inc(vp_done[n], 1)
                            if n == 1:
                                pe.wait_ge(vp_done[1], it + 1)
                                pe.sem_inc(proj_done[s], 1)

            @block.sync
            def _(sp):
                with sp.Fori(0, NI * 2) as it:
                    for n in range(4):
                        dst = io["s_q"] if n < 2 else io["s_k"]
                        for part, (buf, done, out) in enumerate(((hi, hi_done, hi_out), (lo, lo_done, lo_out))):
                            sp.wait_ge(done[n], it + 1)
                            sp.dma_start(dst[part, bass.ds(it * JT, JT), (n % 2) * P:(n % 2 + 1) * P, :].rearrange("i r t -> r i t"),
                                         buf[:, n, :].rearrange("p (i t) -> p i t", t=P)).then_inc(out[n], 16)
                    for n in range(2):
                        sp.wait_ge(vx_done[n], it + 1)
                        sp.dma_start(io["s_v"][bass.ds(it * JT + 2 * n, 2)].rearrange("i p h d -> p i (h d)"),
                                     vx[:, 2 * n:2 * n + 2, :, :].rearrange("p i h d -> p i (h d)")).then_inc(vx_out[n], 16)
                for n in range(4):
                    sp.wait_ge(hi_out[n], NI * 32)
                    sp.wait_ge(lo_out[n], NI * 32)
                for n in range(2):
                    sp.wait_ge(vx_out[n], NI * 32)


def phase_row_max(nc, io, keep):
    NG = P // G
    with PhaseMemory(nc, "max") as a:
        kA = a.sb("kA", [P, 2, EH, S], F16)
        qn = a.sb("qn", [P, 2, EH, P], F16)
        qe = a.sb("qe", [P, 2, EH, HH * P], F16)
        qbd = a.sb("qbd", [P, 2, EH, NG, HH, G], F16)
        qex = a.sb("qex", [P, 2, NG, H, G], F16)
        mx = a.sb("mx", [P, 2, NG])
        mrow = a.sb("mrow", [NG, 2, P], F16)
        pa = [a.ps(f"pa{i}", [P, S]) for i in range(2)]
        k_in, q_in, qx_done, tiles_done, mx_done, mrow_done, m_out = (
            a.sems(n, 2) for n in ("k_in", "q_in", "qx_done", "tiles_done", "mx_done", "mrow_done", "m_out"))
        pa_full, pa_free = a.sems("pa_full", 2), a.sems("pa_free", 2)
        NT = NG + 1

        with nc.Block() as block:

            @block.sync
            def _(sp):
                for i in range(NB):
                    with sp.Fori(0, B // 2) as t:
                        for s in range(2):
                            u = t + i * (B // 2)
                            sp.wait_ge(tiles_done[s], u)
                            for e in range(EH):
                                sp.dma_start(kA[:, s, e, 0:(i + 1) * P].rearrange("p (j t) -> p j t", t=P),
                                             io["s_k"][0, bass.ds(t * (2 * NB) + s * NB, i + 1), e * P:(e + 1) * P, :]
                                             .rearrange("j r t -> r j t")).then_inc(k_in[s], 16)
                            sp.wait_ge(qx_done[s], u)
                            blk = t * (2 * NB) + (s * NB + i)
                            sp.dma_start(qn[:, s], io["s_q"][0, bass.ds(blk, 1)].rearrange("o (e r) t -> r (o e) t", e=EH)).then_inc(q_in[s], 16)
                            for e in range(EH):
                                sp.dma_start(qe[:, s, e, :], io["s_q"][0, bass.ds(blk, 1), e * P:(e + 1) * P, :]
                                             .rearrange("o (d h) t -> (o d) (h t)", d=D).partition_broadcast(G)).then_inc(q_in[s], 16)

            @block.gpsimd
            def _(pool):
                for i in range(NB):
                    with pool.Fori(0, B // 2) as t:
                        for s in range(2):
                            u = t + i * (B // 2)
                            pool.wait_ge(q_in[s], u * 48 + 48)
                            pool.wait_ge(tiles_done[s], u)
                            for e in range(EH):
                                pool.tensor_tensor(qbd[:, s, e],
                                                   qn[:, s, e, :].rearrange("p (g i) -> p g i", i=G).unsqueeze(2).broadcast_to([P, NG, HH, G]),
                                                   keep["mask_h"][:, :].unsqueeze(1).unsqueeze(3).broadcast_to([P, NG, HH, G]), ALU.mult)
                                last = pool.tensor_tensor(qex[:, s, :, e * HH:(e + 1) * HH, :],
                                                          qe[:, s, e, :].rearrange("p (h g i) -> p g h i", h=HH, i=G),
                                                          keep["mask_i"][:, :].unsqueeze(1).unsqueeze(1).broadcast_to([P, NG, HH, G]), ALU.mult)
                            last.then_inc(qx_done[s], 1)

            @block.tensor
            def _(pe):
                for i in range(NB):
                    with pe.Fori(0, B // 2) as t:
                        for s in range(2):
                            u = t + i * (B // 2)
                            pe.wait_ge(k_in[s], u * 32 + 32)
                            pe.wait_ge(qx_done[s], u + 1)
                            for g in range(NG):
                                n = NT * s + g
                                buf = pa[n % 2]
                                first = i * P + g * G
                                end = first + G
                                pe.wait_ge(pa_free[n % 2], u * NT + n // 2)
                                for c in range(0, end, CH):
                                    for e in range(EH):
                                        pe.matmul(buf[64 * e:64 * e + 64, c:min(c + CH, end)], qbd[:, s, e, g], kA[:, s, e, c:min(c + CH, end)],
                                                  start=True, stop=False, skip_group_check=True)
                                lo = max(0, first - W)
                                while lo < end:
                                    hi = min(end, lo // CH * CH + CH)
                                    pe.matmul(buf[:, lo:hi], qex[:, s, g], keep["table"][:, 0, lo - first + TAB0:hi - first + TAB0],
                                              start=False, stop=False, skip_group_check=True)
                                    lo = hi
                                last = pe.matmul(buf[:, first:end], keep["ident_s"][:, :, :], keep["mask_f"][:, :],
                                                 start=False, stop=True, skip_group_check=True)
                                last.then_inc(pa_full[n % 2], 1)
                                if g == NG - 1:
                                    pe.wait_ge(pa_full[n % 2], u * NT + n // 2 + 1)
                                    pe.sem_inc(tiles_done[s], 1)
                            n = NT * s + NG
                            pe.wait_ge(mx_done[s], u + 1)
                            pe.wait_ge(pa_free[n % 2], u * NT + n // 2)
                            pe.transpose(pa[n % 2][0:NG, 0:P], mx[:, s, :], keep["ident"][:, :]).then_inc(pa_full[n % 2], 1)

            @block.vector
            def _(dve):
                for i in range(NB):
                    with dve.Fori(0, B // 2) as t:
                        for s in range(2):
                            u = t + i * (B // 2)
                            for g in range(NG):
                                n = NT * s + g
                                dve.wait_ge(pa_full[n % 2], u * NT + n // 2 + 1)
                                last = dve.reduce_max(mx[:, s, g:g + 1], pa[n % 2][:, 0:i * P + g * G + G], AX.X)
                                last.then_inc(pa_free[n % 2], 1)
                            dve.wait_ge(pa_free[(NT * s + NG - 1) % 2], u * NT + (NT * s + NG - 1) // 2 + 1)
                            dve.sem_inc(mx_done[s], 1)
                            n = NT * s + NG
                            dve.wait_ge(pa_full[n % 2], u * NT + n // 2 + 1)
                            dve.wait_ge(m_out[s], u * 16)
                            dve.tensor_copy(mrow[:, s, :], pa[n % 2][0:NG, 0:P]).then_inc(pa_free[n % 2], 1)
                            dve.wait_ge(pa_free[n % 2], u * NT + n // 2 + 1)
                            dve.sem_inc(mrow_done[s], 1)

            @block.scalar
            def _(act):
                for i in range(NB):
                    with act.Fori(0, B // 2) as t:
                        for s in range(2):
                            u = t + i * (B // 2)
                            blk = t * (2 * NB) + (s * NB + i)
                            act.wait_ge(mrow_done[s], u + 1)
                            act.dma_start(io["s_m"][bass.ds(blk, 1)].rearrange("o h (g i) -> g (o h) i", i=G),
                                          mrow[:, s, :].rearrange("g (h i) -> g h i", i=G)).then_inc(m_out[s], 16)
                for s in range(2):
                    act.wait_ge(m_out[s], NB * B // 2 * 16)

def phase_far(nc, io, keep):
    NF = NB - FARI
    chunks = ((FARI, 8), (8, 12), (12, 16))
    steps = [(c, j, max(lo, j + NJ), hi) for c, (lo, hi) in enumerate(chunks) for j in range(hi - NJ)]
    NS = len(steps)
    with PhaseMemory(nc, "far") as a:
        kf = a.sb("kf", [KR, 2, NF, 4 * P], F16)
        qf = a.sb("qf", [KR, 2, NF, 4, P], F16)
        vf = a.sb("vf", [P, 2, NF, 4, 2 * D])
        pt = a.sb("pt", [P, 3, 4, CH])
        of = a.sb("of", [P, 2, 4, P])
        ps = [a.ps(f"ps{i}", [P, 2, CH]) for i in range(3)]
        po = [a.ps(f"po{i}", [P, 4, P]) for i in range(2)]
        ones = a.sem("ones")
        in_, unit_done = a.sems("in", 2), a.sems("unit_done", 2)
        s_full, s_free, p_full, p_free = (a.sems(n, 3) for n in ("s_full", "s_free", "p_full", "p_free"))
        po_full, po_free, of_out = (a.sems(n, 2) for n in ("po_full", "po_free", "of_out"))
        NIN = 10 * 16

        with nc.Block() as block:

            @block.sync
            def _(sp):
                with sp.Fori(0, B) as b:
                    with sp.Fori(0, 2) as w:
                        t = b * 2 + w
                        for s in range(2):
                            sp.wait_ge(unit_done[s], t)
                            rows = lambda buf, part, j0: (buf[part, bass.ds(b * NB + j0, NF), bass.ds(w * P, P), :]
                                                          .rearrange("j (d h) t -> d j h t", h=HH)[:, :, 4 * s:4 * s + 4, :]
                                                          .rearrange("d j h t -> d j (h t)"))
                            for r, part in enumerate((0, 1, 0, 1)):
                                sp.dma_start(kf[r * D:(r + 1) * D, s], rows(io["s_k"], part, 0)).then_inc(in_[s], 16)
                            for r, part in enumerate((0, 0, 1, 1)):
                                sp.dma_start(qf[r * D:(r + 1) * D, s].rearrange("d i h t -> d i (h t)"),
                                             rows(io["s_q"], part, FARI)).then_inc(in_[s], 16)
                            sp.dma_start(qf[4 * D:KR, s].rearrange("d i h t -> d i (h t)"),
                                         io["s_m"][bass.ds(b * NB + FARI, NF), bass.ds(w * HH + 4 * s, 4), :]
                                         .rearrange("i h t -> i (h t)").unsqueeze(0)).then_inc(in_[s], 16)
                            sp.dma_start(vf[:, s].rearrange("p j h d -> p j (h d)"),
                                         io["s_v"][bass.ds(b * NB, NF), :, bass.ds(w * HH + 4 * s, 4), :]
                                         .rearrange("j p h d -> p j (h d)")).then_inc(in_[s], 16)

            @block.tensor
            def _(pe):
                pe.wait_ge(ones, 1)
                with pe.Fori(0, B * 2) as t:
                    for s in range(2):
                        v = t * 2 + s
                        pe.wait_ge(in_[s], t * NIN + NIN)

                        def pv(k):
                            c, j, lo, hi = steps[k]
                            c0, chi = chunks[c]
                            buf, uses = (3 * s + c) % 2, t * 3 + (3 * s + c) // 2
                            if j == 0:
                                pe.wait_ge(po_free[buf], uses)
                            pe.wait_ge(p_full[k % 3], (v * (NS // 3) + k // 3) * 2 + 2)
                            for h in range(4):
                                last = pe.matmul(po[buf][32 * h:32 * h + 32, lo - c0:hi - c0, :], vf[:, s, j, h, :],
                                                 pt[:, k % 3, h, 0:(hi - lo) * P],
                                                 start=(j == 0), stop=(j == chi - NJ - 1), skip_group_check=True)
                            last.then_inc(p_free[k % 3], 1)
                            if j == chi - NJ - 1:
                                pe.wait_ge(p_free[k % 3], v * (NS // 3) + k // 3 + 1)
                                pe.sem_inc(po_full[buf], 1)

                        for k, (c, j, lo, hi) in enumerate(steps):
                            for r in range(2):
                                n = 2 * k + r
                                pe.wait_ge(s_free[n % 3], v * (2 * NS // 3) + n // 3)
                                for h in range(2):
                                    last = pe.matmul(ps[n % 3][:, h, 0:(hi - lo) * P], kf[:, s, j, (2 * r + h) * P:(2 * r + h + 1) * P],
                                                     qf[:, s, lo - FARI:hi - FARI, 2 * r + h, :], start=True, stop=True)
                                last.then_inc(s_full[n % 3], 1)
                            if k:
                                pv(k - 1)
                        pv(NS - 1)
                        pe.wait_ge(p_free[(NS - 1) % 3], v * (NS // 3) + (NS - 1) // 3 + 1)
                        pe.sem_inc(unit_done[s], 1)

            @block.scalar
            def _(act):
                with act.Fori(0, B * 2) as t:
                    for s in range(2):
                        v = t * 2 + s
                        for k, (c, j, lo, hi) in enumerate(steps):
                            act.wait_ge(p_free[k % 3], v * (NS // 3) + k // 3)
                            for r in range(2):
                                n = 2 * k + r
                                act.wait_ge(s_full[n % 3], v * (2 * NS // 3) + n // 3 + 1)
                                act.activation(pt[:, k % 3, 2 * r:2 * r + 2, 0:(hi - lo) * P], ps[n % 3][:, :, 0:(hi - lo) * P],
                                               ACT.Exp, scale=SCALE).then_inc(p_full[k % 3], 1)
                                act.wait_ge(p_full[k % 3], (v * (NS // 3) + k // 3) * 2 + r + 1)
                                act.sem_inc(s_free[n % 3], 1)

            @block.vector
            def _(dve):
                dve.memset(kf[4 * D:KR, :, :, :], -1.0).then_inc(ones, 1)
                with dve.Fori(0, B * 2) as t:
                    for s in range(2):
                        for c, (lo, hi) in enumerate(chunks):
                            buf, uses = (3 * s + c) % 2, t * 3 + (3 * s + c) // 2
                            dve.wait_ge(po_full[buf], uses + 1)
                            dve.wait_ge(of_out[buf], uses * 16)
                            dve.tensor_copy(of[:, buf, 0:hi - lo, :], po[buf][:, 0:hi - lo, :]).then_inc(po_free[buf], 1)

            @block.gpsimd
            def _(pool):
                with pool.Fori(0, B) as b:
                    with pool.Fori(0, 2) as w:
                        t = b * 2 + w
                        for s in range(2):
                            for c, (lo, hi) in enumerate(chunks):
                                buf, uses = (3 * s + c) % 2, t * 3 + (3 * s + c) // 2
                                pool.wait_ge(po_free[buf], uses + 1)
                                pool.dma_start(io["s_of"][bass.ds(b * NB + lo, hi - lo), bass.ds(w * 2 + s, 1), :, :]
                                               .rearrange("i o r t -> r (i o) t"),
                                               of[:, buf, 0:hi - lo, :]).then_inc(of_out[buf], 16)
                for buf in range(2):
                    pool.wait_ge(of_out[buf], B * 2 * 3 * 16)


def phase_near(nc, io, keep):
    NG = P // G
    with PhaseMemory(nc, "near") as a:
        kn = a.sb("kn", [KR, 2, NJ, HH * P], F16)
        vn = a.sb("vn", [P, 2, NJ, HH, 2 * D])
        qs = a.sb("qs", [KR, 2, HH, P], F16)
        qe = a.sb("qe", [P, 2, 2, HH, P], F16)
        qx = a.sb("qx", [P, 2, 2, NG, HH, G], F16)
        pt = a.sb("pt", [P, 2, HH, P])
        tick = a.sb("tick", [P, 1])
        fo = a.sb("fo", [P, 2, 2, P])
        on = a.sb("on", [P, 2, 2, P])
        ps = [a.ps(f"ps{i}", [P, 2, HH, P // 2]) for i in range(2)]
        po = [a.ps(f"po{i}", [P, 2, P]) for i in range(2)]
        ones = a.sem("ones")
        k_in, q_in, f_in, qx_done, unit_done, unit_full, on_done, on_out = (
            a.sems(n, 2) for n in ("k_in", "q_in", "f_in", "qx_done", "unit_done", "unit_full", "on_done", "on_out"))
        s_full, s_free, p_full, p_free, diag = (a.sems(n, 2) for n in ("s_full", "s_free", "p_full", "p_free", "diag"))
        NIN = 8 * 16

        def levels(eng, body):
            for i in range(FARI):
                with eng.Fori(0, B) as b:
                    nj = i + 1
                    body(b, i, nj, False, b + i * B, b * nj + B * i * (i + 1) // 2)
            with eng.Fori(0, B) as b:
                with eng.Fori(0, NB - FARI) as r:
                    u = b * (NB - FARI) + r
                    body(b, r + FARI, NJ, True, u + FARI * B, u * NJ + B * FARI * (FARI + 1) // 2)

        with nc.Block() as block:

            @block.sync
            def _(sp):
                def body(b, i, nj, far, u, k):
                    for s in range(2):
                        blk = b * NB + i
                        sp.wait_ge(unit_done[s], u)
                        for r, part in enumerate((0, 1, 0, 1)):
                            sp.dma_start(kn[r * D:(r + 1) * D, s, 0:nj, :],
                                         io["s_k"][part, bass.ds(blk - (nj - 1), nj), s * P:(s + 1) * P, :]
                                         .rearrange("j (d h) t -> d j (h t)", h=HH)).then_inc(k_in[s], 16)
                        for r, part in enumerate((0, 1)):
                            sp.dma_start(qs[r * 2 * D:(r + 1) * 2 * D, s].rearrange("r h t -> r (h t)"),
                                         io["s_q"][part, bass.ds(blk, 1), s * P:(s + 1) * P, :]
                                         .rearrange("o (d h) t -> (o d) (h t)", h=HH).partition_broadcast(2)).then_inc(k_in[s], 16)
                        sp.dma_start(qs[4 * D:KR, s].rearrange("r h t -> r (h t)"),
                                     io["s_m"][bass.ds(blk, 1), s * HH:(s + 1) * HH, :].rearrange("o h t -> o (h t)")).then_inc(k_in[s], 16)
                        sp.dma_start(vn[:, s, 0:nj].rearrange("p j h d -> p j (h d)"),
                                     io["s_v"][bass.ds(blk - (nj - 1), nj), :, s * HH:(s + 1) * HH, :]
                                     .rearrange("j p h d -> p j (h d)")).then_inc(k_in[s], 16)
                        sp.wait_ge(qx_done[s], u)
                        for part in range(2):
                            sp.dma_start(qe[:, s, part].rearrange("r h t -> r (h t)"),
                                           io["s_q"][part, bass.ds(blk, 1), s * P:(s + 1) * P, :]
                                           .rearrange("o (d h) t -> (o d) (h t)", h=HH).partition_broadcast(G)).then_inc(q_in[s], 16)
                        if far:
                            sp.wait_ge(on_done[s], u)
                            sp.dma_start(fo[:, s], io["s_of"][bass.ds(blk, 1), 2 * s:2 * s + 2, :, :]
                                         .rearrange("o c r t -> r (o c) t")).then_inc(f_in[s], 16)
                levels(sp, body)

            @block.gpsimd
            def _(pool):
                def body(b, i, nj, far, u, k):
                    for s in range(2):
                        pool.wait_ge(q_in[s], u * 32 + 32)
                        pool.wait_ge(unit_done[s], u)
                        for part in range(2):
                            last = pool.tensor_tensor(qx[:, s, part], qe[:, s, part].rearrange("p h (g i) -> p g h i", i=G),
                                                      keep["mask_i"][:, :].unsqueeze(1).unsqueeze(1).broadcast_to([P, NG, HH, G]), ALU.mult)
                        last.then_inc(qx_done[s], 1)
                        n = nj * s
                        pool.wait_ge(p_full[n % 2], k + n // 2 + 1)
                        pool.tensor_tensor(tick[:, :], keep["mask_i"][:, 0:1], keep["mask_i"][:, 0:1], ALU.mult)
                        pool.affine_select(out=pt[:, n % 2], in_=pt[:, n % 2], compare_op=ALU.is_ge, fill=0.0, base=0,
                                           pattern=[[0, HH], [1, P]], channel_multiplier=-1).then_inc(diag[s], 1)
                levels(pool, body)

            @block.vector
            def _(dve):
                dve.memset(kn[4 * D:KR, :, :, :], -1.0).then_inc(ones, 1)

                def body(b, i, nj, far, u, k):
                    for s in range(2):
                        dve.wait_ge(unit_full[s], u + 1)
                        dve.wait_ge(on_out[s], u * 16)
                        if far:
                            dve.wait_ge(f_in[s], (u - FARI * B) * 16 + 16)
                            dve.tensor_tensor(on[:, s], po[s][:, :, :], fo[:, s], ALU.add).then_inc(on_done[s], 1)
                        else:
                            dve.tensor_copy(on[:, s], po[s][:, :, :]).then_inc(on_done[s], 1)
                levels(dve, body)

            @block.scalar
            def _(act):
                def body(b, i, nj, far, u, k):
                    for s in range(2):
                        for j in range(nj):
                            n = nj * s + j
                            act.wait_ge(p_free[n % 2], k + n // 2)
                            act.wait_ge(s_full[n % 2], k + n // 2 + 1)
                            act.activation(pt[:, n % 2].rearrange("p h (x t) -> p x h t", x=2), ps[n % 2][:, :, :, :],
                                           ACT.Exp, scale=SCALE).then_inc(p_full[n % 2], 1)
                    for s in range(2):
                        act.wait_ge(on_done[s], u + 1)
                        act.dma_start(io["s_o"][bass.ds(b * NB + i, 1), 2 * s:2 * s + 2, :, :]
                                      .rearrange("o c r t -> r (o c) t"), on[:, s]).then_inc(on_out[s], 16)
                levels(act, body)
                for s in range(2):
                    act.wait_ge(on_out[s], NB * B * 16)

            @block.tensor
            def _(pe):
                pe.wait_ge(ones, 1)

                def body(b, i, nj, far, u, k):
                    steps = [(s, j) for s in range(2) for j in range(nj)]

                    def pv(n):
                        s, j = steps[n]
                        if j == 0:
                            pe.wait_ge(on_done[s], u)
                            pe.wait_ge(diag[s], u + 1)
                        pe.wait_ge(p_full[n % 2], k + n // 2 + 1)
                        for h in range(HH):
                            last = pe.matmul(po[s][32 * (h % 4):32 * (h % 4) + 32, h // 4, :], vn[:, s, nj - 1 - j, h, :],
                                             pt[:, n % 2, h, :], start=(j == 0 and h < 4), stop=(j == nj - 1 and h >= 4),
                                             skip_group_check=True)
                        last.then_inc(p_free[n % 2], 1)
                        if j == nj - 1:
                            pe.wait_ge(p_free[n % 2], k + n // 2 + 1)
                            pe.sem_inc(unit_full[s], 1)
                            pe.sem_inc(unit_done[s], 1)

                    for n, (s, j) in enumerate(steps):
                        if j == 0:
                            pe.wait_ge(k_in[s], u * NIN + NIN)
                            pe.wait_ge(qx_done[s], u + 1)
                        pe.wait_ge(p_full[n % 2], k + n // 2)
                        for x in range(2):
                            bank = ps[n % 2][:, x]
                            for h in range(HH):
                                pe.matmul(bank[:, h, :], kn[:, s, nj - 1 - j, h * P:(h + 1) * P], qs[:, s, h, x * 64:x * 64 + 64],
                                          start=(h == 0), stop=False, skip_group_check=True)
                            for g in range(NG // 2):
                                y = TAB0 - j * P - (x * 64 + g * G)
                                out = bank[:, :, g * G:g * G + G]
                                for part, qpart in ((0, 0), (0, 1), (1, 0)):
                                    last = pe.matmul(out, keep["table"][:, part, y:y + P], qx[:, s, qpart, x * (NG // 2) + g],
                                                     start=False, stop=(g == NG // 2 - 1 and part == 1), skip_group_check=True)
                        last.then_inc(s_full[n % 2], 1)
                        if n:
                            pv(n - 1)
                    pv(len(steps) - 1)
                levels(pe, body)


def phase_output(nc, io, keep):
    JT = CH // P
    NK = B * CPB
    with PhaseMemory(nc, "out") as a:
        wo = a.sb("wo", [P, 4, E])
        gw = a.sb("gw", [P, EH, NX])
        gbias = a.sb("gbias", [P, NX])
        b3 = a.sb("b3", [NX, E])
        bo = a.sb("bo", [P, E])
        gbo = a.sb("gbo", [P, B, E])
        gbo_now = a.sb("gbo_now", [P, 1, E])
        x = a.sb("x", [P, 2, JT, E])
        heads = a.sb("heads", [P, 2, JT * 4, P])
        rec = a.sb("rec", [P, 2, 4, P])
        nrm = a.sb("nrm", [P, 2, 4, P])
        att = a.sb("att", [P, 2, 2, E])
        x1 = a.sb("x1", [P, 2, JT, E])
        stats = a.sb("stats", [P, JT, 6])
        tick = a.sb("tick", [P, 1])
        mod_now = a.sb("mod_now", [P, 2, EH])
        mv = a.sb("mv", [P, JT, 2])
        ve, sd, r1, r2, rstd = (a.sb(n, [P, JT]) for n in ("ve", "sd", "r1", "r2", "rstd"))
        xn = a.sb("xn", [P, JT, E])
        hT = a.sb("hT", [P, 2, EH, CH])
        lg, sh, ex, pr, o1, o2, w1, w2 = (a.sb(n, [P, JT, NX]) for n in ("lg", "sh", "ex", "pr", "o1", "o2", "w1", "w2"))
        cw = a.sb("cw", [P, JT, NX])
        top, topf = a.sb("top", [P, JT, 8]), a.sb("topf", [P, JT, 8])
        topi = a.sb("topi", [P, JT, 8], U32)
        mxs, sums, rsum = (a.sb(n, [P, JT]) for n in ("mxs", "sums", "rsum"))
        cwT = a.sb("cwT", [NX, CH])
        wb = a.sb("wb", [P, 2, 2, E])
        base = a.sb("base", [P, 2, 2, E])
        dp = [a.ps(f"dp{i}", [P, 4, P]) for i in range(2)]
        ap = [a.ps(f"ap{i}", [P, 2, E]) for i in range(2)]
        tp = [a.ps(f"tp{i}", [P, CH]) for i in range(2)]
        lp = a.ps("lp", [P, JT, NX])
        cp = a.ps("cp", [P, CH])
        zeroed, weights, once, gbo_set = (a.sem(n) for n in ("zeroed", "weights", "once", "gbo_set"))
        x_in, heads_in, xb_done, x1_done, hT_out = (a.sems(n, 2) for n in ("x_in", "heads_in", "xb_done", "x1_done", "hT_out"))
        den_full, rec_done, nrm_done, wo_done, att_done = (
            a.sems(n, 2) for n in ("den_full", "rec_done", "nrm_done", "wo_done", "att_done"))
        ln_step, var_done, sd_done, xn_done, tp_done, hT_done, mod_set = (
            a.sem(n) for n in ("ln_step", "var_done", "sd_done", "xn_done", "tp_done", "hT_done", "mod_set"))
        lg_full, route_step, sh_done, ex_done, cw_done, cp_full, cwT_done = (
            a.sem(n) for n in ("lg_full", "route_step", "sh_done", "ex_done", "cw_done", "cp_full", "cwT_done"))
        bp_full, wb_done, base_done, base_out = (a.sems(n, 2) for n in ("bp_full", "wb_done", "base_done", "base_out"))
        NW = 9 * 16
        LN, RS = 6, 11
        chunk_of = lambda b, c: b * CPB + c
        slot_use = lambda b, c: b * (CPB // 2) + c // 2

        def order(eng, attend, norm, route, start=None):
            with eng.Fori(0, B) as b:
                if start:
                    start(b)
                for c in range(CPB + 1):
                    if c:
                        norm(b, c - 1, chunk_of(b, c - 1), slot_use(b, c - 1), (c - 1) % 2)
                    if c < CPB:
                        attend(b, c, chunk_of(b, c), slot_use(b, c), c % 2)
                    if c:
                        route(b, c - 1, chunk_of(b, c - 1), slot_use(b, c - 1), (c - 1) % 2)

        nothing = lambda *args: None
        with nc.Block() as block:

            @block.sync
            def _(sp):
                sp.wait_ge(zeroed, 1)
                for q in range(4):
                    sp.dma_start(wo[32 * q:32 * q + D, :, :], io["wo"].rearrange("(g q d) n -> q d g n", q=4, d=D)[q]).then_inc(weights, 16)
                sp.dma_start(bo[:, :], io["bo"].partition_broadcast(P)).then_inc(weights, 16)
                sp.dma_start(gbias[:, :], io["gate_b"].partition_broadcast(P)).then_inc(weights, 16)
                sp.dma_start(b3[:, :], io["b3"]).then_inc(weights, 16)
                for eh in range(EH):
                    sp.dma_start(gw[:, eh, :], io["gwT"][eh * P:(eh + 1) * P, :]).then_inc(weights, 16)

                def attend(b, c, it, u, s):
                    sp.wait_ge(x1_done[s], u)
                    sp.dma_start(x[:, s], io["x"][bass.ds(b, 1), c * CH:(c + 1) * CH, :]
                                 .rearrange("o (j p) e -> p (o j) e", p=P)).then_inc(x_in[s], 16)
                    for j in range(JT):
                        sp.dma_start(heads[:, s, 4 * j:4 * j + 4], io["s_o"][bass.ds(it * JT + j, 1)].rearrange("i o r t -> r (i o) t")).then_inc(heads_in[s], 16)
                order(sp, attend, nothing, nothing)

            @block.gpsimd
            def _(pool):
                pool.memset(wo[:, :, :], 0.0).then_inc(zeroed, 1)
                pool.wait_ge(once, 1)

                def start(b):
                    pool.tensor_copy(gbo_now[:, :, :], gbo[:, bass.ds(b, 1), :]).then_inc(gbo_set, 1)
                    pool.wait_ge(gbo_set, b + 1)

                def attend(b, c, it, u, s):
                    pool.wait_ge(x_in[s], u * 16 + 16)
                    pool.tensor_tensor(x[:, s], x[:, s], gbo_now[:, :, :].broadcast_to([P, JT, E]), ALU.add).then_inc(xb_done[s], 1)

                def route(b, c, it, u, s):
                    for m in range(2):
                        pool.wait_ge(wb_done[m], it + 1)
                        pool.wait_ge(base_out[m], it * 16)
                        pool.tensor_tensor(base[:, m], wb[:, m], x1[:, s, 2 * m:2 * m + 2, :], ALU.add).then_inc(base_done[m], 1)
                    for m in range(2):
                        pool.wait_ge(base_done[m], it + 1)
                        pool.dma_start(io["s_x1"][bass.ds(it * JT + 2 * m, 2)].rearrange("i p e -> p i e"), base[:, m]).then_inc(base_out[m], 16)
                order(pool, attend, nothing, route, start)
                for m in range(2):
                    pool.wait_ge(base_out[m], NK * 16)

            @block.vector
            def _(dve):
                dve.wait_ge(weights, NW)
                dve.tensor_tensor(gbo[:, :, :], keep["gates"][:, 0, :, :], bo[:, :].unsqueeze(1).broadcast_to([P, B, E]), ALU.mult).then_inc(once, 1)

                def attend(b, c, it, u, s):
                    dve.wait_ge(heads_in[s], (u * 16 + 16) * JT)
                    def normalise(j):
                        n, k = j % 2, it * 2 + j // 2
                        dve.wait_ge(rec_done[n], k + 1)
                        dve.wait_ge(wo_done[n], k)
                        dve.tensor_tensor(nrm[:, n], heads[:, s, 4 * j:4 * j + 4, :], rec[:, n], ALU.mult).then_inc(nrm_done[n], 1)
                    for j in range(JT):
                        n, k = j % 2, it * 2 + j // 2
                        dve.wait_ge(den_full[n], k + 1)
                        dve.reciprocal(rec[:, n], dp[n][:, :, :]).then_inc(rec_done[n], 1)
                        if j:
                            normalise(j - 1)
                    normalise(JT - 1)
                    dve.wait_ge(xb_done[s], u + 1)
                    for m in range(2):
                        for n in range(2):
                            dve.wait_ge(wo_done[n], it * 2 + m + 1)
                        dve.tensor_tensor(att[:, m], ap[m][:, :, :], keep["gates"][:, 0, bass.ds(b, 1), :].broadcast_to([P, 2, E]), ALU.mult).then_inc(att_done[m], 1)
                    for m in range(2):
                        dve.wait_ge(att_done[m], it + 1)
                        dve.wait_ge(base_done[m], it - 1 if c >= 2 else b * CPB)
                        last = dve.tensor_tensor(x1[:, s, 2 * m:2 * m + 2, :], att[:, m], x[:, s, 2 * m:2 * m + 2, :], ALU.add)
                    last.then_inc(x1_done[s], 1)

                def norm(b, c, it, u, s):
                    dve.wait_ge(x1_done[s], u + 1)
                    dve.memset(tick[:, :], 0.0)
                    for j in range(JT):
                        last = dve.bn_stats(stats[:, j, :], x1[:, s, j, :])
                    last.then_inc(ln_step, 1)
                    dve.wait_ge(ln_step, it * LN + 1)
                    dve.memset(tick[:, :], 0.0)
                    for j in range(JT):
                        last = dve.bn_aggr(mv[:, j, :], stats[:, j, :])
                    last.then_inc(ln_step, 1)
                    dve.wait_ge(ln_step, it * LN + 2)
                    dve.tensor_scalar(ve[:, :], mv[:, :, 1], EPS, None, ALU.add).then_inc(var_done, 1)
                    dve.wait_ge(sd_done, it + 1)
                    inverse_root(dve, rstd[:, :], sd[:, :], ve[:, :], r1[:, :], r2[:, :], ln_step, it * LN + 2)
                    dve.wait_ge(tp_done, it)
                    for j in range(JT):
                        last = dve.tensor_scalar(xn[:, j, :], x1[:, s, j, :], mv[:, j, 0:1], rstd[:, j:j + 1],
                                                 ALU.subtract, ALU.mult)
                    last.then_inc(xn_done, 1)

                def route(b, c, it, u, s):
                    n = [0]

                    def link(ins):
                        n[0] += 1
                        ins.then_inc(route_step, 1)
                        dve.wait_ge(route_step, it * RS + n[0])
                    wide = lambda t: t.unsqueeze(2).broadcast_to([P, JT, NX])
                    dve.wait_ge(lg_full, it + 1)
                    link(dve.tensor_tensor(lg[:, :, :], lp[:, :, :], gbias[:, :].unsqueeze(1).broadcast_to([P, JT, NX]), ALU.add))
                    link(dve.reduce_max(mxs[:, :], lg[:, :, :], AX.X))
                    dve.tensor_tensor(sh[:, :, :], lg[:, :, :], wide(mxs[:, :]), ALU.subtract).then_inc(sh_done, 1)
                    dve.wait_ge(ex_done, it + 1)
                    link(dve.reduce_sum(sums[:, :], ex[:, :, :], AX.X))
                    link(dve.reciprocal(rsum[:, :], sums[:, :]))
                    link(dve.tensor_tensor(pr[:, :, :], ex[:, :, :], wide(rsum[:, :]), ALU.mult))
                    dve.memset(tick[:, :], 0.0)
                    for j in range(JT):
                        last = dve.max(out=top[:, j, :], in_=pr[:, j, :])
                    link(last)
                    dve.memset(tick[:, :], 0.0)
                    for j in range(JT):
                        last = dve.max_index(out=topi[:, j, :], in_max=top[:, j, :], in_values=pr[:, j, :])
                    link(last)
                    link(dve.tensor_copy(topf[:, :, :], topi[:, :, :]))
                    iota = keep["iota8"][:, :].unsqueeze(1).broadcast_to([P, JT, NX])
                    dve.tensor_tensor(o1[:, :, :], iota, wide(topf[:, :, 0]), ALU.is_equal)
                    link(dve.tensor_tensor(o2[:, :, :], iota, wide(topf[:, :, 1]), ALU.is_equal))
                    dve.tensor_tensor(w1[:, :, :], o1[:, :, :], wide(pr[:, :, 0]), ALU.mult)
                    link(dve.tensor_tensor(w2[:, :, :], o2[:, :, :], wide(pr[:, :, 1]), ALU.mult))
                    dve.wait_ge(cp_full, it)
                    link(dve.tensor_tensor(cw[:, :, :], w1[:, :, :], w2[:, :, :], ALU.add))
                    dve.tensor_copy(keep["cw"][:, bass.ds(it * JT, JT), :], cw[:, :, :]).then_inc(cw_done, 1)
                    for m in range(2):
                        dve.wait_ge(bp_full[m], it + 1)
                        dve.wait_ge(base_done[m], it)
                        dve.tensor_tensor(wb[:, m], tp[m][:, :].rearrange("p (j e) -> p j e", e=E),
                                          keep["gates"][:, 1, bass.ds(b, 1), :].broadcast_to([P, 2, E]), ALU.mult).then_inc(wb_done[m], 1)
                    assert n[0] == RS
                order(dve, attend, norm, route)

            @block.scalar
            def _(act):
                def start(b):
                    for k, name in enumerate(("shift_b", "scale_b")):
                        act.activation(mod_now[:, k, :].unsqueeze(2), keep[name][:, :, bass.ds(b, 1)], ACT.Copy).then_inc(mod_set, 1)
                    act.wait_ge(mod_set, b * 2 + 2)

                def norm(b, c, it, u, s):
                    act.wait_ge(var_done, it + 1)
                    act.activation(sd[:, :], ve[:, :], ACT.Sqrt).then_inc(sd_done, 1)
                    act.wait_ge(tp_done, it + 1)
                    act.wait_ge(lg_full, it)
                    act.wait_ge(hT_out[s], u * 16)
                    for eh in range(EH):
                        last = act.activation(hT[:, s, eh, :], tp[eh][:, :], ACT.Identity, bias=mod_now[:, 0, eh:eh + 1],
                                              scale=mod_now[:, 1, eh:eh + 1])
                    last.then_inc(hT_done, 1)

                def route(b, c, it, u, s):
                    act.wait_ge(hT_done, it + 1)
                    act.dma_start(io["s_h"][bass.ds(it, 1)].rearrange("o e r t -> r (o e) t"), hT[:, s]).then_inc(hT_out[s], 16)
                    act.wait_ge(sh_done, it + 1)
                    act.activation(ex[:, :, :], sh[:, :, :], ACT.Exp).then_inc(ex_done, 1)
                    act.wait_ge(cp_full, it + 1)
                    act.wait_ge(bp_full[1], it)
                    act.activation(cwT[:, :], cp[0:NX, :], ACT.Copy).then_inc(cwT_done, 1)
                order(act, nothing, norm, route, start)
                for s in range(2):
                    act.wait_ge(hT_out[s], NK // 2 * 16)

            @block.tensor
            def _(pe):
                pe.wait_ge(weights, NW)

                def attend(b, c, it, u, s):
                    def project(j):
                        n, k = j % 2, it * 2 + j // 2
                        pe.wait_ge(nrm_done[n], k + 1)
                        if n == 0:
                            pe.wait_ge(att_done[j // 2], it)
                        for g in range(4):
                            last = pe.matmul(ap[j // 2][:, n, :], nrm[:, n, g, :], wo[:, g, :], start=(g == 0), stop=(g == 3))
                        last.then_inc(wo_done[n], 1)
                    pe.wait_ge(heads_in[s], (u * 16 + 16) * JT)
                    for j in range(JT):
                        n, k = j % 2, it * 2 + j // 2
                        pe.wait_ge(rec_done[n], k)
                        pe.matmul(dp[n][:, :, :], keep["spread"][:, :], heads[:, s, 4 * j:4 * j + 4, :],
                                  start=True, stop=True).then_inc(den_full[n], 1)
                        if j:
                            project(j - 1)
                    project(JT - 1)

                def norm(b, c, it, u, s):
                    pe.wait_ge(xn_done, it + 1)
                    pe.wait_ge(wb_done[0], it)
                    pe.wait_ge(wb_done[1], it)
                    for eh in range(EH):
                        for j in range(JT):
                            last = pe.transpose(tp[eh][:, j * P:(j + 1) * P], xn[:, j, eh * P:(eh + 1) * P], keep["ident"][:, :])
                    last.then_inc(tp_done, 1)

                def route(b, c, it, u, s):
                    pe.wait_ge(hT_done, it + 1)
                    pe.wait_ge(cw_done, it)
                    for j in range(JT):
                        for eh in range(EH):
                            last = pe.matmul(lp[:, j, :], hT[:, s, eh, j * P:(j + 1) * P], gw[:, eh, :], start=(eh == 0), stop=(eh == EH - 1))
                    last.then_inc(lg_full, 1)
                    pe.wait_ge(cw_done, it + 1)
                    pe.wait_ge(cwT_done, it)
                    for j in range(JT):
                        last = pe.transpose(cp[0:NX, j * P:(j + 1) * P], cw[:, j, :], keep["ident"][:, :])
                    last.then_inc(cp_full, 1)
                    pe.wait_ge(cwT_done, it + 1)
                    for m in range(2):
                        for j in range(2):
                            last = pe.matmul(tp[m][:, j * E:(j + 1) * E], cwT[:, (2 * m + j) * P:(2 * m + j + 1) * P], b3[:, :],
                                             start=True, stop=True)
                        last.then_inc(bp_full[m], 1)
                order(pe, attend, norm, route)


def phase_experts(nc, io, keep):
    JT = CH // P
    with PhaseMemory(nc, "exp") as a:
        w1, w2, w3 = (a.sb(n, [P, NX, EH, E]) for n in ("w1", "w2", "w3"))
        b1, b2 = (a.sb(n, [P, NX, EH]) for n in ("b1", "b2"))
        hT = a.sb("hT", [P, 2, EH, CH])
        h1 = a.sb("h1", [P, 2, EH, CH])
        h2 = a.sb("h2", [P, 2, EH, CH])
        y = a.sb("y", [P, 2, JT, E])
        base = a.sb("base", [P, 2, JT, E])
        p1 = [a.ps(f"p1{i}", [P, CH]) for i in range(EH)]
        p2 = [a.ps(f"p2{i}", [P, CH]) for i in range(EH)]
        p3 = [a.ps(f"p3{i}", [P, 2, E]) for i in range(4)]
        gb_now = a.sb("gb_now", [P, 1, E])
        w_in, gb_set = a.sems("w_in", NX), a.sem("gb_set")
        h_in, base_in, out_done, out_sent = (a.sems(n, 2) for n in ("h_in", "base_in", "out_done", "out_sent"))
        p1_full, h1_done, p2_full, h2_done = (a.sems(n, EH) for n in ("p1_full", "h1_done", "p2_full", "h2_done"))
        p3_full, p3_free = a.sems("p3_full", 4), a.sems("p3_free", 4)
        steps = [(s, e) for s in range(2) for e in range(NX)]
        NS = len(steps)
        NT = B * CPB // 2

        with nc.Block() as block:

            @block.sync
            def _(sp):
                for e in range(NX):
                    for w, name in ((w1, "w1"), (w2, "w2"), (w3, "w3")):
                        sp.dma_start(w[:, e], io[name][e].rearrange("(k p) n -> p k n", p=P)).then_inc(w_in[e], 16)
                    for w, name in ((b1, "b1"), (b2, "b2")):
                        sp.dma_start(w[:, e, :], io[name][e]).then_inc(w_in[e], 16)

                def load(t, s):
                    sp.dma_start(hT[:, s], io["s_h"][bass.ds(t * 2 + s, 1)]
                                 .rearrange("o e r t -> r (o e) t")).then_inc(h_in[s], 16)
                for s in range(2):
                    load(0, s)
                with sp.Fori(0, NT - 1) as t:
                    for s in range(2):
                        sp.wait_ge(p1_full[EH - 1], t * NS + (s + 1) * NX)
                        load(t + 1, s)

            @block.gpsimd
            def _(pool):
                with pool.Fori(0, B) as b:
                    pool.tensor_copy(gb_now[:, :, :], keep["gates"][:, 1, bass.ds(b, 1), :]).then_inc(gb_set, 1)
                    with pool.Fori(0, CPB // 2) as r:
                        t = b * (CPB // 2) + r
                        for s in range(2):
                            pool.wait_ge(out_sent[s], t * 16)
                            pool.dma_start(base[:, s], io["s_x1"][bass.ds(t * (2 * JT) + s * JT, JT)].rearrange("j p e -> p j e")).then_inc(base_in[s], 16)
                        for s in range(2):
                            pool.wait_ge(gb_set, b + 1)
                            for buf in (2, 3):
                                pool.wait_ge(p3_free[buf], t * (NS // 2) + (s + 1) * (NX // 2))
                            pool.tensor_tensor(y[:, s], y[:, s], gb_now[:, :, :].broadcast_to([P, JT, E]), ALU.mult).then_inc(out_done[s], 1)
                            pool.wait_ge(out_done[s], t * 2 + 1)
                            pool.wait_ge(base_in[s], t * 16 + 16)
                            pool.tensor_tensor(base[:, s], y[:, s], base[:, s], ALU.add).then_inc(out_done[s], 1)
                            pool.wait_ge(out_done[s], t * 2 + 2)
                            pool.dma_start(io["out"][bass.ds(b, 1), bass.ds(r * (2 * CH) + s * CH, CH), :]
                                           .rearrange("o (j p) e -> p (o j) e", p=P), base[:, s]).then_inc(out_sent[s], 16)
                for s in range(2):
                    pool.wait_ge(out_sent[s], NT * 16)

            @block.scalar
            def _(act):
                with act.Fori(0, NT) as t:
                    def relu(dst, src, bias, full, done, k):
                        n = t * NS + k
                        for eh in range(EH):
                            act.wait_ge(full[eh], n + 1)
                            act.activation(dst[:, k % 2, eh, :], src[eh][:, :], ACT.Relu,
                                           bias=bias[:, steps[k][1], eh:eh + 1]).then_inc(done[eh], 1)
                    for k in range(NS + 1):
                        if k < NS:
                            act.wait_ge(p2_full[EH - 1], t * NS + max(k - 1, 0))
                            relu(h1, p1, b1, p1_full, h1_done, k)
                        if k:
                            act.wait_ge(p3_full[2 * ((k - 1) % 2) + 1], t * (NS // 2) + (k - 1) // 2)
                            relu(h2, p2, b2, p2_full, h2_done, k - 1)

            @block.vector
            def _(dve):
                with dve.Fori(0, NT) as t:
                    for k, (s, e) in enumerate(steps):
                        if e == 0:
                            dve.wait_ge(out_done[s], t * 2)
                        for m in range(2):
                            buf = 2 * (k % 2) + m
                            if e:
                                dve.wait_ge(p3_free[2 * ((k - 1) % 2) + m], t * (NS // 2) + (k - 1) // 2 + 1)
                            dve.wait_ge(p3_full[buf], t * (NS // 2) + k // 2 + 1)
                            for j in range(2):
                                jj = 2 * m + j
                                w = keep["cw"][:, bass.ds(t * (2 * JT) + (s * JT + jj), 1), e:e + 1].rearrange("p o e -> p (o e)")
                                if e == 0:
                                    last = dve.tensor_scalar(y[:, s, jj, :], p3[buf][:, j, :], w, None, ALU.mult)
                                else:
                                    last = dve.scalar_tensor_tensor(out=y[:, s, jj, :], in0=p3[buf][:, j, :], scalar=w,
                                                                    in1=y[:, s, jj, :], op0=ALU.mult, op1=ALU.add)
                            last.then_inc(p3_free[buf], 1)

            @block.tensor
            def _(pe):
                for e in range(NX):
                    pe.wait_ge(w_in[e], 5 * 16)
                with pe.Fori(0, NT) as t:
                    def layer(k, w, src, dst, full, free):
                        s, e = steps[k]
                        for eh in range(EH):
                            pe.wait_ge(free[eh], t * NS + k)
                            for ki in range(EH):
                                last = pe.matmul(dst[eh][:, :], w[:, e, ki, eh * P:(eh + 1) * P], src[:, ki, :],
                                                 start=(ki == 0), stop=(ki == EH - 1))
                            last.then_inc(full[eh], 1)
                    for k in range(NS + 2):
                        if k < NS:
                            if steps[k][1] == 0:
                                pe.wait_ge(h_in[steps[k][0]], t * 16 + 16)
                            layer(k, w1, hT[:, steps[k][0]], p1, p1_full, h1_done)
                        if 1 <= k <= NS:
                            pe.wait_ge(h1_done[EH - 1], t * NS + k)
                            layer(k - 1, w2, h1[:, (k - 1) % 2], p2, p2_full, h2_done)
                        if k >= 2:
                            s, e = steps[k - 2]
                            pe.wait_ge(h2_done[EH - 1], t * NS + k - 1)
                            for m in range(2):
                                buf = 2 * (k % 2) + m
                                pe.wait_ge(p3_free[buf], t * (NS // 2) + (k - 2) // 2)
                                for j in range(2):
                                    for ki in range(EH):
                                        last = pe.matmul(p3[buf][:, j, :], h2[:, k % 2, ki, (2 * m + j) * P:(2 * m + j + 1) * P],
                                                         w3[:, e, ki, :], start=(ki == 0), stop=(ki == EH - 1))
                                last.then_inc(p3_full[buf], 1)


SCRATCH = {
    "s_rel": ([2, D, TAB + 2 * G], F16),
    "s_q": ([2, B * NB, EH * P, P], F16),
    "s_k": ([2, B * NB, EH * P, P], F16),
    "s_v": ([B * NB, P, H, 2 * D], F32),
    "s_m": ([B * NB, H, P], F16),
    "s_of": ([B * NB, 4, P, P], F32),
    "s_o": ([B * NB, 4, P, P], F32),
    "s_h": ([B * CPB, EH, P, CH], F32),
    "s_x1": ([B * NB, P, E], F32),
}

KEEP = {
    "ident": ([P, P], F32), "mask_h": ([P, HH], F16), "mask_i": ([P, G], F16),
    "ident_s": ([G, H, G], F16), "mask_f": ([G, G], F16), "iota8": ([P, NX], F32),
    "spread": ([P, P], F32), "table": ([P, 2, TAB], F16),
    "shift_a": ([P, EH, B], F32), "scale_a": ([P, EH, B], F32),
    "shift_b": ([P, EH, B], F32), "scale_b": ([P, EH, B], F32), "gates": ([P, 2, B, E], F32),
    "cw": ([P, B * NB, NX], F32),
}


def adaln_moe_layer(nc, **io):
    for name, (shape, dt) in SCRATCH.items():
        io[name] = nc.dram_tensor(name, shape, dt).ap()
    with ExitStack() as ctx:
        keep = {name: ctx.enter_context(nc.sbuf_tensor(name, shape, dt)) for name, (shape, dt) in KEEP.items()}
        phase_modulation(nc, io, keep)
        phase_project(nc, io, keep)
        phase_row_max(nc, io, keep)
        phase_far(nc, io, keep)
        phase_near(nc, io, keep)
        phase_output(nc, io, keep)
        phase_experts(nc, io, keep)


def kernel(**inputs):
    import numpy as _np
    import concourse.bacc as _bacc
    from concourse import mybir as _mybir
    from concourse.bass_utils import run_bass_kernel_spmd as _run

    def heads_inside(w):
        return w.reshape(-1, EH, HH, D).transpose(0, 1, 3, 2).reshape(w.shape)

    def on_partitions(v):
        return v.reshape(v.shape[:-1] + (EH, P)).swapaxes(-1, -2)

    get = {name: _np.asarray(v) for name, v in inputs.items()}
    r0 = _np.broadcast_to(get["L0_attn_rel_key"][0][None, :, None], (EH, D, HH)).reshape(E)
    laid = {
        "x": get["L0_attn_x"], "wq": heads_inside(get["L0_attn_Wq"]), "wk": heads_inside(get["L0_attn_Wk"]),
        "wv": get["L0_attn_Wv"], "wo": get["L0_attn_Wo"], "bv": get["L0_attn_bv"], "bo": get["L0_attn_bo"],
        "bq": on_partitions(heads_inside(get["L0_attn_bq"])), "bk": on_partitions(heads_inside(get["L0_attn_bk"])),
        "r0": on_partitions(r0), "relT": get["L0_attn_rel_key"].T, "cT": get["L0_c"].T, "wmod": get["L0_wmod"],
        "gwT": get["L0_ffn_gate_w"].T, "gate_b": get["L0_ffn_gate_b"],
        "w1": get["L0_ffn_w1"], "w2": get["L0_ffn_w2"], "w3": get["L0_ffn_w3"],
        "b1": on_partitions(get["L0_ffn_b1"]), "b2": on_partitions(get["L0_ffn_b2"]), "b3": get["L0_ffn_b3"],
    }
    nc = _bacc.Bacc("TRN2", target_bir_lowering=False, num_devices=1)
    arrays, io = {}, {}
    for name, v in laid.items():
        v = _np.ascontiguousarray(v)
        arrays[f"in_{name}"] = v
        io[name] = nc.dram_tensor(f"in_{name}", v.shape, _mybir.dt.from_np(v.dtype), kind="ExternalInput").ap()
    io["out"] = nc.dram_tensor("out_0", (B, S, E), _mybir.dt.from_np(_np.dtype("float32")), kind="ExternalOutput").ap()
    adaln_moe_layer(nc, **io)
    r = _run(nc, [arrays], core_ids=[0])
    return r.results[0]["out_0"]
```

```python
from contextlib import ExitStack

import concourse.bass as bass
from concourse import mybir

ALU = mybir.AluOpType
ACT = mybir.ActivationFunctionType
AX = mybir.AxisListType
F32 = mybir.dt.float32
F16 = mybir.dt.float16
U32 = mybir.dt.uint32

B, S, E = 4, 2048, 256
H, D, W = 16, 16, 512
P = 128
NB = S // P
EH = E // P
HH = 8
CH = 512
CPB = S // CH
NX, TOP = 8, 2
G = 8
EPS = 1e-5
SCALE = D ** -0.5
KR = 4 * D + 1
NJ = W // P + 1
TAB = 760
TAB0 = 632
FARI = NJ
MASK = 30000.0


class PhaseMemory:

    def __init__(self, nc, tag):
        self.nc, self.tag, self.ctx, self.taken = nc, tag, ExitStack(), []

    def __enter__(self):
        return self

    def __exit__(self, *a):
        self.nc.clear_and_free_semaphores(self.taken)
        self.nc.all_engine_barrier()
        return self.ctx.__exit__(*a)

    def sb(self, name, shape, dt=F32):
        return self.ctx.enter_context(self.nc.sbuf_tensor(f"{self.tag}_{name}", shape, dt))

    def ps(self, name, shape):
        return self.ctx.enter_context(self.nc.psum_tensor(f"{self.tag}_{name}", shape, F32))

    def sem(self, name):
        self.taken.append(self.nc.alloc_semaphore(name=f"{self.tag}_{name}"))
        return self.taken[-1]

    def sems(self, name, n):
        return [self.sem(f"{name}{i}") for i in range(n)]


def phase_modulation(nc, io, keep):
    with PhaseMemory(nc, "mod") as a:
        cT = a.sb("cT", [P, EH, B])
        e_c = a.sb("e_c", [P, EH, B])
        den = a.sb("den", [P, EH, B])
        rec = a.sb("rec", [P, EH, B])
        silu = a.sb("silu", [P, EH, B])
        silu_b = a.sb("silu_b", [P, EH, B, P])
        wmod = a.sb("wmod", [P, EH, 6 * E])
        mag = a.sb("mag", [P, 2, B, E])
        raw = a.sb("raw", [P, 2, B, E])
        sgn = a.sb("sgn", [P, 2, B, E])
        relT = a.sb("relT", [D, W])
        relx = a.sb("relx", [D, TAB + 2 * G])
        relh = a.sb("relh", [D, TAB + 2 * G], F16)
        rell = a.sb("rell", [D, TAB + 2 * G], F16)
        mask_dh = a.sb("mask_dh", [P, D, HH])
        pm = a.ps("pm", [P, 12, B])
        pg = [a.ps(f"pg{i}", [P, 2, E]) for i in range(4)]
        loaded, wloaded = a.sem("loaded"), a.sem("wloaded")
        pool_step, act_exp, dve_step = a.sem("pool_step"), a.sem("act_exp"), a.sem("dve_step")
        silu_ready, mod_ready, gate_ready = a.sem("silu_ready"), a.sem("mod_ready"), a.sem("gate_ready")
        rel_ready, table_out, table_in = a.sem("rel_ready"), a.sem("table_out"), a.sem("table_in")
        rel_step = a.sem("rel_step")
        with nc.Block() as block:

            @block.sync
            def _(sp):
                sp.dma_start(cT[:, :, :], io["cT"].rearrange("(e p) b -> p e b", p=P)).then_inc(loaded, 16)
                sp.dma_start(relT[:, :], io["relT"]).then_inc(loaded, 16)
                sp.dma_start(wmod[:, :, :], io["wmod"].rearrange("(e p) n -> p e n", p=P)).then_inc(wloaded, 16)
                sp.wait_ge(rel_ready, 1)
                sp.dma_start(io["s_rel"][0], relh[:, :]).then_inc(table_out, 16)
                sp.dma_start(io["s_rel"][1], rell[:, :]).then_inc(table_out, 16)
                sp.wait_ge(table_out, 32)
                for part in range(2):
                    for i in range(G):
                        sp.dma_start(keep["table"][i * D:(i + 1) * D, part, :],
                                     io["s_rel"][part][:, G - 1 - i:G - 1 - i + TAB]).then_inc(table_in, 16)
                sp.wait_ge(table_in, 32 * G)

            @block.gpsimd
            def _(pool):
                pool.memset(keep["ident"][:, :], 0.0)
                pool.memset(mask_dh[:, :, :], 1.0)
                pool.memset(keep["mask_i"][:, :], 1.0)
                pool.memset(keep["ident_s"][:, :, :], MASK)
                pool.memset(keep["mask_f"][:, :], -MASK)
                pool.memset(keep["ident_m"][:, :], 0.0)
                pool.memset(keep["mask_n"][:, :], -MASK)
                pool.memset(keep["iota8"][:, :], 0.0)
                pool.memset(keep["spread"][:, :], 0.0).then_inc(pool_step, 1)
                pool.wait_ge(pool_step, 1)
                pool.affine_select(out=keep["ident"][:, :], in_=keep["ident"][:, :], compare_op=ALU.not_equal,
                                   fill=1.0, base=0, pattern=[[-1, P]], channel_multiplier=1)
                pool.affine_select(out=keep["mask_i"][:, :], in_=keep["mask_i"][:, :], compare_op=ALU.is_ge,
                                   fill=0.0, base=0, pattern=[[-D, G]], channel_multiplier=1)
                pool.affine_select(out=keep["ident_s"][:, :, :], in_=keep["ident_s"][:, :, :], compare_op=ALU.is_equal,
                                   fill=0.0, base=0, pattern=[[0, H], [-1, G]], channel_multiplier=1)
                pool.affine_select(out=keep["mask_f"][:, :], in_=keep["mask_f"][:, :], compare_op=ALU.is_ge,
                                   fill=0.0, base=-1, pattern=[[1, G]], channel_multiplier=-1)
                pool.affine_select(out=keep["ident_m"][:, :], in_=keep["ident_m"][:, :], compare_op=ALU.not_equal,
                                   fill=MASK, base=0, pattern=[[-1, P]], channel_multiplier=1)
                pool.affine_select(out=keep["mask_n"][:, :], in_=keep["mask_n"][:, :], compare_op=ALU.is_ge,
                                   fill=0.0, base=-1, pattern=[[-1, P]], channel_multiplier=1)
                pool.affine_select(out=mask_dh[:, :, :], in_=mask_dh[:, :, :], compare_op=ALU.is_equal,
                                   fill=0.0, base=0, pattern=[[-HH, D], [-1, HH]], channel_multiplier=1)
                for n in range(1, NX):
                    pool.memset(keep["iota8"][:, n:n + 1], float(n))
                for q in range(4):
                    v = keep["spread"][:, 32 * q:32 * q + 32]
                    last = pool.affine_select(out=v, in_=v, compare_op=ALU.not_equal, fill=1.0,
                                              base=-(32 * q + D), pattern=[[0, 32]], channel_multiplier=1)
                last.then_inc(pool_step, 1)
                pool.wait_ge(pool_step, 2)
                pool.affine_select(out=keep["mask_i"][:, :], in_=keep["mask_i"][:, :], compare_op=ALU.is_ge,
                                   fill=0.0, base=D - 1, pattern=[[D, G]], channel_multiplier=-1).then_inc(pool_step, 1)
                pool.wait_ge(pool_step, 3)

            @block.scalar
            def _(act):
                act.wait_ge(loaded, 32)
                act.activation(e_c[:, :, :], cT[:, :, :], ACT.Exp, scale=-1.0).then_inc(act_exp, 1)

            @block.vector
            def _(dve):
                n = [0]

                def link(ins):
                    n[0] += 1
                    ins.then_inc(dve_step, 1)
                    dve.wait_ge(dve_step, n[0])

                dve.wait_ge(act_exp, 1)
                link(dve.tensor_scalar(den[:, :, :], e_c[:, :, :], 1.0, None, ALU.add))
                link(dve.reciprocal(rec[:, :, :], den[:, :, :]))
                dve.wait_ge(loaded, 32)
                link(dve.tensor_tensor(silu[:, :, :], cT[:, :, :], rec[:, :, :], ALU.mult))
                dve.tensor_copy(silu_b[:, :, :, :], silu[:, :, :].unsqueeze(3).broadcast_to([P, EH, B, P])).then_inc(silu_ready, 1)
                link(dve.tensor_scalar(relx[:, P:P + W], relT[:, :], relT[:, 0:1], None, ALU.subtract))
                dve.memset(relx[:, 0:P], 0.0)
                link(dve.tensor_copy(relx[:, P + W:], relx[:, P + W - 1:P + W].broadcast_to([D, TAB + 2 * G - P - W])))
                link(dve.tensor_copy(relh[:, :], relx[:, :]))
                dve.tensor_tensor(rell[:, :], relx[:, :], relh[:, :], ALU.subtract).then_inc(rel_ready, 1)
                dve.wait_ge(pool_step, 2)
                with nc.allow_low_precision("zeros and one one"):
                    dve.tensor_reduce(keep["mask_h"][:, :], mask_dh[:, :, :].rearrange("p d h -> p h d"), AX.X, ALU.add)
                dve.wait_ge(mod_ready, 1)
                for kind, dst in ((0, "shift_a"), (3, "shift_b")):
                    dve.tensor_copy(keep[dst][:, :, :], pm[:, 2 * kind:2 * kind + 2, :])
                for kind, dst in ((1, "scale_a"), (4, "scale_b")):
                    dve.tensor_scalar(keep[dst][:, :, :], pm[:, 2 * kind:2 * kind + 2, :], 1.0, None, ALU.add)
                for b in range(B):
                    dve.wait_ge(gate_ready, b + 1)
                    dve.tensor_copy(raw[:, :, b, :], pg[b][:, :, :])
                    link(dve.tensor_scalar(sgn[:, :, b, :], pg[b][:, :, :], 0.0, 2.0, ALU.is_ge, ALU.mult))
                flat = lambda t: t[:, :, :, :].rearrange("p k b e -> p (k b e)")
                link(dve.scalar_tensor_tensor(out=flat(mag), in0=flat(raw), scalar=-1.0, in1=flat(raw),
                                              op0=ALU.mult, op1=ALU.max))
                link(dve.tensor_scalar(flat(raw), flat(mag), 0.25, None, ALU.max))
                link(dve.scalar_tensor_tensor(out=keep["gates"][:, :, :, :].rearrange("p k b e -> p (k b e)"),
                                              in0=sgn[:, :, :, :].rearrange("p k b e -> p (k b e)"), scalar=-1.0,
                                              in1=flat(raw),
                                              op0=ALU.add, op1=ALU.mult))

            @block.tensor
            def _(pe):
                pe.wait_ge(silu_ready, 1)
                pe.wait_ge(wloaded, 16)
                for n in range(12):
                    for eh in range(EH):
                        last = pe.matmul(pm[:, n, :], wmod[:, eh, n * P:(n + 1) * P], silu[:, eh, :],
                                         start=(eh == 0), stop=(eh == EH - 1))
                last.then_inc(mod_ready, 1)
                for b in range(B):
                    for k, kind in enumerate((2, 5)):
                        for eh in range(EH):
                            last = pe.matmul(pg[b][:, k, :], silu_b[:, eh, b, :],
                                             wmod[:, eh, kind * E:(kind + 1) * E],
                                             start=(eh == 0), stop=(eh == EH - 1))
                    last.then_inc(gate_ready, 1)


def inverse_root(dve, out, sd, ve, t1, t2, step, n):
    dve.reciprocal(t1, sd).then_inc(step, 1)
    dve.wait_ge(step, n + 1)
    dve.tensor_tensor(t2, t1, ve, ALU.mult).then_inc(step, 1)
    dve.wait_ge(step, n + 2)
    dve.scalar_tensor_tensor(out=t2, in0=t2, scalar=-0.5, in1=t1, op0=ALU.mult, op1=ALU.mult).then_inc(step, 1)
    dve.wait_ge(step, n + 3)
    dve.scalar_tensor_tensor(out=out, in0=t2, scalar=1.5, in1=t1, op0=ALU.add, op1=ALU.mult).then_inc(step, 1)
    dve.wait_ge(step, n + 4)


def phase_project(nc, io, keep):
    with PhaseMemory(nc, "prj") as a:
        JT = CH // P
        wq, wk, wv = (a.sb(n, [P, EH, E]) for n in ("wq", "wk", "wv"))
        bq, bk, r0, bkr = (a.sb(n, [P, EH]) for n in ("bq", "bk", "r0", "bkr"))
        bv = a.sb("bv", [P, E])
        x = a.sb("x", [P, 2, JT, E])
        stats = a.sb("stats", [P, 2, JT, 6])
        tick = a.sb("tick", [P, 1])
        mod_now = a.sb("mod_now", [P, 2, EH])
        mv = a.sb("mv", [P, 2, JT, 2])
        ve, sd, r1, r2, rstd = (a.sb(n, [P, 2, JT]) for n in ("ve", "sd", "r1", "r2", "rstd"))
        xn = a.sb("xn", [P, 2, JT, E])
        hT = a.sb("hT", [P, 2, EH, CH])
        qf = a.sb("qf", [P, 4, CH])
        hi = a.sb("hi", [P, 4, CH], F16)
        lo = a.sb("lo", [P, 4, CH], F16)
        vx = a.sb("vx", [P, JT, H, 2 * D])
        tp = [a.ps(f"tp{i}", [P, CH]) for i in range(EH)]
        qp = [a.ps(f"qp{i}", [P, CH]) for i in range(4)]
        vp = [a.ps(f"vp{i}", [P, 2, E]) for i in range(2)]
        weights, biases = a.sem("weights"), a.sem("biases")
        x_in = a.sems("x_in", 2)
        xn_done, tp_done, hT_done = (a.sems(n, 2) for n in ("xn_done", "tp_done", "hT_done"))
        ln_step, once = a.sem("ln_step"), a.sem("once")
        mod_set = a.sem("mod_set")
        var_done, sd_done = a.sems("var_done", 2), a.sems("sd_done", 2)
        LN = 6
        qp_done, qf_done, hi_done, lo_done, hi_out, lo_out = (
            a.sems(n, 4) for n in ("qp_done", "qf_done", "hi_done", "lo_done", "hi_out", "lo_out"))
        vp_done, vx_done, vx_out = (a.sems(n, 2) for n in ("vp_done", "vx_done", "vx_out"))
        xv = io["x"].rearrange("b (c j p) e -> (b c) p j e", j=JT, p=P)
        NI = B * CPB // 2

        with nc.Block() as block:

            def low(dve, it, n):
                dve.wait_ge(hi_done[n], it + 1)
                dve.wait_ge(lo_out[n], it * 16)
                dve.tensor_tensor(lo[:, n, :], qf[:, n, :], hi[:, n, :], ALU.subtract).then_inc(lo_done[n], 1)

            @block.gpsimd
            def _(pool):
                for w, name in ((wq, "wq"), (wk, "wk"), (wv, "wv")):
                    pool.dma_start(w[:, :, :], io[name].rearrange("(e p) n -> p e n", p=P)).then_inc(weights, 16)
                for w, name in ((bq, "bq"), (bk, "bk"), (r0, "r0")):
                    pool.dma_start(w[:, :], io[name]).then_inc(biases, 16)
                pool.dma_start(bv[:, :], io["bv"].partition_broadcast(P)).then_inc(biases, 16)
                with pool.Fori(0, NI) as t:
                    for s in range(2):
                        pool.wait_ge(xn_done[s], t)
                        pool.dma_start(x[:, s], xv[bass.ds(t * 2 + s, 1)].rearrange("o p j e -> p (o j) e")).then_inc(x_in[s], 16)

            @block.vector
            def _(dve):
                dve.memset(vx[:, :, :, D:], 1.0)
                dve.wait_ge(biases, 64)
                dve.tensor_tensor(bkr[:, :], bk[:, :], r0[:, :], ALU.add).then_inc(once, 1)
                dve.wait_ge(once, 1)
                with dve.Fori(0, NI) as t:
                    for s in range(2):
                        it = t * 2 + s
                        dve.wait_ge(x_in[s], t * 16 + 16)
                        for j in range(JT):
                            last = dve.bn_stats(stats[:, s, j, :], x[:, s, j, :])
                        last.then_inc(ln_step, 1)
                        dve.wait_ge(ln_step, it * LN + 1)
                        dve.memset(tick[:, :], 0.0)
                        for j in range(JT):
                            last = dve.bn_aggr(mv[:, s, j, :], stats[:, s, j, :])
                        last.then_inc(ln_step, 1)
                        dve.wait_ge(ln_step, it * LN + 2)
                        dve.tensor_scalar(ve[:, s, :], mv[:, s, :, 1], EPS, None, ALU.add).then_inc(var_done[s], 1)
                        dve.wait_ge(sd_done[s], t + 1)
                        inverse_root(dve, rstd[:, s, :], sd[:, s, :], ve[:, s, :], r1[:, s, :], r2[:, s, :], ln_step, it * LN + 2)
                        dve.wait_ge(tp_done[s], t)
                        for j in range(JT):
                            last = dve.tensor_scalar(xn[:, s, j, :], x[:, s, j, :], mv[:, s, j, 0:1], rstd[:, s, j:j + 1],
                                                     ALU.subtract, ALU.mult)
                        last.then_inc(xn_done[s], 1)
                        for n in range(4):
                            dve.wait_ge(qp_done[n], it + 1)
                            dve.wait_ge(lo_done[n], it)
                            bias = bq[:, n:n + 1] if n < 2 else bkr[:, n - 2:n - 1]
                            dve.tensor_scalar(qf[:, n, :], qp[n][:, :], bias, None, ALU.add).then_inc(qf_done[n], 1)
                            if n:
                                low(dve, it, n - 1)
                        low(dve, it, 3)
                        for n in range(2):
                            dve.wait_ge(vp_done[n], it + 1)
                            dve.wait_ge(vx_out[n], it * 16)
                            for j in range(2):
                                last = dve.tensor_tensor(vx[:, 2 * n + j, :, 0:D],
                                                         vp[n][:, j, :].rearrange("p (h d) -> p h d", d=D),
                                                         bv[:, :].rearrange("p (h d) -> p h d", d=D), ALU.add)
                            last.then_inc(vx_done[n], 1)

            @block.scalar
            def _(act):
                with act.Fori(0, B) as b:
                    for k, name in enumerate(("shift_a", "scale_a")):
                        act.activation(mod_now[:, k, :].unsqueeze(2), keep[name][:, :, bass.ds(b, 1)], ACT.Copy).then_inc(mod_set, 1)
                    act.wait_ge(mod_set, b * 2 + 2)
                    with act.Fori(0, CPB // 2) as u:
                        t = b * (CPB // 2) + u
                        for s in range(2):
                            it = t * 2 + s
                            act.wait_ge(var_done[s], t + 1)
                            act.activation(sd[:, s, :], ve[:, s, :], ACT.Sqrt).then_inc(sd_done[s], 1)
                            act.wait_ge(tp_done[s], t + 1)
                            act.wait_ge(vp_done[1], it - s)
                            for eh in range(EH):
                                last = act.activation(hT[:, s, eh, :], tp[eh][:, :], ACT.Identity,
                                                      bias=mod_now[:, 0, eh:eh + 1],
                                                      scale=mod_now[:, 1, eh:eh + 1])
                            last.then_inc(hT_done[s], 1)
                            for n in range(4):
                                act.wait_ge(qf_done[n], it + 1)
                                act.wait_ge(hi_out[n], it * 16)
                                act.wait_ge(lo_done[n], it)
                                act.activation(hi[:, n, :], qf[:, n, :], ACT.Copy).then_inc(hi_done[n], 1)

            @block.tensor
            def _(pe):
                pe.wait_ge(weights, 48)
                with pe.Fori(0, NI) as t:
                    for s in range(2):
                        it = t * 2 + s
                        pe.wait_ge(xn_done[s], t + 1)
                        pe.wait_ge(hT_done[1 - s], t + s)
                        for eh in range(EH):
                            for j in range(JT):
                                last = pe.transpose(tp[eh][:, j * P:(j + 1) * P], xn[:, s, j, eh * P:(eh + 1) * P],
                                                    keep["ident"][:, :])
                        last.then_inc(tp_done[s], 1)
                        pe.wait_ge(hT_done[s], t + 1)
                        for n in range(4):
                            w = wq if n < 2 else wk
                            pe.wait_ge(qf_done[n], it)
                            for eh in range(EH):
                                last = pe.matmul(qp[n][:, :], w[:, eh, (n % 2) * P:(n % 2 + 1) * P], hT[:, s, eh, :],
                                                 start=(eh == 0), stop=(eh == EH - 1))
                            last.then_inc(qp_done[n], 1)
                        for n in range(2):
                            pe.wait_ge(vx_done[n], it)
                            for j in range(2):
                                for eh in range(EH):
                                    last = pe.matmul(vp[n][:, j, :], hT[:, s, eh, (2 * n + j) * P:(2 * n + j + 1) * P],
                                                     wv[:, eh, :], start=(eh == 0), stop=(eh == EH - 1))
                            last.then_inc(vp_done[n], 1)

            @block.sync
            def _(sp):
                with sp.Fori(0, NI * 2) as it:
                    for n in range(4):
                        dst = io["s_q"] if n < 2 else io["s_k"]
                        for part, (buf, done, out) in enumerate(((hi, hi_done, hi_out), (lo, lo_done, lo_out))):
                            sp.wait_ge(done[n], it + 1)
                            sp.dma_start(dst[part, bass.ds(it * JT, JT), (n % 2) * P:(n % 2 + 1) * P, :].rearrange("i r t -> r i t"),
                                         buf[:, n, :].rearrange("p (i t) -> p i t", t=P)).then_inc(out[n], 16)
                    for n in range(2):
                        sp.wait_ge(vx_done[n], it + 1)
                        sp.dma_start(io["s_v"][bass.ds(it * JT + 2 * n, 2)].rearrange("i p h d -> p i (h d)"),
                                     vx[:, 2 * n:2 * n + 2, :, :].rearrange("p i h d -> p i (h d)")).then_inc(vx_out[n], 16)
                for n in range(4):
                    sp.wait_ge(hi_out[n], NI * 32)
                    sp.wait_ge(lo_out[n], NI * 32)
                for n in range(2):
                    sp.wait_ge(vx_out[n], NI * 32)


def phase_row_max(nc, io, keep):
    NG = P // G
    with PhaseMemory(nc, "max") as a:
        kA = a.sb("kA", [P, 2, EH, S], F16)
        qn = a.sb("qn", [P, 2, EH, P], F16)
        qe = a.sb("qe", [P, 2, EH, HH * P], F16)
        qbd = a.sb("qbd", [P, 2, EH, NG, HH, G], F16)
        qex = a.sb("qex", [P, 2, NG, H, G], F16)
        mx = a.sb("mx", [P, 2, NG])
        mrow = a.sb("mrow", [NG, 2, P], F16)
        pa = [a.ps(f"pa{i}", [P, S]) for i in range(2)]
        k_in, q_in, qx_done, m_out = (a.sems(n, 2) for n in ("k_in", "q_in", "qx_done", "m_out"))
        pa_full, pa_free = [a.sems(f"pa_full{s}", 2) for s in range(2)], a.sems("pa_free", 2)
        NE = NG // 2 + 1
        NT = NG + 1

        with nc.Block() as block:

            @block.sync
            def _(sp):
                for i in range(NB):
                    with sp.Fori(0, B // 2) as t:
                        for s in range(2):
                            u = t + i * (B // 2)
                            sp.wait_ge(pa_full[s][0], u * NE)
                            for e in range(EH):
                                sp.dma_start(kA[:, s, e, 0:(i + 1) * P].rearrange("p (j t) -> p j t", t=P),
                                             io["s_k"][0, bass.ds(t * (2 * NB) + s * NB, i + 1), e * P:(e + 1) * P, :]
                                             .rearrange("j r t -> r j t")).then_inc(k_in[s], 16)
                            sp.wait_ge(qx_done[s], u)
                            blk = t * (2 * NB) + (s * NB + i)
                            sp.dma_start(qn[:, s], io["s_q"][0, bass.ds(blk, 1)].rearrange("o (e r) t -> r (o e) t", e=EH)).then_inc(q_in[s], 16)
                            for e in range(EH):
                                sp.dma_start(qe[:, s, e, :], io["s_q"][0, bass.ds(blk, 1), e * P:(e + 1) * P, :]
                                             .rearrange("o (d h) t -> (o d) (h t)", d=D).partition_broadcast(G)).then_inc(q_in[s], 16)

            @block.gpsimd
            def _(pool):
                for i in range(NB):
                    with pool.Fori(0, B // 2) as t:
                        for s in range(2):
                            u = t + i * (B // 2)
                            pool.wait_ge(q_in[s], u * 48 + 48)
                            pool.wait_ge(pa_full[s][0], u * NE)
                            for e in range(EH):
                                pool.tensor_tensor(qbd[:, s, e],
                                                   qn[:, s, e, :].rearrange("p (g i) -> p g i", i=G).unsqueeze(2).broadcast_to([P, NG, HH, G]),
                                                   keep["mask_h"][:, :].unsqueeze(1).unsqueeze(3).broadcast_to([P, NG, HH, G]), ALU.mult)
                                last = pool.tensor_tensor(qex[:, s, :, e * HH:(e + 1) * HH, :],
                                                          qe[:, s, e, :].rearrange("p (h g i) -> p g h i", h=HH, i=G),
                                                          keep["mask_i"][:, :].unsqueeze(1).unsqueeze(1).broadcast_to([P, NG, HH, G]), ALU.mult)
                            last.then_inc(qx_done[s], 1)

            @block.tensor
            def _(pe):
                for i in range(NB):
                    with pe.Fori(0, B // 2) as t:
                        for s in range(2):
                            u = t + i * (B // 2)
                            pe.wait_ge(k_in[s], u * 32 + 32)
                            pe.wait_ge(qx_done[s], u + 1)
                            for g in range(NG):
                                n = NT * s + g
                                buf = pa[n % 2]
                                first = i * P + g * G
                                end = first + G
                                pe.wait_ge(pa_free[n % 2], u * NT + n // 2)
                                for c in range(0, end, CH):
                                    for e in range(EH):
                                        pe.matmul(buf[64 * e:64 * e + 64, c:min(c + CH, end)], qbd[:, s, e, g], kA[:, s, e, c:min(c + CH, end)],
                                                  start=True, stop=False, skip_group_check=True)
                                lo = max(0, first - W)
                                while lo < end:
                                    hi = min(end, lo // CH * CH + CH)
                                    pe.matmul(buf[:, lo:hi], qex[:, s, g], keep["table"][:, 0, lo - first + TAB0:hi - first + TAB0],
                                              start=False, stop=False, skip_group_check=True)
                                    lo = hi
                                last = pe.matmul(buf[:, first:end], keep["ident_s"][:, :, :], keep["mask_f"][:, :],
                                                 start=False, stop=True, skip_group_check=True)
                                last.then_inc(pa_full[s][g % 2], 1)
                            n = NT * s + NG
                            for m in (n - 2, n - 1):
                                pe.wait_ge(pa_free[m % 2], u * NT + m // 2 + 1)
                            pe.wait_ge(pa_free[n % 2], u * NT + n // 2)
                            pe.transpose(pa[n % 2][0:NG, 0:P], mx[:, s, :], keep["ident"][:, :]).then_inc(pa_full[s][0], 1)

            @block.vector
            def _(dve):
                for i in range(NB):
                    with dve.Fori(0, B // 2) as t:
                        for s in range(2):
                            u = t + i * (B // 2)
                            for g in range(NG):
                                n = NT * s + g
                                dve.wait_ge(pa_full[s][g % 2], u * (NE, NT - NE)[g % 2] + g // 2 + 1)
                                last = dve.reduce_max(mx[:, s, g:g + 1], pa[n % 2][:, 0:i * P + g * G + G], AX.X)
                                last.then_inc(pa_free[n % 2], 1)
                            n = NT * s + NG
                            dve.wait_ge(pa_full[s][0], u * NE + NE)
                            dve.wait_ge(m_out[s], u * 16)
                            dve.tensor_copy(mrow[:, s, :], pa[n % 2][0:NG, 0:P]).then_inc(pa_free[n % 2], 1)

            @block.scalar
            def _(act):
                for i in range(NB):
                    with act.Fori(0, B // 2) as t:
                        for s in range(2):
                            u = t + i * (B // 2)
                            blk = t * (2 * NB) + (s * NB + i)
                            n = NT * s + NG
                            act.wait_ge(pa_free[n % 2], u * NT + n // 2 + 1)
                            act.dma_start(io["s_m"][bass.ds(blk, 1)].rearrange("o h (g i) -> g (o h) i", i=G),
                                          mrow[:, s, :].rearrange("g (h i) -> g h i", i=G)).then_inc(m_out[s], 16)
                for s in range(2):
                    act.wait_ge(m_out[s], NB * B // 2 * 16)

def phase_far(nc, io, keep):
    NF = NB - FARI
    chunks = ((FARI, 8), (8, 12), (12, 16))
    steps = [(c, j, max(lo, j + NJ), hi) for c, (lo, hi) in enumerate(chunks) for j in range(hi - NJ)]
    NS = len(steps)
    with PhaseMemory(nc, "far") as a:
        kf = a.sb("kf", [KR, 2, NF, 4 * P], F16)
        qf = a.sb("qf", [KR, 2, NF, 4, P], F16)
        vf = a.sb("vf", [P, 2, NF, 4, 2 * D])
        pt = a.sb("pt", [P, 3, 4, CH])
        of = a.sb("of", [P, 2, 4, P])
        ps = [a.ps(f"ps{i}", [P, 2, CH]) for i in range(3)]
        po = [a.ps(f"po{i}", [P, 4, P]) for i in range(2)]
        ones = a.sem("ones")
        in_, unit_done = a.sems("in", 2), a.sems("unit_done", 2)
        s_full, p_full, p_free = (a.sems(n, 3) for n in ("s_full", "p_full", "p_free"))
        po_free, of_out = (a.sems(n, 2) for n in ("po_free", "of_out"))
        NIN = 10 * 16

        with nc.Block() as block:

            @block.sync
            def _(sp):
                with sp.Fori(0, B) as b:
                    with sp.Fori(0, 2) as w:
                        t = b * 2 + w
                        for s in range(2):
                            sp.wait_ge(unit_done[s], t + s)
                            rows = lambda buf, part, j0: (buf[part, bass.ds(b * NB + j0, NF), bass.ds(w * P, P), :]
                                                          .rearrange("j (d h) t -> d j h t", h=HH)[:, :, 4 * s:4 * s + 4, :]
                                                          .rearrange("d j h t -> d j (h t)"))
                            for r, part in enumerate((0, 1, 0, 1)):
                                sp.dma_start(kf[r * D:(r + 1) * D, s], rows(io["s_k"], part, 0)).then_inc(in_[s], 16)
                            for r, part in enumerate((0, 0, 1, 1)):
                                sp.dma_start(qf[r * D:(r + 1) * D, s].rearrange("d i h t -> d i (h t)"),
                                             rows(io["s_q"], part, FARI)).then_inc(in_[s], 16)
                            sp.dma_start(qf[4 * D:KR, s].rearrange("d i h t -> d i (h t)"),
                                         io["s_m"][bass.ds(b * NB + FARI, NF), bass.ds(w * HH + 4 * s, 4), :]
                                         .rearrange("i h t -> i (h t)").unsqueeze(0)).then_inc(in_[s], 16)
                            sp.dma_start(vf[:, s].rearrange("p j h d -> p j (h d)"),
                                         io["s_v"][bass.ds(b * NB, NF), :, bass.ds(w * HH + 4 * s, 4), :]
                                         .rearrange("j p h d -> p j (h d)")).then_inc(in_[s], 16)

            @block.tensor
            def _(pe):
                pe.wait_ge(ones, 1)
                with pe.Fori(0, B * 2) as t:
                    for s in range(2):
                        v = t * 2 + s
                        pe.wait_ge(in_[s], t * NIN + NIN)

                        def pv(k):
                            c, j, lo, hi = steps[k]
                            c0, chi = chunks[c]
                            buf, uses = (3 * s + c) % 2, t * 3 + (3 * s + c) // 2
                            if j == 0:
                                pe.wait_ge(po_free[buf], uses)
                            pe.wait_ge(p_full[k % 3], (v * (NS // 3) + k // 3) * 2 + 2)
                            for h in range(4):
                                last = pe.matmul(po[buf][32 * h:32 * h + 32, lo - c0:hi - c0, :], vf[:, s, j, h, :],
                                                 pt[:, k % 3, h, 0:(hi - lo) * P],
                                                 start=(j == 0), stop=(j == chi - NJ - 1), skip_group_check=True)
                            last.then_inc(p_free[k % 3], 1)

                        for k, (c, j, lo, hi) in enumerate(steps):
                            for r in range(2):
                                n = 2 * k + r
                                if n < 3:
                                    pe.wait_ge(p_full[(NS - 2 + (n + 1) // 2) % 3 if n < 2 else (NS - 1) % 3], v * (2 * NS // 3))
                                else:
                                    m = n - 3
                                    pe.wait_ge(p_full[m // 2 % 3], (v * (NS // 3) + m // 6) * 2 + m % 2 + 1)
                                for h in range(2):
                                    last = pe.matmul(ps[n % 3][:, h, 0:(hi - lo) * P], kf[:, s, j, (2 * r + h) * P:(2 * r + h + 1) * P],
                                                     qf[:, s, lo - FARI:hi - FARI, 2 * r + h, :], start=True, stop=True)
                                    if n == h == 0:
                                        last.then_inc(unit_done[1 - s], 1)
                                last.then_inc(s_full[n % 3], 1)
                            if k:
                                pv(k - 1)
                        pv(NS - 1)

            @block.scalar
            def _(act):
                with act.Fori(0, B * 2) as t:
                    for s in range(2):
                        v = t * 2 + s
                        for k, (c, j, lo, hi) in enumerate(steps):
                            act.wait_ge(p_free[k % 3], v * (NS // 3) + k // 3)
                            for r in range(2):
                                n = 2 * k + r
                                act.wait_ge(s_full[n % 3], v * (2 * NS // 3) + n // 3 + 1)
                                act.activation(pt[:, k % 3, 2 * r:2 * r + 2, 0:(hi - lo) * P], ps[n % 3][:, :, 0:(hi - lo) * P],
                                               ACT.Exp, scale=SCALE).then_inc(p_full[k % 3], 1)

            @block.vector
            def _(dve):
                dve.memset(kf[4 * D:KR, :, :, :], -1.0).then_inc(ones, 1)
                with dve.Fori(0, B * 2) as t:
                    for s in range(2):
                        for c, (lo, hi) in enumerate(chunks):
                            buf, uses = (3 * s + c) % 2, t * 3 + (3 * s + c) // 2
                            k = max(k for k in range(NS) if steps[k][0] == c)
                            dve.wait_ge(p_free[k % 3], (t * 2 + s) * (NS // 3) + k // 3 + 1)
                            dve.wait_ge(of_out[buf], uses * 16)
                            dve.tensor_copy(of[:, buf, 0:hi - lo, :], po[buf][:, 0:hi - lo, :]).then_inc(po_free[buf], 1)

            @block.gpsimd
            def _(pool):
                with pool.Fori(0, B) as b:
                    with pool.Fori(0, 2) as w:
                        t = b * 2 + w
                        for s in range(2):
                            for c, (lo, hi) in enumerate(chunks):
                                buf, uses = (3 * s + c) % 2, t * 3 + (3 * s + c) // 2
                                pool.wait_ge(po_free[buf], uses + 1)
                                pool.dma_start(io["s_of"][bass.ds(b * NB + lo, hi - lo), bass.ds(w * 2 + s, 1), :, :]
                                               .rearrange("i o r t -> r (i o) t"),
                                               of[:, buf, 0:hi - lo, :]).then_inc(of_out[buf], 16)
                for buf in range(2):
                    pool.wait_ge(of_out[buf], B * 2 * 3 * 16)


def phase_near(nc, io, keep):
    NG = P // G
    with PhaseMemory(nc, "near") as a:
        kn = a.sb("kn", [KR, 4, NJ, HH * P], F16)
        vn = a.sb("vn", [P, 4, NJ, HH, 2 * D])
        qs = a.sb("qs", [KR, 4, HH, P], F16)
        qe = a.sb("qe", [P, 4, 2, HH, P], F16)
        qx = a.sb("qx", [P, 4, 2, NG, HH, G], F16)
        pt = a.sb("pt", [P, 2, HH, P])
        fo = a.sb("fo", [P, 4, 2, P])
        on = a.sb("on", [P, 2, 2, P])
        ps = [a.ps(f"ps{i}", [P, 2, HH, P // 2]) for i in range(2)]
        po = [a.ps(f"po{i}", [P, 2, P]) for i in range(2)]
        ones = a.sem("ones")
        k_in, q_in, f_in, qx_done, unit_done = (a.sems(n, 4) for n in ("k_in", "q_in", "f_in", "qx_done", "unit_done"))
        on_done, on_out = (a.sems(n, 2) for n in ("on_done", "on_out"))
        s_full, p_full, p_free = (a.sems(n, 2) for n in ("s_full", "p_full", "p_free"))
        NIN = 8 * 16

        def levels(eng, body):
            for i in range(FARI):
                with eng.Fori(0, B // 2) as c:
                    nj = i + 1
                    body(c, i, nj, False, c + i * (B // 2), c * (2 * nj) + B * i * (i + 1) // 2)
            with eng.Fori(0, B // 2) as c:
                with eng.Fori(0, NB - FARI) as r:
                    u = c * (NB - FARI) + r
                    body(c, r + FARI, NJ, True, u + FARI * (B // 2), u * (2 * NJ) + B * FARI * (FARI + 1) // 2)

        block_of = lambda c, i, v: c * (2 * NB) + i + v // 2 * NB
        even_use = lambda u, v: u * 2 + v // 2

        with nc.Block() as block:

            @block.sync
            def _(sp):
                def body(c, i, nj, far, u, k):
                    for v in range(4):
                        blk, s = block_of(c, i, v), v % 2
                        sp.wait_ge(qx_done[v], u)
                        for part in range(2):
                            sp.dma_start(qe[:, v, part].rearrange("r h t -> r (h t)"),
                                         io["s_q"][part, bass.ds(blk, 1), s * P:(s + 1) * P, :]
                                         .rearrange("o (d h) t -> (o d) (h t)", h=HH).partition_broadcast(G)).then_inc(q_in[v], 16)
                        sp.wait_ge(unit_done[v], u + v // 3)
                        for r, part in enumerate((0, 1, 0, 1)):
                            sp.dma_start(kn[r * D:(r + 1) * D, v, 0:nj, :],
                                         io["s_k"][part, bass.ds(blk - (nj - 1), nj), s * P:(s + 1) * P, :]
                                         .rearrange("j (d h) t -> d j (h t)", h=HH)).then_inc(k_in[v], 16)
                        for r, part in enumerate((0, 1)):
                            sp.dma_start(qs[r * 2 * D:(r + 1) * 2 * D, v].rearrange("r h t -> r (h t)"),
                                         io["s_q"][part, bass.ds(blk, 1), s * P:(s + 1) * P, :]
                                         .rearrange("o (d h) t -> (o d) (h t)", h=HH).partition_broadcast(2)).then_inc(k_in[v], 16)
                        sp.dma_start(qs[4 * D:KR, v].rearrange("r h t -> r (h t)"),
                                     io["s_m"][bass.ds(blk, 1), s * HH:(s + 1) * HH, :].rearrange("o h t -> o (h t)")).then_inc(k_in[v], 16)
                        sp.dma_start(vn[:, v, 0:nj].rearrange("p j h d -> p j (h d)"),
                                     io["s_v"][bass.ds(blk - (nj - 1), nj), :, s * HH:(s + 1) * HH, :]
                                     .rearrange("j p h d -> p j (h d)")).then_inc(k_in[v], 16)
                        if far:
                            sp.wait_ge(on_done[s], even_use(u, v) - 1)
                            sp.dma_start(fo[:, v], io["s_of"][bass.ds(blk, 1), 2 * s:2 * s + 2, :, :]
                                         .rearrange("o c r t -> r (o c) t")).then_inc(f_in[v], 16)
                levels(sp, body)

            @block.gpsimd
            def _(pool):
                def body(c, i, nj, far, u, k):
                    for v in range(4):
                        pool.wait_ge(q_in[v], u * 32 + 32)
                        pool.wait_ge(unit_done[v], u + v // 3)
                        for part in range(2):
                            last = pool.tensor_tensor(qx[:, v, part], qe[:, v, part].rearrange("p h (g i) -> p g h i", i=G),
                                                      keep["mask_i"][:, :].unsqueeze(1).unsqueeze(1).broadcast_to([P, NG, HH, G]), ALU.mult)
                        last.then_inc(qx_done[v], 1)
                levels(pool, body)

            @block.vector
            def _(dve):
                dve.memset(kn[4 * D:KR, :, :, :], -1.0).then_inc(ones, 1)

                def body(c, i, nj, far, u, k):
                    for v in range(4):
                        n, s = nj * v + nj - 1, v % 2
                        dve.wait_ge(p_free[n % 2], k + n // 2 + 1)
                        dve.wait_ge(on_out[s], even_use(u, v) * 16)
                        if far:
                            dve.wait_ge(f_in[v], (u - FARI * (B // 2)) * 16 + 16)
                            dve.tensor_tensor(on[:, s], po[s][:, :, :], fo[:, v], ALU.add).then_inc(on_done[s], 1)
                        else:
                            dve.tensor_copy(on[:, s], po[s][:, :, :]).then_inc(on_done[s], 1)
                levels(dve, body)

            @block.scalar
            def _(act):
                def body(c, i, nj, far, u, k):
                    def store(v):
                        s = v % 2
                        act.wait_ge(on_done[s], even_use(u, v) + 1)
                        act.dma_start(io["s_o"][bass.ds(block_of(c, i, v), 1), 2 * s:2 * s + 2, :, :]
                                      .rearrange("o c r t -> r (o c) t"), on[:, s]).then_inc(on_out[s], 16)
                    for v in range(4):
                        for j in range(nj):
                            n = nj * v + j
                            act.wait_ge(p_free[n % 2], k + n // 2)
                            act.wait_ge(s_full[n % 2], k + n // 2 + 1)
                            act.activation(pt[:, n % 2].rearrange("p h (x t) -> p x h t", x=2), ps[n % 2][:, :, :, :],
                                           ACT.Exp, scale=SCALE).then_inc(p_full[n % 2], 1)
                        if v:
                            store(v - 1)
                    store(3)
                levels(act, body)
                for s in range(2):
                    act.wait_ge(on_out[s], NB * B * 16)

            @block.tensor
            def _(pe):
                pe.wait_ge(ones, 1)

                def body(c, i, nj, far, u, k):
                    steps = [(v, j) for v in range(4) for j in range(nj)]

                    def pv(n):
                        v, j = steps[n]
                        s = v % 2
                        if j == 0:
                            pe.wait_ge(on_done[s], even_use(u, v))
                        pe.wait_ge(p_full[n % 2], k + n // 2 + 1)
                        for h in range(HH):
                            last = pe.matmul(po[s][32 * (h % 4):32 * (h % 4) + 32, h // 4, :], vn[:, v, nj - 1 - j, h, :],
                                             pt[:, n % 2, h, :], start=(j == 0 and h < 4), stop=(j == nj - 1 and h >= 4),
                                             skip_group_check=True)
                            if j == h == 0:
                                last.then_inc(unit_done[(v - 1) % 4], 1)
                        last.then_inc(p_free[n % 2], 1)

                    for n, (v, j) in enumerate(steps):
                        if j == 0:
                            pe.wait_ge(k_in[v], u * NIN + NIN)
                            pe.wait_ge(qx_done[v], u + 1)
                        pe.wait_ge(p_full[n % 2], k + n // 2)
                        for x in range(2):
                            bank = ps[n % 2][:, x]
                            for h in range(HH):
                                pe.matmul(bank[:, h, :], kn[:, v, nj - 1 - j, h * P:(h + 1) * P], qs[:, v, h, x * 64:x * 64 + 64],
                                          start=(h == 0), stop=False, skip_group_check=True)
                            if j == 0:
                                pe.matmul(bank[:, :, :], keep["ident_m"][:, :],
                                          keep["mask_n"][:, x * 64:x * 64 + 64].unsqueeze(1).broadcast_to([P, HH, 64]),
                                          start=False, stop=False, skip_group_check=True)
                            for g in range(NG // 2):
                                y = TAB0 - j * P - (x * 64 + g * G)
                                out = bank[:, :, g * G:g * G + G]
                                for part, qpart in ((0, 0), (0, 1), (1, 0)):
                                    last = pe.matmul(out, keep["table"][:, part, y:y + P], qx[:, v, qpart, x * (NG // 2) + g],
                                                     start=False, stop=(g == NG // 2 - 1 and part == 1), skip_group_check=True)
                        last.then_inc(s_full[n % 2], 1)
                        if nj == 1:
                            pv(n)
                        elif n:
                            pv(n - 1)
                    if nj > 1:
                        pv(len(steps) - 1)
                levels(pe, body)


def phase_ffn(nc, io, keep):
    JT = CH // P
    NK = B * CPB
    with PhaseMemory(nc, "ffn") as a:
        wo = a.sb("wo", [P, 4, E])
        gw = a.sb("gw", [P, EH, NX])
        gbias = a.sb("gbias", [P, NX])
        b3 = a.sb("b3", [NX, E])
        bo = a.sb("bo", [P, E])
        gbo = a.sb("gbo", [P, B, E])
        w_f = a.sb("w_f", [P, 2, 3, EH, E])
        w_s = a.sb("w_s", [P, 2, NX, 3, EH, E], F16)
        b1, b2 = (a.sb(n, [P, NX, EH]) for n in ("b1", "b2"))
        gbo_now, gb_now = a.sb("gbo_now", [P, 1, E]), a.sb("gb_now", [P, 1, E])
        mod_now = a.sb("mod_now", [P, 2, EH])
        x = a.sb("x", [P, 2, JT, E])
        heads = a.sb("heads", [P, 2, JT * 4, P])
        rec = a.sb("rec", [P, 2, 4, P])
        nrm = a.sb("nrm", [P, JT, 4, P])
        att = a.sb("att", [P, 2, 2, E])
        x1 = a.sb("x1", [P, JT, E])
        xn = a.sb("xn", [P, JT, E])
        stats, mv = a.sb("stats", [P, JT, 6]), a.sb("mv", [P, JT, 2])
        tick = a.sb("tick", [P, 1])
        ve, sd, r1, r2, rstd = (a.sb(n, [P, JT]) for n in ("ve", "sd", "r1", "r2", "rstd"))
        lg, sh, ex, pr, o1, o2, g1, g2 = (a.sb(n, [P, JT, NX]) for n in ("lg", "sh", "ex", "pr", "o1", "o2", "g1", "g2"))
        top, topf = a.sb("top", [P, JT, 8]), a.sb("topf", [P, JT, 8])
        topi = a.sb("topi", [P, JT, 8], U32)
        mxs, sums, rsum = (a.sb(n, [P, JT]) for n in ("mxs", "sums", "rsum"))
        cwT = a.sb("cwT", [NX, CH])
        wb = a.sb("wb", [P, 2, 2, E])
        hT = a.sb("hT", [P, 2, EH, CH])
        cw = a.sb("cw", [P, 2, JT, NX])
        base = a.sb("base", [P, 2, JT, E])
        hT_s = a.sb("hT_s", [P, 2, 2, EH, CH], F16)
        h1_f, h2_f = a.sb("h1_f", [P, EH, CH]), a.sb("h2_f", [P, EH, CH])
        h1_s, h2_s = (a.sb(n, [P, 2, 2, EH, CH], F16) for n in ("h1_s", "h2_s"))
        y = a.sb("y", [P, 2, JT, E])
        p1 = [a.ps(f"p1{i}", [P, CH]) for i in range(EH)]
        p2 = [a.ps(f"p2{i}", [P, CH]) for i in range(EH)]
        p3 = [a.ps(f"p3{i}", [P, 2, E]) for i in range(2)]
        px = [a.ps(f"px{i}", [P, CH]) for i in range(2)]
        halves = lambda bank: bank[:, :].rearrange("p (j e) -> p j e", e=E)

        zeroed, weights, once, gbo_set, gb_set, mod_set = (
            a.sem(n) for n in ("zeroed", "weights", "once", "gbo_set", "gb_set", "mod_set"))
        w_in, w_hi, w_split = a.sems("w_in", 2), a.sem("w_hi"), a.sem("w_split")
        hT_split, h1_split, h2_split = a.sem("hT_split"), a.sems("h1_split", 2), a.sems("h2_split", 2)
        x_in, heads_in, out_done, out_sent = (a.sems(n, 2) for n in ("x_in", "heads_in", "out_done", "out_sent"))
        den_full, rec_done, nrm_done, wo_full, att_done, bp_full, wb_done, base_done = (
            a.sems(n, 2) for n in ("den_full", "rec_done", "nrm_done", "wo_full", "att_done", "bp_full", "wb_done", "base_done"))
        xb_done, x1_done, ln_step, var_done, sd_done, xn_done, tp_done, hT_done = (
            a.sem(n) for n in ("xb_done", "x1_done", "ln_step", "var_done", "sd_done", "xn_done", "tp_done", "hT_done"))
        lg_full, route_step, sh_done, ex_done, cw_done, cp_full, cwT_done = (
            a.sem(n) for n in ("lg_full", "route_step", "sh_done", "ex_done", "cw_done", "cp_full", "cwT_done"))
        p1_full, h1_done, p2_full, h2_done, p3_full, p3_free = (
            a.sems(n, 2) for n in ("p1_full", "h1_done", "p2_full", "h2_done", "p3_full", "p3_free"))
        NW = 9 * 16
        LN, RS = 6, 11
        NS = CPB * NX
        LAG = 2

        def order(eng, piece=None, step=None, piece_first=False):
            if piece:
                for n in range(NX):
                    piece(0, 0, 0, n)

            def batch(b, last):
                for k in range(NS + LAG):
                    prepare = piece and k < NS and not (last and k >= NS - NX)
                    nb, nc_ = (b, k // NX + 1) if k // NX + 1 < CPB else (b + 1, 0)
                    if prepare and piece_first:
                        piece(nb, nc_, b * CPB + k // NX + 1, k % NX)
                    if step:
                        step(b, k)
                    if prepare and not piece_first:
                        piece(nb, nc_, b * CPB + k // NX + 1, k % NX)
            with eng.Fori(0, B - 1) as b:
                batch(b, False)
            batch(B - 1, True)

        with nc.Block() as block:

            @block.sync
            def _(sp):
                sp.wait_ge(zeroed, 1)
                for q in range(4):
                    sp.dma_start(wo[32 * q:32 * q + D, :, :], io["wo"].rearrange("(g q d) n -> q d g n", q=4, d=D)[q]).then_inc(weights, 16)
                sp.dma_start(bo[:, :], io["bo"].partition_broadcast(P)).then_inc(weights, 16)
                sp.dma_start(gbias[:, :], io["gate_b"].partition_broadcast(P)).then_inc(weights, 16)
                sp.dma_start(b3[:, :], io["b3"]).then_inc(weights, 16)
                for eh in range(EH):
                    sp.dma_start(gw[:, eh, :], io["gwT"][eh * P:(eh + 1) * P, :]).then_inc(weights, 16)
                xv = io["x"].rearrange("b (c j p) e -> (b c) p j e", j=JT, p=P)

                def load(u, s):
                    it = u * 2 + s
                    sp.dma_start(x[:, s], xv[bass.ds(it, 1)].rearrange("o p j e -> p (o j) e")).then_inc(x_in[s], 16)
                    for j in range(JT):
                        sp.dma_start(heads[:, s, 4 * j:4 * j + 4], io["s_o"][bass.ds(it * JT + j, 1)].rearrange("i o r t -> r (i o) t")).then_inc(heads_in[s], 16)
                load(0, 0)
                load(0, 1)
                for e in range(NX):
                    if e >= 2:
                        sp.wait_ge(w_split, e - 1)
                    for i, name in enumerate(("w1", "w2", "w3")):
                        sp.dma_start(w_f[:, e % 2, i], io[name][e].rearrange("(k p) n -> p k n", p=P)).then_inc(w_in[e % 2], 16)
                    for w, name in ((b1, "b1"), (b2, "b2")):
                        sp.dma_start(w[:, e, :], io[name][e]).then_inc(w_in[e % 2], 16)
                with sp.Fori(0, NK // 2 - 1) as u:
                    for s in range(2):
                        sp.wait_ge(x1_done, u * 2 + (s + 1))
                        load(u + 1, s)

            @block.gpsimd
            def _(pool):
                pool.memset(wo[:, :, :], 0.0).then_inc(zeroed, 1)
                pool.wait_ge(once, 1)

                def piece(b, c, it, n):
                    s = c % 2
                    if n == 0:
                        if c == 0:
                            pool.tensor_copy(gbo_now[:, :, :], gbo[:, bass.ds(b, 1), :]).then_inc(gbo_set, 1)
                            pool.wait_ge(gbo_set, b + 1)
                        pool.wait_ge(x_in[s], (b * (CPB // 2) + c // 2) * 16 + 16)
                        pool.tensor_tensor(x[:, s], x[:, s], gbo_now[:, :, :].broadcast_to([P, JT, E]), ALU.add).then_inc(xb_done, 1)
                    if n == 7:
                        pool.wait_ge(out_sent[s], (b * (CPB // 2) + c // 2) * 16)
                        for m in range(2):
                            pool.wait_ge(wb_done[m], it + 1)
                            pool.tensor_tensor(base[:, s, 2 * m:2 * m + 2, :], wb[:, m], x1[:, 2 * m:2 * m + 2, :], ALU.add).then_inc(base_done[m], 1)

                def step(b, k):
                    if k < NS:
                        pool.wait_ge(p2_full[EH - 1], b * NS + max(k - 1, 0))
                        for eh in range(EH):
                            pool.wait_ge(h1_done[eh], b * NS + k + 1)
                            pool.tensor_tensor(h1_s[:, k % 2, 1, eh, :], h1_f[:, eh, :], h1_s[:, k % 2, 0, eh, :], ALU.subtract).then_inc(h1_split[eh], 1)
                    if k % NX != LAG - 1 or k < NX:
                        return
                    c = k // NX - 1
                    s, it, u = c % 2, b * CPB + c, b * (CPB // 2) + c // 2
                    if c == 0:
                        pool.tensor_copy(gb_now[:, :, :], keep["gates"][:, 1, bass.ds(b, 1), :]).then_inc(gb_set, 1)
                        pool.wait_ge(gb_set, b + 1)
                    for m in range(2):
                        pool.wait_ge(p3_free[m], it * NX + NX)
                    pool.tensor_tensor(y[:, s], y[:, s], gb_now[:, :, :].broadcast_to([P, JT, E]), ALU.mult).then_inc(out_done[s], 1)
                    pool.wait_ge(out_done[s], u * 2 + 1)
                    for m in range(2):
                        pool.wait_ge(base_done[m], it + 1)
                    pool.tensor_tensor(base[:, s], y[:, s], base[:, s], ALU.add).then_inc(out_done[s], 1)
                    pool.wait_ge(out_done[s], u * 2 + 2)
                    pool.dma_start(io["out"][bass.ds(b, 1), c * CH:(c + 1) * CH, :]
                                   .rearrange("o (j p) e -> p (o j) e", p=P), base[:, s]).then_inc(out_sent[s], 16)
                order(pool, piece, step, piece_first=True)
                for s in range(2):
                    pool.wait_ge(out_sent[s], NK // 2 * 16)

            @block.vector
            def _(dve):
                dve.wait_ge(weights, NW)
                dve.tensor_tensor(gbo[:, :, :], keep["gates"][:, 0, :, :], bo[:, :].unsqueeze(1).broadcast_to([P, B, E]), ALU.mult).then_inc(once, 1)
                for e in range(NX):
                    dve.wait_ge(w_hi, e + 1)
                    dve.tensor_tensor(w_s[:, 1, e], w_f[:, e % 2], w_s[:, 0, e], ALU.subtract).then_inc(w_split, 1)
                wide = lambda t: t.unsqueeze(2).broadcast_to([P, JT, NX])
                gate = lambda kind, b: keep["gates"][:, kind, bass.ds(b, 1), :].broadcast_to([P, 2, E])

                def normalise_heads(b, c, it, half):
                    s, u = c % 2, b * (CPB // 2) + c // 2
                    for n in range(2):
                        dve.wait_ge(den_full[n], it * 2 + half + 1)
                        dve.reciprocal(rec[:, n], px[n][:, :].rearrange("p (g t) -> p g t", t=P)).then_inc(rec_done[n], 1)
                    if half == 0:
                        dve.wait_ge(wo_full[1], it)
                    for n in range(2):
                        j = 2 * half + n
                        dve.wait_ge(rec_done[n], it * 2 + half + 1)
                        dve.tensor_tensor(nrm[:, j], heads[:, s, 4 * j:4 * j + 4, :], rec[:, n], ALU.mult).then_inc(nrm_done[n], 1)

                def residual_and_norm(b, c, it):
                    s = c % 2
                    for m in range(2):
                        dve.wait_ge(wo_full[m], it + 1)
                        dve.tensor_tensor(att[:, m], halves(px[m]), gate(0, b), ALU.mult).then_inc(att_done[m], 1)
                    dve.wait_ge(xb_done, it + 1)
                    for m in range(2):
                        dve.wait_ge(att_done[m], it + 1)
                        dve.wait_ge(base_done[m], it)
                        last = dve.tensor_tensor(x1[:, 2 * m:2 * m + 2, :], att[:, m], x[:, s, 2 * m:2 * m + 2, :], ALU.add)
                    last.then_inc(x1_done, 1)
                    dve.wait_ge(x1_done, it + 1)
                    dve.memset(tick[:, :], 0.0)
                    for j in range(JT):
                        last = dve.bn_stats(stats[:, j, :], x1[:, j, :])
                    last.then_inc(ln_step, 1)
                    dve.wait_ge(ln_step, it * LN + 1)
                    dve.memset(tick[:, :], 0.0)
                    for j in range(JT):
                        last = dve.bn_aggr(mv[:, j, :], stats[:, j, :])
                    last.then_inc(ln_step, 1)
                    dve.wait_ge(ln_step, it * LN + 2)
                    dve.tensor_scalar(ve[:, :], mv[:, :, 1], EPS, None, ALU.add).then_inc(var_done, 1)
                    dve.wait_ge(sd_done, it + 1)
                    inverse_root(dve, rstd[:, :], sd[:, :], ve[:, :], r1[:, :], r2[:, :], ln_step, it * LN + 2)
                    for j in range(JT):
                        last = dve.tensor_scalar(xn[:, j, :], x1[:, j, :], mv[:, j, 0:1], rstd[:, j:j + 1],
                                                 ALU.subtract, ALU.mult)
                    last.then_inc(xn_done, 1)

                def route(b, c, it):
                    n = [0]

                    def link(ins):
                        n[0] += 1
                        ins.then_inc(route_step, 1)
                        dve.wait_ge(route_step, it * RS + n[0])
                    dve.wait_ge(lg_full, it + 1)
                    link(dve.tensor_tensor(lg[:, :, :], px[0][:, 0:JT * NX].rearrange("p (j n) -> p j n", n=NX),
                                           gbias[:, :].unsqueeze(1).broadcast_to([P, JT, NX]), ALU.add))
                    link(dve.reduce_max(mxs[:, :], lg[:, :, :], AX.X))
                    dve.tensor_tensor(sh[:, :, :], lg[:, :, :], wide(mxs[:, :]), ALU.subtract).then_inc(sh_done, 1)
                    dve.wait_ge(ex_done, it + 1)
                    link(dve.reduce_sum(sums[:, :], ex[:, :, :], AX.X))
                    link(dve.reciprocal(rsum[:, :], sums[:, :]))
                    link(dve.tensor_tensor(pr[:, :, :], ex[:, :, :], wide(rsum[:, :]), ALU.mult))
                    dve.memset(tick[:, :], 0.0)
                    for j in range(JT):
                        last = dve.max(out=top[:, j, :], in_=pr[:, j, :])
                    link(last)
                    dve.memset(tick[:, :], 0.0)
                    for j in range(JT):
                        last = dve.max_index(out=topi[:, j, :], in_max=top[:, j, :], in_values=pr[:, j, :])
                    link(last)
                    link(dve.tensor_copy(topf[:, :, :], topi[:, :, :]))
                    iota = keep["iota8"][:, :].unsqueeze(1).broadcast_to([P, JT, NX])
                    dve.tensor_tensor(o1[:, :, :], iota, wide(topf[:, :, 0]), ALU.is_equal)
                    link(dve.tensor_tensor(o2[:, :, :], iota, wide(topf[:, :, 1]), ALU.is_equal))
                    dve.tensor_tensor(g1[:, :, :], o1[:, :, :], wide(pr[:, :, 0]), ALU.mult)
                    link(dve.tensor_tensor(g2[:, :, :], o2[:, :, :], wide(pr[:, :, 1]), ALU.mult))
                    dve.tensor_tensor(cw[:, c % 2], g1[:, :, :], g2[:, :, :], ALU.add).then_inc(cw_done, 1)
                    link(dve.memset(tick[:, :], 0.0))
                    assert n[0] == RS

                def piece(b, c, it, n):
                    if n in (1, 2):
                        normalise_heads(b, c, it, n - 1)
                    if n == 3:
                        residual_and_norm(b, c, it)
                    if n == 5:
                        route(b, c, it)
                    if n == 5:
                        dve.wait_ge(hT_done, it + 1)
                        dve.tensor_tensor(hT_s[:, c % 2, 1], hT[:, c % 2], hT_s[:, c % 2, 0], ALU.subtract).then_inc(hT_split, 1)
                    if n == 7:
                        for m in range(2):
                            dve.wait_ge(bp_full[m], it + 1)
                            dve.wait_ge(base_done[m], it)
                            dve.tensor_tensor(wb[:, m], halves(px[m]), gate(1, b), ALU.mult).then_inc(wb_done[m], 1)

                def step(b, k):
                    if 1 <= k <= NS:
                        dve.wait_ge(p3_full[1], b * NS + max(k - LAG, 0))
                        n = k - 1
                        for eh in range(EH):
                            dve.wait_ge(h2_done[eh], b * NS + n + 1)
                            dve.tensor_tensor(h2_s[:, n % 2, 1, eh, :], h2_f[:, eh, :], h2_s[:, n % 2, 0, eh, :], ALU.subtract).then_inc(h2_split[eh], 1)
                    k -= LAG
                    if k < 0:
                        return
                    c, e = k // NX, k % NX
                    s, g = c % 2, b * NS + k
                    if e == 0:
                        dve.wait_ge(out_done[s], (b * (CPB // 2) + c // 2) * 2)
                        dve.wait_ge(cw_done, b * CPB + c + 1)
                    for m in range(2):
                        if e:
                            dve.wait_ge(p3_free[m], g)
                        dve.wait_ge(p3_full[m], g + 1)
                        for j in (2 * m, 2 * m + 1):
                            w = cw[:, s, j, e:e + 1]
                            if e == 0:
                                last = dve.tensor_scalar(y[:, s, j, :], p3[m][:, j % 2, :], w, None, ALU.mult)
                            else:
                                last = dve.scalar_tensor_tensor(out=y[:, s, j, :], in0=p3[m][:, j % 2, :], scalar=w,
                                                                in1=y[:, s, j, :], op0=ALU.mult, op1=ALU.add)
                        last.then_inc(p3_free[m], 1)
                order(dve, piece, step, piece_first=True)

            @block.scalar
            def _(act):
                for e in range(NX):
                    act.wait_ge(w_in[e % 2], (e // 2 + 1) * 5 * 16)
                    act.activation(w_s[:, 0, e], w_f[:, e % 2], ACT.Copy).then_inc(w_hi, 1)

                def relu(hi, whole, src, bias, full, split, done, b, k):
                    for eh in range(EH):
                        act.wait_ge(full[eh], b * NS + k + 1)
                        act.activation(hi[:, k % 2, 0, eh, :], src[eh][:, :], ACT.Relu, bias=bias[:, k % NX, eh:eh + 1])
                        act.wait_ge(split[eh], b * NS + k)
                        act.activation(whole[:, eh, :], src[eh][:, :], ACT.Relu,
                                       bias=bias[:, k % NX, eh:eh + 1]).then_inc(done[eh], 1)

                def piece(b, c, it, n):
                    if n == 3:
                        if c == 0:
                            for k, name in enumerate(("shift_b", "scale_b")):
                                act.activation(mod_now[:, k, :].unsqueeze(2), keep[name][:, :, bass.ds(b, 1)], ACT.Copy).then_inc(mod_set, 1)
                            act.wait_ge(mod_set, b * 2 + 2)
                        act.wait_ge(var_done, it + 1)
                        act.activation(sd[:, :], ve[:, :], ACT.Sqrt).then_inc(sd_done, 1)
                    if n == 4:
                        act.wait_ge(lg_full, it)
                        act.wait_ge(tp_done, it + 1)
                        for dst in (hT_s[:, c % 2, 0], hT[:, c % 2]):
                            for eh in range(EH):
                                last = act.activation(dst[:, eh, :], px[eh][:, :], ACT.Identity, bias=mod_now[:, 0, eh:eh + 1],
                                                      scale=mod_now[:, 1, eh:eh + 1])
                        last.then_inc(hT_done, 1)
                    if n == 5:
                        act.wait_ge(sh_done, it + 1)
                        act.activation(ex[:, :, :], sh[:, :, :], ACT.Exp).then_inc(ex_done, 1)
                    if n == 6:
                        act.wait_ge(cp_full, it + 1)
                        act.activation(cwT[:, :], px[1][0:NX, :], ACT.Copy).then_inc(cwT_done, 1)

                def step(b, k):
                    if k < NS:
                        act.wait_ge(p2_full[EH - 1], b * NS + max(k - 1, 0))
                        relu(h1_s, h1_f, p1, b1, p1_full, h1_split, h1_done, b, k)
                    if 1 <= k <= NS:
                        act.wait_ge(p3_full[1], b * NS + max(k - LAG, 0))
                        relu(h2_s, h2_f, p2, b2, p2_full, h2_split, h2_done, b, k - 1)
                order(act, piece, step, piece_first=True)

            @block.tensor
            def _(pe):
                pe.wait_ge(weights, NW)

                PARTS = ((0, 0), (0, 1), (1, 0))

                def layer(b, k, i, src, dst, full, free):
                    for eh in range(EH):
                        pe.wait_ge(free[eh], b * NS + k)
                        for n, (pw, px_) in enumerate(PARTS):
                            for ki in range(EH):
                                last = pe.matmul(dst[eh][:, :], w_s[:, pw, k % NX, i, ki, eh * P:(eh + 1) * P], src[:, px_, ki, :],
                                                 start=(n == ki == 0), stop=(n == 2 and ki == EH - 1))
                        last.then_inc(full[eh], 1)

                def step(b, k):
                    if k < NS:
                        if k % NX == 0:
                            pe.wait_ge(hT_split, b * CPB + k // NX + 1)
                        layer(b, k, 0, hT_s[:, k // NX % 2], p1, p1_full, h1_done)
                    if 1 <= k <= NS:
                        for eh in range(EH):
                            pe.wait_ge(h1_split[eh], b * NS + k)
                        layer(b, k - 1, 1, h1_s[:, (k - 1) % 2], p2, p2_full, h2_done)
                    if k >= LAG:
                        k -= LAG
                        for eh in range(EH):
                            pe.wait_ge(h2_split[eh], b * NS + k + 1)
                        for m in range(2):
                            pe.wait_ge(p3_free[m], b * NS + k)
                            for j in range(2):
                                for n, (ph, pw) in enumerate(PARTS):
                                    for ki in range(EH):
                                        last = pe.matmul(p3[m][:, j, :], h2_s[:, k % 2, ph, ki, (2 * m + j) * P:(2 * m + j + 1) * P],
                                                         w_s[:, pw, k % NX, 2, ki, :], start=(n == ki == 0), stop=(n == 2 and ki == EH - 1))
                            last.then_inc(p3_full[m], 1)

                def piece(b, c, it, n):
                    s = c % 2
                    if n in (0, 1):
                        if n == 0:
                            pe.wait_ge(heads_in[s], ((b * (CPB // 2) + c // 2) * 16 + 16) * JT)
                        for i in range(2):
                            j = 2 * n + i
                            if n == 0:
                                pe.wait_ge(wb_done[i], it)
                            else:
                                pe.wait_ge(nrm_done[i], it * 2 + 1)
                            pe.matmul(px[i][:, :], keep["spread"][:, :], heads[:, s, 4 * j:4 * j + 4, :].rearrange("p g t -> p (g t)"),
                                      start=True, stop=True).then_inc(den_full[i], 1)
                    if n == 2:
                        for i in range(2):
                            pe.wait_ge(nrm_done[i], it * 2 + 2)
                        for m in range(2):
                            for j in (2 * m, 2 * m + 1):
                                for g in range(4):
                                    last = pe.matmul(halves(px[m])[:, j % 2, :], nrm[:, j, g, :], wo[:, g, :], start=(g == 0), stop=(g == 3))
                            last.then_inc(wo_full[m], 1)
                    if n == 3:
                        pe.wait_ge(xn_done, it + 1)
                        for eh in range(EH):
                            for j in range(JT):
                                last = pe.transpose(px[eh][:, j * P:(j + 1) * P], xn[:, j, eh * P:(eh + 1) * P], keep["ident"][:, :])
                        last.then_inc(tp_done, 1)
                    if n == 4:
                        pe.wait_ge(hT_done, it + 1)
                        for j in range(JT):
                            for eh in range(EH):
                                last = pe.matmul(px[0][:, j * NX:(j + 1) * NX], hT[:, s, eh, j * P:(j + 1) * P], gw[:, eh, :],
                                                 start=(eh == 0), stop=(eh == EH - 1))
                        last.then_inc(lg_full, 1)
                    if n == 5:
                        pe.wait_ge(cw_done, it + 1)
                        for j in range(JT):
                            last = pe.transpose(px[1][0:NX, j * P:(j + 1) * P], cw[:, s, j, :], keep["ident"][:, :])
                        last.then_inc(cp_full, 1)
                    if n == 6:
                        pe.wait_ge(cwT_done, it + 1)
                        for m in range(2):
                            for j in range(2):
                                last = pe.matmul(halves(px[m])[:, j, :], cwT[:, (2 * m + j) * P:(2 * m + j + 1) * P], b3[:, :],
                                                 start=True, stop=True)
                            last.then_inc(bp_full[m], 1)
                pe.wait_ge(w_split, NX)
                order(pe, piece, step)


SCRATCH = {
    "s_rel": ([2, D, TAB + 2 * G], F16),
    "s_q": ([2, B * NB, EH * P, P], F16),
    "s_k": ([2, B * NB, EH * P, P], F16),
    "s_v": ([B * NB, P, H, 2 * D], F32),
    "s_m": ([B * NB, H, P], F16),
    "s_of": ([B * NB, 4, P, P], F32),
    "s_o": ([B * NB, 4, P, P], F32),
}

KEEP = {
    "ident": ([P, P], F32), "mask_h": ([P, HH], F16), "mask_i": ([P, G], F16),
    "ident_s": ([G, H, G], F16), "mask_f": ([G, G], F16), "iota8": ([P, NX], F32),
    "ident_m": ([P, P], F16), "mask_n": ([P, P], F16),
    "spread": ([P, P], F32), "table": ([P, 2, TAB], F16),
    "shift_a": ([P, EH, B], F32), "scale_a": ([P, EH, B], F32),
    "shift_b": ([P, EH, B], F32), "scale_b": ([P, EH, B], F32), "gates": ([P, 2, B, E], F32),
}


def adaln_moe_layer(nc, **io):
    for name, (shape, dt) in SCRATCH.items():
        io[name] = nc.dram_tensor(name, shape, dt).ap()
    with ExitStack() as ctx:
        keep = {name: ctx.enter_context(nc.sbuf_tensor(name, shape, dt)) for name, (shape, dt) in KEEP.items()}
        phase_modulation(nc, io, keep)
        phase_project(nc, io, keep)
        phase_row_max(nc, io, keep)
        phase_far(nc, io, keep)
        phase_near(nc, io, keep)
        phase_ffn(nc, io, keep)


def kernel(**inputs):
    import numpy as _np
    import concourse.bacc as _bacc
    from concourse import mybir as _mybir
    from concourse.bass_utils import run_bass_kernel_spmd as _run

    def heads_inside(w):
        return w.reshape(-1, EH, HH, D).transpose(0, 1, 3, 2).reshape(w.shape)

    def on_partitions(v):
        return v.reshape(v.shape[:-1] + (EH, P)).swapaxes(-1, -2)

    get = {name: _np.asarray(v) for name, v in inputs.items()}
    r0 = _np.broadcast_to(get["L0_attn_rel_key"][0][None, :, None], (EH, D, HH)).reshape(E)
    laid = {
        "x": get["L0_attn_x"], "wq": heads_inside(get["L0_attn_Wq"]), "wk": heads_inside(get["L0_attn_Wk"]),
        "wv": get["L0_attn_Wv"], "wo": get["L0_attn_Wo"], "bv": get["L0_attn_bv"], "bo": get["L0_attn_bo"],
        "bq": on_partitions(heads_inside(get["L0_attn_bq"])), "bk": on_partitions(heads_inside(get["L0_attn_bk"])),
        "r0": on_partitions(r0), "relT": get["L0_attn_rel_key"].T, "cT": get["L0_c"].T, "wmod": get["L0_wmod"],
        "gwT": get["L0_ffn_gate_w"].T, "gate_b": get["L0_ffn_gate_b"],
        "w1": get["L0_ffn_w1"], "w2": get["L0_ffn_w2"], "w3": get["L0_ffn_w3"],
        "b1": on_partitions(get["L0_ffn_b1"]), "b2": on_partitions(get["L0_ffn_b2"]), "b3": get["L0_ffn_b3"],
    }
    nc = _bacc.Bacc("TRN2", target_bir_lowering=False, num_devices=1)
    arrays, io = {}, {}
    for name, v in laid.items():
        v = _np.ascontiguousarray(v)
        arrays[f"in_{name}"] = v
        io[name] = nc.dram_tensor(f"in_{name}", v.shape, _mybir.dt.from_np(v.dtype), kind="ExternalInput").ap()
    io["out"] = nc.dram_tensor("out_0", (B, S, E), _mybir.dt.from_np(_np.dtype("float32")), kind="ExternalOutput").ap()
    adaln_moe_layer(nc, **io)
    r = _run(nc, [arrays], core_ids=[0])
    return r.results[0]["out_0"]
```

```python
from contextlib import ExitStack

import concourse.bass as bass
from concourse import mybir

ALU = mybir.AluOpType
ACT = mybir.ActivationFunctionType
AX = mybir.AxisListType
F32 = mybir.dt.float32
F16 = mybir.dt.float16
U32 = mybir.dt.uint32

B, S, E = 4, 2048, 256
H, D, W = 16, 16, 512
P = 128
NB = S // P
EH = E // P
HH = 8
CH = 512
CPB = S // CH
NX = 8
G = 8
EPS = 1e-5
SCALE = D ** -0.5
KR = 4 * D + 1
NJ = W // P + 1
TAB = 760
TAB0 = 632
FARI = NJ
MASK = 30000.0


class PhaseMemory:

    def __init__(self, nc, tag):
        self.nc, self.tag, self.ctx, self.taken = nc, tag, ExitStack(), []

    def __enter__(self):
        return self

    def __exit__(self, *a):
        self.nc.clear_and_free_semaphores(self.taken)
        self.nc.all_engine_barrier()
        return self.ctx.__exit__(*a)

    def sb(self, name, shape, dt=F32):
        return self.ctx.enter_context(self.nc.sbuf_tensor(f"{self.tag}_{name}", shape, dt))

    def ps(self, name, shape):
        return self.ctx.enter_context(self.nc.psum_tensor(f"{self.tag}_{name}", shape, F32))

    def sem(self, name):
        self.taken.append(self.nc.alloc_semaphore(name=f"{self.tag}_{name}"))
        return self.taken[-1]

    def sems(self, name, n):
        return [self.sem(f"{name}{i}") for i in range(n)]


def phase_modulation(nc, io, keep):
    with PhaseMemory(nc, "mod") as a:
        cT = a.sb("cT", [P, EH, B])
        e_c = a.sb("e_c", [P, EH, B])
        den = a.sb("den", [P, EH, B])
        rec = a.sb("rec", [P, EH, B])
        silu = a.sb("silu", [P, EH, B])
        silu_b = a.sb("silu_b", [P, EH, B, P])
        wmod = a.sb("wmod", [P, EH, 6 * E])
        mag = a.sb("mag", [P, 2, B, E])
        raw = a.sb("raw", [P, 2, B, E])
        sgn = a.sb("sgn", [P, 2, B, E])
        relT = a.sb("relT", [D, W])
        relx = a.sb("relx", [D, TAB + 2 * G])
        relh = a.sb("relh", [D, TAB + 2 * G], F16)
        rell = a.sb("rell", [D, TAB + 2 * G], F16)
        mask_dh = a.sb("mask_dh", [P, D, HH])
        pm = a.ps("pm", [P, 12, B])
        pg = [a.ps(f"pg{i}", [P, 2, E]) for i in range(4)]
        loaded, wloaded = a.sem("loaded"), a.sem("wloaded")
        pool_step, act_exp, dve_step = a.sem("pool_step"), a.sem("act_exp"), a.sem("dve_step")
        silu_ready, mod_ready, gate_ready = a.sem("silu_ready"), a.sem("mod_ready"), a.sem("gate_ready")
        rel_ready, table_out, table_in = a.sem("rel_ready"), a.sem("table_out"), a.sem("table_in")
        with nc.Block() as block:

            @block.sync
            def _(sp):
                sp.dma_start(cT[:, :, :], io["cT"].rearrange("(e p) b -> p e b", p=P)).then_inc(loaded, 16)
                sp.dma_start(relT[:, :], io["relT"]).then_inc(loaded, 16)
                sp.dma_start(wmod[:, :, :], io["wmod"].rearrange("(e p) n -> p e n", p=P)).then_inc(wloaded, 16)
                sp.wait_ge(rel_ready, 1)
                sp.dma_start(io["s_rel"][0], relh[:, :]).then_inc(table_out, 16)
                sp.dma_start(io["s_rel"][1], rell[:, :]).then_inc(table_out, 16)
                sp.wait_ge(table_out, 32)
                for part in range(2):
                    for i in range(G):
                        sp.dma_start(keep["table"][i * D:(i + 1) * D, part, :],
                                     io["s_rel"][part][:, G - 1 - i:G - 1 - i + TAB]).then_inc(table_in, 16)
                sp.wait_ge(table_in, 32 * G)

            @block.gpsimd
            def _(pool):
                pool.memset(keep["ident"][:, :], 0.0)
                pool.memset(mask_dh[:, :, :], 1.0)
                pool.memset(keep["mask_i"][:, :], 1.0)
                pool.memset(keep["ident_s"][:, :, :], 1.0)
                pool.memset(keep["mask_f"][:, :], -MASK)
                pool.memset(keep["ident_m"][:, :], 0.0)
                pool.memset(keep["mask_n"][:, :], -MASK)
                pool.memset(keep["iota8"][:, :], 0.0).then_inc(pool_step, 1)
                pool.wait_ge(pool_step, 1)
                pool.affine_select(out=keep["ident"][:, :], in_=keep["ident"][:, :], compare_op=ALU.not_equal,
                                   fill=1.0, base=0, pattern=[[-1, P]], channel_multiplier=1)
                pool.affine_select(out=keep["mask_i"][:, :], in_=keep["mask_i"][:, :], compare_op=ALU.is_ge,
                                   fill=0.0, base=0, pattern=[[-D, G]], channel_multiplier=1)
                pool.affine_select(out=keep["ident_s"][:, :, :], in_=keep["ident_s"][:, :, :], compare_op=ALU.is_equal,
                                   fill=0.0, base=0, pattern=[[0, H], [-1, G]], channel_multiplier=1)
                pool.affine_select(out=keep["mask_f"][:, :], in_=keep["mask_f"][:, :], compare_op=ALU.is_ge,
                                   fill=0.0, base=-1, pattern=[[1, P]], channel_multiplier=-1)
                pool.affine_select(out=keep["ident_m"][:, :], in_=keep["ident_m"][:, :], compare_op=ALU.not_equal,
                                   fill=MASK, base=0, pattern=[[-1, P]], channel_multiplier=1)
                pool.affine_select(out=keep["mask_n"][:, :], in_=keep["mask_n"][:, :], compare_op=ALU.is_ge,
                                   fill=0.0, base=-1, pattern=[[-1, P]], channel_multiplier=1)
                pool.affine_select(out=mask_dh[:, :, :], in_=mask_dh[:, :, :], compare_op=ALU.is_equal,
                                   fill=0.0, base=0, pattern=[[-HH, D], [-1, HH]], channel_multiplier=1)
                for n in range(1, NX):
                    last = pool.memset(keep["iota8"][:, n:n + 1], float(n))
                last.then_inc(pool_step, 1)
                pool.wait_ge(pool_step, 2)
                pool.affine_select(out=keep["mask_i"][:, :], in_=keep["mask_i"][:, :], compare_op=ALU.is_ge,
                                   fill=0.0, base=D - 1, pattern=[[D, G]], channel_multiplier=-1).then_inc(pool_step, 1)
                pool.wait_ge(pool_step, 3)

            @block.scalar
            def _(act):
                act.wait_ge(loaded, 32)
                act.activation(e_c[:, :, :], cT[:, :, :], ACT.Exp, scale=-1.0).then_inc(act_exp, 1)

            @block.vector
            def _(dve):
                n = [0]

                def link(ins):
                    n[0] += 1
                    ins.then_inc(dve_step, 1)
                    dve.wait_ge(dve_step, n[0])

                dve.wait_ge(act_exp, 1)
                link(dve.tensor_scalar(den[:, :, :], e_c[:, :, :], 1.0, None, ALU.add))
                link(dve.reciprocal(rec[:, :, :], den[:, :, :]))
                dve.wait_ge(loaded, 32)
                link(dve.tensor_tensor(silu[:, :, :], cT[:, :, :], rec[:, :, :], ALU.mult))
                dve.tensor_copy(silu_b[:, :, :, :], silu[:, :, :].unsqueeze(3).broadcast_to([P, EH, B, P])).then_inc(silu_ready, 1)
                link(dve.tensor_scalar(relx[:, P:P + W], relT[:, :], relT[:, 0:1], None, ALU.subtract))
                dve.memset(relx[:, 0:P], 0.0)
                link(dve.tensor_copy(relx[:, P + W:], relx[:, P + W - 1:P + W].broadcast_to([D, TAB + 2 * G - P - W])))
                link(dve.tensor_copy(relh[:, :], relx[:, :]))
                dve.tensor_tensor(rell[:, :], relx[:, :], relh[:, :], ALU.subtract).then_inc(rel_ready, 1)
                dve.wait_ge(pool_step, 2)
                with nc.allow_low_precision("zeros and one one"):
                    dve.tensor_reduce(keep["mask_h"][:, :], mask_dh[:, :, :].rearrange("p d h -> p h d"), AX.X, ALU.add)
                dve.wait_ge(mod_ready, 1)
                for kind, dst in ((0, "shift_a"), (3, "shift_b")):
                    dve.tensor_copy(keep[dst][:, :, :], pm[:, 2 * kind:2 * kind + 2, :])
                for kind, dst in ((1, "scale_a"), (4, "scale_b")):
                    dve.tensor_scalar(keep[dst][:, :, :], pm[:, 2 * kind:2 * kind + 2, :], 1.0, None, ALU.add)
                for b in range(B):
                    dve.wait_ge(gate_ready, b + 1)
                    dve.tensor_copy(raw[:, :, b, :], pg[b][:, :, :])
                    link(dve.tensor_scalar(sgn[:, :, b, :], pg[b][:, :, :], 0.0, 2.0, ALU.is_ge, ALU.mult))
                flat = lambda t: t[:, :, :, :].rearrange("p k b e -> p (k b e)")
                link(dve.scalar_tensor_tensor(out=flat(mag), in0=flat(raw), scalar=-1.0, in1=flat(raw),
                                              op0=ALU.mult, op1=ALU.max))
                link(dve.tensor_scalar(flat(raw), flat(mag), 0.25, None, ALU.max))
                link(dve.scalar_tensor_tensor(out=keep["gates"][:, :, :, :].rearrange("p k b e -> p (k b e)"),
                                              in0=sgn[:, :, :, :].rearrange("p k b e -> p (k b e)"), scalar=-1.0,
                                              in1=flat(raw),
                                              op0=ALU.add, op1=ALU.mult))

            @block.tensor
            def _(pe):
                pe.wait_ge(silu_ready, 1)
                pe.wait_ge(wloaded, 16)
                for n in range(12):
                    for eh in range(EH):
                        last = pe.matmul(pm[:, n, :], wmod[:, eh, n * P:(n + 1) * P], silu[:, eh, :],
                                         start=(eh == 0), stop=(eh == EH - 1))
                last.then_inc(mod_ready, 1)
                for b in range(B):
                    for k, kind in enumerate((2, 5)):
                        for eh in range(EH):
                            last = pe.matmul(pg[b][:, k, :], silu_b[:, eh, b, :],
                                             wmod[:, eh, kind * E:(kind + 1) * E],
                                             start=(eh == 0), stop=(eh == EH - 1))
                    last.then_inc(gate_ready, 1)


def inverse_root(dve, out, sd, ve, t1, t2, step, n):
    dve.reciprocal(t1, sd).then_inc(step, 1)
    dve.wait_ge(step, n + 1)
    dve.tensor_tensor(t2, t1, ve, ALU.mult).then_inc(step, 1)
    dve.wait_ge(step, n + 2)
    dve.scalar_tensor_tensor(out=t2, in0=t2, scalar=-0.5, in1=t1, op0=ALU.mult, op1=ALU.mult).then_inc(step, 1)
    dve.wait_ge(step, n + 3)
    dve.scalar_tensor_tensor(out=out, in0=t2, scalar=1.5, in1=t1, op0=ALU.add, op1=ALU.mult).then_inc(step, 1)
    dve.wait_ge(step, n + 4)


def phase_project(nc, io, keep):
    with PhaseMemory(nc, "prj") as a:
        JT = CH // P
        wq, wk, wv = (a.sb(n, [P, EH, E]) for n in ("wq", "wk", "wv"))
        bq, bk, r0, bkr = (a.sb(n, [P, EH]) for n in ("bq", "bk", "r0", "bkr"))
        bv = a.sb("bv", [P, E])
        x = a.sb("x", [P, 2, JT, E])
        stats = a.sb("stats", [P, 2, JT, 6])
        tick = a.sb("tick", [P, 1])
        mod_now = a.sb("mod_now", [P, 2, EH])
        mv = a.sb("mv", [P, 2, JT, 2])
        ve, sd, r1, r2, rstd = (a.sb(n, [P, 2, JT]) for n in ("ve", "sd", "r1", "r2", "rstd"))
        xn = a.sb("xn", [P, 2, JT, E])
        hT = a.sb("hT", [P, 2, EH, CH])
        qf = a.sb("qf", [P, 4, CH])
        hi = a.sb("hi", [P, 4, CH], F16)
        lo = a.sb("lo", [P, 4, CH], F16)
        vx = a.sb("vx", [P, JT, H, 2 * D])
        tp = [a.ps(f"tp{i}", [P, CH]) for i in range(EH)]
        qp = [a.ps(f"qp{i}", [P, CH]) for i in range(4)]
        vp = [a.ps(f"vp{i}", [P, 2, E]) for i in range(2)]
        weights, biases = a.sem("weights"), a.sem("biases")
        x_in = a.sems("x_in", 2)
        xn_done, tp_done, hT_done = (a.sems(n, 2) for n in ("xn_done", "tp_done", "hT_done"))
        ln_step, once = a.sem("ln_step"), a.sem("once")
        mod_set = a.sem("mod_set")
        var_done, sd_done = a.sems("var_done", 2), a.sems("sd_done", 2)
        LN = 6
        qp_done, qf_done, hi_done, lo_done, hi_out, lo_out = (
            a.sems(n, 4) for n in ("qp_done", "qf_done", "hi_done", "lo_done", "hi_out", "lo_out"))
        vp_done, vx_done, vx_out = (a.sems(n, 2) for n in ("vp_done", "vx_done", "vx_out"))
        xv = io["x"].rearrange("b (c j p) e -> (b c) p j e", j=JT, p=P)
        NK = B * CPB

        def order(eng, ahead, main):
            def batch(b, last):
                for c in range(CPB):
                    it = b * CPB + c
                    following = (b, c + 1, it + 1) if c + 1 < CPB else (b + 1, 0, it + 1)
                    main(b, c, it, None if last and c == CPB - 1 else following)
            ahead(0, 0, 0)
            with eng.Fori(0, B - 1) as b:
                batch(b, False)
            batch(B - 1, True)
        slot_use = lambda b, c: b * (CPB // 2) + c // 2

        with nc.Block() as block:

            @block.gpsimd
            def _(pool):
                for w, name in ((wq, "wq"), (wk, "wk"), (wv, "wv")):
                    pool.dma_start(w[:, :, :], io[name].rearrange("(e p) n -> p e n", p=P)).then_inc(weights, 16)
                for w, name in ((bq, "bq"), (bk, "bk"), (r0, "r0")):
                    pool.dma_start(w[:, :], io[name]).then_inc(biases, 16)
                pool.dma_start(bv[:, :], io["bv"].partition_broadcast(P)).then_inc(biases, 16)
                with pool.Fori(0, NK // 2) as t:
                    for s in range(2):
                        pool.wait_ge(xn_done[s], t)
                        pool.dma_start(x[:, s], xv[bass.ds(t * 2 + s, 1)].rearrange("o p j e -> p (o j) e")).then_inc(x_in[s], 16)

            @block.vector
            def _(dve):
                dve.memset(vx[:, :, :, D:], 1.0)

                def ahead(b, c, it):
                    s, u = c % 2, slot_use(b, c)
                    dve.wait_ge(x_in[s], u * 16 + 16)
                    for j in range(JT):
                        last = dve.bn_stats(stats[:, s, j, :], x[:, s, j, :])
                    last.then_inc(ln_step, 1)
                    dve.wait_ge(ln_step, it * LN + 1)
                    dve.memset(tick[:, :], 0.0)
                    for j in range(JT):
                        last = dve.bn_aggr(mv[:, s, j, :], stats[:, s, j, :])
                    last.then_inc(ln_step, 1)
                    dve.wait_ge(ln_step, it * LN + 2)
                    dve.tensor_scalar(ve[:, s, :], mv[:, s, :, 1], EPS, None, ALU.add).then_inc(var_done[s], 1)
                    dve.wait_ge(sd_done[s], u + 1)
                    inverse_root(dve, rstd[:, s, :], sd[:, s, :], ve[:, s, :], r1[:, s, :], r2[:, s, :], ln_step, it * LN + 2)
                    dve.wait_ge(tp_done[s], u)
                    for j in range(JT):
                        last = dve.tensor_scalar(xn[:, s, j, :], x[:, s, j, :], mv[:, s, j, 0:1], rstd[:, s, j:j + 1],
                                                 ALU.subtract, ALU.mult)
                    last.then_inc(xn_done[s], 1)

                def low(it, n):
                    dve.wait_ge(hi_done[n], it + 1)
                    dve.wait_ge(lo_out[n], it * 16)
                    dve.tensor_tensor(lo[:, n, :], qf[:, n, :], hi[:, n, :], ALU.subtract).then_inc(lo_done[n], 1)

                def main(b, c, it, following):
                    for n in range(4):
                        dve.wait_ge(qp_done[n], it + 1)
                        dve.wait_ge(lo_done[n], it)
                        bias = bq[:, n:n + 1] if n < 2 else bkr[:, n - 2:n - 1]
                        dve.tensor_scalar(qf[:, n, :], qp[n][:, :], bias, None, ALU.add).then_inc(qf_done[n], 1)
                        if n:
                            low(it, n - 1)
                        elif following:
                            ahead(*following)
                    low(it, 3)
                    for n in range(2):
                        dve.wait_ge(vp_done[n], it + 1)
                        dve.wait_ge(vx_out[n], it * 16)
                        for j in range(2):
                            last = dve.tensor_tensor(vx[:, 2 * n + j, :, 0:D],
                                                     vp[n][:, j, :].rearrange("p (h d) -> p h d", d=D),
                                                     bv[:, :].rearrange("p (h d) -> p h d", d=D), ALU.add)
                        last.then_inc(vx_done[n], 1)

                dve.wait_ge(biases, 64)
                dve.tensor_tensor(bkr[:, :], bk[:, :], r0[:, :], ALU.add).then_inc(once, 1)
                dve.wait_ge(once, 1)
                order(dve, ahead, main)

            @block.scalar
            def _(act):
                def root(b, c, it):
                    s, u = c % 2, slot_use(b, c)
                    act.wait_ge(var_done[s], u + 1)
                    act.activation(sd[:, s, :], ve[:, s, :], ACT.Sqrt).then_inc(sd_done[s], 1)

                def modulate(b, c, it):
                    s, u = c % 2, slot_use(b, c)
                    if c == 0:
                        for k, name in enumerate(("shift_a", "scale_a")):
                            act.activation(mod_now[:, k, :].unsqueeze(2), keep[name][:, :, bass.ds(b, 1)], ACT.Copy).then_inc(mod_set, 1)
                        act.wait_ge(mod_set, b * 2 + 2)
                    act.wait_ge(tp_done[s], u + 1)
                    for eh in range(EH):
                        last = act.activation(hT[:, s, eh, :], tp[eh][:, :], ACT.Identity,
                                              bias=mod_now[:, 0, eh:eh + 1],
                                              scale=mod_now[:, 1, eh:eh + 1])
                    last.then_inc(hT_done[s], 1)

                def ahead(b, c, it):
                    root(b, c, it)
                    modulate(b, c, it)

                def split(it, n):
                    act.wait_ge(qf_done[n], it + 1)
                    act.wait_ge(hi_out[n], it * 16)
                    act.wait_ge(lo_done[n], it)
                    act.activation(hi[:, n, :], qf[:, n, :], ACT.Copy).then_inc(hi_done[n], 1)

                def main(b, c, it, following):
                    split(it, 0)
                    if following:
                        root(*following)
                    for n in range(1, 4):
                        split(it, n)
                    if following:
                        act.wait_ge(vp_done[1], it)
                        modulate(*following)
                order(act, ahead, main)

            @block.tensor
            def _(pe):
                pe.wait_ge(weights, 48)

                def ahead(b, c, it):
                    s, u = c % 2, slot_use(b, c)
                    pe.wait_ge(xn_done[s], u + 1)
                    pe.wait_ge(hT_done[1 - s], u + s)
                    for eh in range(EH):
                        for j in range(JT):
                            last = pe.transpose(tp[eh][:, j * P:(j + 1) * P], xn[:, s, j, eh * P:(eh + 1) * P],
                                                keep["ident"][:, :])
                    last.then_inc(tp_done[s], 1)

                def main(b, c, it, following):
                    s, u = c % 2, slot_use(b, c)
                    pe.wait_ge(hT_done[s], u + 1)
                    for n in range(4):
                        w = wq if n < 2 else wk
                        pe.wait_ge(qf_done[n], it)
                        for eh in range(EH):
                            last = pe.matmul(qp[n][:, :], w[:, eh, (n % 2) * P:(n % 2 + 1) * P], hT[:, s, eh, :],
                                             start=(eh == 0), stop=(eh == EH - 1))
                        last.then_inc(qp_done[n], 1)
                    if following:
                        ahead(*following)
                    for n in range(2):
                        pe.wait_ge(vx_done[n], it)
                        for j in range(2):
                            for eh in range(EH):
                                last = pe.matmul(vp[n][:, j, :], hT[:, s, eh, (2 * n + j) * P:(2 * n + j + 1) * P],
                                                 wv[:, eh, :], start=(eh == 0), stop=(eh == EH - 1))
                        last.then_inc(vp_done[n], 1)
                order(pe, ahead, main)

            @block.sync
            def _(sp):
                with sp.Fori(0, NK) as it:
                    for n in range(4):
                        dst = io["s_q"] if n < 2 else io["s_k"]
                        for part, (buf, done, out) in enumerate(((hi, hi_done, hi_out), (lo, lo_done, lo_out))):
                            sp.wait_ge(done[n], it + 1)
                            sp.dma_start(dst[part, bass.ds(it * JT, JT), (n % 2) * P:(n % 2 + 1) * P, :].rearrange("i r t -> r i t"),
                                         buf[:, n, :].rearrange("p (i t) -> p i t", t=P)).then_inc(out[n], 16)
                    for n in range(2):
                        sp.wait_ge(vx_done[n], it + 1)
                        sp.dma_start(io["s_v"][bass.ds(it * JT + 2 * n, 2)].rearrange("i p h d -> p i (h d)"),
                                     vx[:, 2 * n:2 * n + 2, :, :].rearrange("p i h d -> p i (h d)")).then_inc(vx_out[n], 16)
                for n in range(4):
                    sp.wait_ge(hi_out[n], NK * 16)
                    sp.wait_ge(lo_out[n], NK * 16)
                for n in range(2):
                    sp.wait_ge(vx_out[n], NK * 16)


def phase_row_max(nc, io, keep):
    NG, Q, TW, NBUF = P // G, 4, 1024, 4
    NQ = NG // Q
    IA, IP = 3, TW // P
    parts = lambda i: 1 if i < IP else 2
    by_act = lambda i, g, p: i >= IA and p == 0 and (i >= IP or g % Q > 0)
    in_quad = lambda i: Q if i >= IP else Q - 1
    TB = 0

    def tiles(i):
        row, k, groups, both = [], 0, [0] * NBUF, [0] * NBUF
        for s in range(2):
            for g in range(NG):
                if g == 2 * Q:
                    row.append((1 - s, "transpose", 0, TB, 0, both[TB]))
                    both[TB] += 1
                for p in range(parts(i)):
                    buf = k % NBUF
                    row.append((s, g, p, buf, groups[buf], both[buf]))
                    groups[buf], both[buf], k = groups[buf] + 1, both[buf] + 1, k + 1
        return row

    in_pass = lambda i: 2 * NG * parts(i) // NBUF
    T = B // 2
    full = lambda i, t, tile: T * sum(map(in_pass, range(i))) + t * in_pass(i) + tile[4] + 1
    free = lambda i, t, tile: full(i, t, (0, 0, 0, 0, 0)) - 1 + (t + i * T) * 2 * (tile[3] == TB) + tile[5]
    stashed = lambda i, t, s, q: (t + (i - IA) * T) * NQ + s * (NQ // 2) + q // 2
    quads = lambda i, t, s, q: ((t + (i - IA) * T) * 2 + s) * NQ + q

    def order(eng, prepare=None, group=None, transposed=None):
        for i in range(NB):
            with eng.Fori(0, T) as t:
                u = t + i * T
                if prepare:
                    prepare(i, t, u)
                for tile in tiles(i):
                    if tile[1] == "transpose":
                        transposed and transposed(i, t, u, tile)
                    elif group:
                        group(i, t, u, tile)
        if transposed:
            transposed(NB, 0, NB * T, (1, "transpose", 0, TB, 0, 0))

    with PhaseMemory(nc, "max") as a:
        kA = a.sb("kA", [P, 2, EH, S], F16)
        qn = a.sb("qn", [P, 2, EH, P], F16)
        qe = a.sb("qe", [P, 2, EH, HH * P], F16)
        qbd = a.sb("qbd", [P, 2, EH, NG, HH, G], F16)
        qex = a.sb("qex", [P, 2, NG, H, G], F16)
        stash = a.sb("stash", [P, 2, Q, TW], F16)
        half, quarter, eighth = (a.sb(n, [P, Q, TW // d], F16) for n, d in (("half", 2), ("quarter", 4), ("eighth", 8)))
        mx = a.sb("mx", [P, 2, NG])
        mx1 = a.sb("mx1", [P, 2, NG])
        mrow = a.sb("mrow", [NG, 2, P], F16)
        pa = a.ps("pa", [P, NBUF, TW])
        tick = a.sb("tick", [P, 2])
        k_in, q_in, qx_done, m_out, mx_done, mx_ready, unit_done, tr_full = (
            a.sems(n, 2) for n in ("k_in", "q_in", "qx_done", "m_out", "mx_done", "mx_ready", "unit_done", "tr_full"))
        pa_full, pa_free = a.sems("pa_full", NBUF), a.sems("pa_free", NBUF)
        stash_free, tree_step = a.sems("stash_free", 2), a.sem("tree_step")

        with nc.Block() as block:

            @block.sync
            def _(sp):
                def prepare(i, t, u):
                    for s in range(2):
                        sp.wait_ge(qx_done[s], u)
                        blk = t * (2 * NB) + (s * NB + i)
                        sp.dma_start(qn[:, s], io["s_q"][0, bass.ds(blk, 1)].rearrange("o (e r) t -> r (o e) t", e=EH)).then_inc(q_in[s], 16)
                        for e in range(EH):
                            sp.dma_start(qe[:, s, e, :], io["s_q"][0, bass.ds(blk, 1), e * P:(e + 1) * P, :]
                                         .rearrange("o (d h) t -> (o d) (h t)", d=D).partition_broadcast(G)).then_inc(q_in[s], 16)
                        sp.wait_ge(unit_done[s], u + s)
                        for e in range(EH):
                            sp.dma_start(kA[:, s, e, 0:(i + 1) * P].rearrange("p (j t) -> p j t", t=P),
                                         io["s_k"][0, bass.ds(t * (2 * NB) + s * NB, i + 1), e * P:(e + 1) * P, :]
                                         .rearrange("j r t -> r j t")).then_inc(k_in[s], 16)
                order(sp, prepare)

            @block.gpsimd
            def _(pool):
                def prepare(i, t, u):
                    for s in range(2):
                        pool.wait_ge(q_in[s], u * 48 + 48)
                        pool.wait_ge(unit_done[s], u + s)
                        for e in range(EH):
                            pool.tensor_tensor(qbd[:, s, e],
                                               qn[:, s, e, :].rearrange("p (g i) -> p g i", i=G).unsqueeze(2).broadcast_to([P, NG, HH, G]),
                                               keep["mask_h"][:, :].unsqueeze(1).unsqueeze(3).broadcast_to([P, NG, HH, G]), ALU.mult)
                            last = pool.tensor_tensor(qex[:, s, :, e * HH:(e + 1) * HH, :],
                                                      qe[:, s, e, :].rearrange("p (h g i) -> p g h i", h=HH, i=G),
                                                      keep["mask_i"][:, :].unsqueeze(1).unsqueeze(1).broadcast_to([P, NG, HH, G]), ALU.mult)
                        last.then_inc(qx_done[s], 1)
                order(pool, prepare)

            @block.tensor
            def _(pe):
                def group(i, t, u, tile):
                    s, g, p, n = tile[:4]
                    if g == p == 0:
                        pe.wait_ge(k_in[s], u * 32 + 32)
                        pe.wait_ge(qx_done[s], u + 1)
                    first, k0, k1 = i * P + g * G, p * TW, min((p + 1) * TW, (i + 1) * P)
                    mask = max(k0, first)
                    pe.wait_ge(pa_free[n], free(i, t, tile))
                    for c in range(k0, k1, CH):
                        for e in range(EH):
                            last = pe.matmul(pa[64 * e:64 * e + 64, n, c - k0:min(c + CH, k1) - k0], qbd[:, s, e, g], kA[:, s, e, c:min(c + CH, k1)],
                                             start=True, stop=False, skip_group_check=True)
                            if g == p == c == e == 0:
                                last.then_inc(unit_done[1 - s], 1)
                    lo = max(k0, first - W)
                    while lo < min(first + G, k1):
                        hi = min(first + G, k1, lo // CH * CH + CH)
                        last = pe.matmul(pa[:, n, lo - k0:hi - k0], qex[:, s, g], keep["table"][:, 0, lo - first + TAB0:hi - first + TAB0],
                                         start=False, stop=False, skip_group_check=True)
                        lo = hi
                    if mask < k1:
                        last = pe.matmul(pa[:, n, mask - k0:k1 - k0], keep["ident_s"][:, :, :], keep["mask_f"][:, 0:k1 - mask],
                                         start=False, stop=True, skip_group_check=True)
                    last.then_inc(pa_full[n], 1)

                def transposed(i, t, u, tile):
                    s, n = tile[0], tile[3]
                    pe.wait_ge(mx_ready[s], u + 1)
                    pe.wait_ge(pa_free[n], free(i, t, tile))
                    pe.transpose(pa[0:NG, n, 0:P], mx[:, s, :], keep["ident"][:, :]).then_inc(tr_full[s], 1)
                order(pe, None, group, transposed)

            @block.scalar
            def _(act):
                def store(i, t, u, tile):
                    s, n = tile[0], tile[3]
                    act.wait_ge(pa_free[n], free(i, t, tile) + 1)
                    if s == 0:
                        blk = t * (2 * NB) + i
                    else:
                        assert T == 2
                        blk = (T * 2 * NB - NB + i - 1) + t * (1 - 2 * NB)
                    act.dma_start(io["s_m"][bass.ds(blk, 1)].rearrange("o h (g i) -> g (o h) i", i=G),
                                  mrow[:, s, :].rearrange("g (h i) -> g h i", i=G)).then_inc(m_out[s], 16)

                def group(i, t, u, tile):
                    s, g, p, n = tile[:4]
                    q, width = g // Q, min(TW, (i + 1) * P)
                    if by_act(i, g, p):
                        r = g % Q - (Q - in_quad(i))
                        if r == 0:
                            act.wait_ge(stash_free[q % 2], stashed(i, t, s, q))
                        act.wait_ge(pa_full[n], full(i, t, tile))
                        act.activation(stash[:, q % 2, r, 0:width], pa[:, n, 0:width], ACT.Copy).then_inc(pa_free[n], 1)
                    if (g, p) == (3 * Q, 0):
                        store(i, t, u, [x for x in tiles(i) if x[:2] == (1 - s, "transpose")][0])

                def last_one(i, t, u, tile):
                    if i == NB:
                        store(i, t, u, tile)
                order(act, None, group, last_one)
                act.wait_ge(m_out[0], NB * T * 16)
                act.wait_ge(m_out[1], (NB * T + 1) * 16)

            @block.vector
            def _(dve):
                dve.memset(mx[:, :, :], 0.0).then_inc(mx_ready[1], 1)
                dve.wait_ge(mx_ready[1], 1)

                def ready(s):
                    dve.memset(tick[:, s:s + 1], 0.0).then_inc(mx_ready[s], 1)

                def tree(i, t, u, s, q, stage):
                    width, k, r = min(TW, (i + 1) * P), quads(i, t, s, q) * 2, in_quad(i)
                    w2, w4, w8 = width // 2, width // 4, width // 8
                    if stage == 0:
                        last = [x for x in tiles(i) if x[:3] == (s, q * Q + Q - 1, 0)][0]
                        dve.wait_ge(pa_free[last[3]], free(i, t, last) + 1)
                        dve.tensor_tensor(half[:, 0:r, 0:w2], stash[:, q % 2, 0:r, 0:w2], stash[:, q % 2, 0:r, w2:width],
                                          ALU.max).then_inc(stash_free[q % 2], 1)
                    if stage == 1:
                        dve.wait_ge(stash_free[q % 2], stashed(i, t, s, q) + 1)
                        dve.tensor_tensor(quarter[:, 0:r, 0:w4], half[:, 0:r, 0:w4], half[:, 0:r, w4:w2], ALU.max).then_inc(tree_step, 1)
                    if stage == 2:
                        dve.wait_ge(tree_step, k + 1)
                        dve.tensor_tensor(eighth[:, 0:r, 0:w8], quarter[:, 0:r, 0:w8], quarter[:, 0:r, w8:w4], ALU.max).then_inc(tree_step, 1)
                    if stage == 3:
                        dve.wait_ge(tree_step, k + 2)
                        dve.reduce_max(mx[:, s, q * Q + Q - r:q * Q + Q], eighth[:, 0:r, 0:w8], AX.X).then_inc(mx_done[s], 1)
                        if i >= IP and q == NQ - 1:
                            dve.wait_ge(mx_done[s], (u - IA * T) * NQ + NQ)
                            dve.tensor_tensor(mx[:, s, :], mx[:, s, :], mx1[:, s, :], ALU.max)
                        if q == NQ - 1:
                            ready(s)

                def group(i, t, u, tile):
                    s, g, p, n = tile[:4]
                    if not by_act(i, g, p):
                        dve.wait_ge(pa_full[n], full(i, t, tile))
                        dve.reduce_max((mx1 if p else mx)[:, s, g:g + 1], pa[:, n, 0:min(TW, (i + 1) * P - p * TW)],
                                       AX.X).then_inc(pa_free[n], 1)
                    if i >= IA and (s, g // Q) != (0, 0) and p == parts(i) - 1:
                        tree(i, t, u, *((s, g // Q - 1) if g // Q else (0, NQ - 1)), g % Q)
                    if i < IA and g == NG - 1:
                        ready(s)
                    if i >= IA and (s, g, p) == (1, NG - 1, parts(i) - 1):
                        for stage in range(4):
                            tree(i, t, u, 1, NQ - 1, stage)

                def transposed(i, t, u, tile):
                    s, n = tile[0], tile[3]
                    dve.wait_ge(tr_full[s], u + 1)
                    dve.wait_ge(m_out[s], u * 16)
                    dve.tensor_copy(mrow[:, s, :], pa[0:NG, n, 0:P]).then_inc(pa_free[n], 1)
                order(dve, None, group, transposed)


def phase_far(nc, io, keep):
    NF = NB - FARI
    chunks = ((FARI, 8), (8, 12), (12, 16))
    steps = [(c, j, max(lo, j + NJ), hi) for c, (lo, hi) in enumerate(chunks) for j in range(hi - NJ)]
    NS = len(steps)
    with PhaseMemory(nc, "far") as a:
        kf = a.sb("kf", [KR, 2, NF, 4 * P], F16)
        qf = a.sb("qf", [KR, 2, NF, 4, P], F16)
        vf = a.sb("vf", [P, 2, NF, 4, 2 * D])
        pt = a.sb("pt", [P, 3, 4, CH])
        of = a.sb("of", [P, 2, 4, P])
        ps = [a.ps(f"ps{i}", [P, 2, CH]) for i in range(3)]
        po = [a.ps(f"po{i}", [P, 4, P]) for i in range(2)]
        ones = a.sem("ones")
        in_, unit_done = a.sems("in", 2), a.sems("unit_done", 2)
        s_full, p_full, p_free = (a.sems(n, 3) for n in ("s_full", "p_full", "p_free"))
        po_free, of_out = (a.sems(n, 2) for n in ("po_free", "of_out"))
        NIN = 10 * 16

        with nc.Block() as block:

            @block.sync
            def _(sp):
                with sp.Fori(0, B) as b:
                    with sp.Fori(0, 2) as w:
                        t = b * 2 + w
                        for s in range(2):
                            sp.wait_ge(unit_done[s], t + s)
                            rows = lambda buf, part, j0: (buf[part, bass.ds(b * NB + j0, NF), bass.ds(w * P, P), :]
                                                          .rearrange("j (d h) t -> d j h t", h=HH)[:, :, 4 * s:4 * s + 4, :]
                                                          .rearrange("d j h t -> d j (h t)"))
                            for r, part in enumerate((0, 1, 0, 1)):
                                sp.dma_start(kf[r * D:(r + 1) * D, s], rows(io["s_k"], part, 0)).then_inc(in_[s], 16)
                            for r, part in enumerate((0, 0, 1, 1)):
                                sp.dma_start(qf[r * D:(r + 1) * D, s].rearrange("d i h t -> d i (h t)"),
                                             rows(io["s_q"], part, FARI)).then_inc(in_[s], 16)
                            sp.dma_start(qf[4 * D:KR, s].rearrange("d i h t -> d i (h t)"),
                                         io["s_m"][bass.ds(b * NB + FARI, NF), bass.ds(w * HH + 4 * s, 4), :]
                                         .rearrange("i h t -> i (h t)").unsqueeze(0)).then_inc(in_[s], 16)
                            sp.dma_start(vf[:, s].rearrange("p j h d -> p j (h d)"),
                                         io["s_v"][bass.ds(b * NB, NF), :, bass.ds(w * HH + 4 * s, 4), :]
                                         .rearrange("j p h d -> p j (h d)")).then_inc(in_[s], 16)

            @block.tensor
            def _(pe):
                pe.wait_ge(ones, 1)
                with pe.Fori(0, B * 2) as t:
                    for s in range(2):
                        v = t * 2 + s
                        pe.wait_ge(in_[s], t * NIN + NIN)

                        def pv(k):
                            c, j, lo, hi = steps[k]
                            c0, chi = chunks[c]
                            buf, uses = (3 * s + c) % 2, t * 3 + (3 * s + c) // 2
                            if j == 0:
                                pe.wait_ge(po_free[buf], uses)
                            pe.wait_ge(p_full[k % 3], (v * (NS // 3) + k // 3) * 2 + 2)
                            for h in range(4):
                                last = pe.matmul(po[buf][32 * h:32 * h + 32, lo - c0:hi - c0, :], vf[:, s, j, h, :],
                                                 pt[:, k % 3, h, 0:(hi - lo) * P],
                                                 start=(j == 0), stop=(j == chi - NJ - 1), skip_group_check=True)
                            last.then_inc(p_free[k % 3], 1)

                        for k, (c, j, lo, hi) in enumerate(steps):
                            for r in range(2):
                                n = 2 * k + r
                                if n < 3:
                                    pe.wait_ge(p_full[(NS - 2 + (n + 1) // 2) % 3 if n < 2 else (NS - 1) % 3], v * (2 * NS // 3))
                                else:
                                    m = n - 3
                                    pe.wait_ge(p_full[m // 2 % 3], (v * (NS // 3) + m // 6) * 2 + m % 2 + 1)
                                for h in range(2):
                                    last = pe.matmul(ps[n % 3][:, h, 0:(hi - lo) * P], kf[:, s, j, (2 * r + h) * P:(2 * r + h + 1) * P],
                                                     qf[:, s, lo - FARI:hi - FARI, 2 * r + h, :], start=True, stop=True)
                                    if n == h == 0:
                                        last.then_inc(unit_done[1 - s], 1)
                                last.then_inc(s_full[n % 3], 1)
                            if k:
                                pv(k - 1)
                        pv(NS - 1)

            @block.scalar
            def _(act):
                with act.Fori(0, B * 2) as t:
                    for s in range(2):
                        v = t * 2 + s
                        for k, (c, j, lo, hi) in enumerate(steps):
                            act.wait_ge(p_free[k % 3], v * (NS // 3) + k // 3)
                            for r in range(2):
                                n = 2 * k + r
                                act.wait_ge(s_full[n % 3], v * (2 * NS // 3) + n // 3 + 1)
                                act.activation(pt[:, k % 3, 2 * r:2 * r + 2, 0:(hi - lo) * P], ps[n % 3][:, :, 0:(hi - lo) * P],
                                               ACT.Exp, scale=SCALE).then_inc(p_full[k % 3], 1)

            @block.vector
            def _(dve):
                dve.memset(kf[4 * D:KR, :, :, :], -1.0).then_inc(ones, 1)
                with dve.Fori(0, B * 2) as t:
                    for s in range(2):
                        for c, (lo, hi) in enumerate(chunks):
                            buf, uses = (3 * s + c) % 2, t * 3 + (3 * s + c) // 2
                            k = max(k for k in range(NS) if steps[k][0] == c)
                            dve.wait_ge(p_free[k % 3], (t * 2 + s) * (NS // 3) + k // 3 + 1)
                            dve.wait_ge(of_out[buf], uses * 16)
                            dve.tensor_copy(of[:, buf, 0:hi - lo, :], po[buf][:, 0:hi - lo, :]).then_inc(po_free[buf], 1)

            @block.gpsimd
            def _(pool):
                with pool.Fori(0, B) as b:
                    with pool.Fori(0, 2) as w:
                        t = b * 2 + w
                        for s in range(2):
                            for c, (lo, hi) in enumerate(chunks):
                                buf, uses = (3 * s + c) % 2, t * 3 + (3 * s + c) // 2
                                pool.wait_ge(po_free[buf], uses + 1)
                                pool.dma_start(io["s_of"][bass.ds(b * NB + lo, hi - lo), bass.ds(w * 2 + s, 1), :, :]
                                               .rearrange("i o r t -> r (i o) t"),
                                               of[:, buf, 0:hi - lo, :]).then_inc(of_out[buf], 16)
                for buf in range(2):
                    pool.wait_ge(of_out[buf], B * 2 * 3 * 16)


def phase_near(nc, io, keep):
    NG = P // G
    with PhaseMemory(nc, "near") as a:
        kn = a.sb("kn", [KR, 4, NJ, HH * P], F16)
        vn = a.sb("vn", [P, 4, NJ, HH, 2 * D])
        qs = a.sb("qs", [KR, 4, HH, P], F16)
        qe = a.sb("qe", [P, 4, 2, HH, P], F16)
        qx = a.sb("qx", [P, 4, 2, NG, HH, G], F16)
        pt = a.sb("pt", [P, 2, HH, P])
        fo = a.sb("fo", [P, 4, 2, P])
        on = a.sb("on", [P, 2, 2, P])
        ps = [a.ps(f"ps{i}", [P, 2, HH, P // 2]) for i in range(2)]
        po = [a.ps(f"po{i}", [P, 2, P]) for i in range(2)]
        ones = a.sem("ones")
        k_in, q_in, f_in, qx_done, unit_done = (a.sems(n, 4) for n in ("k_in", "q_in", "f_in", "qx_done", "unit_done"))
        on_done, on_out = (a.sems(n, 2) for n in ("on_done", "on_out"))
        s_full, p_full, p_free = (a.sems(n, 2) for n in ("s_full", "p_full", "p_free"))
        NIN = 8 * 16

        def levels(eng, body):
            for i in range(FARI):
                with eng.Fori(0, B // 2) as c:
                    nj = i + 1
                    body(c, i, nj, False, c + i * (B // 2), c * (2 * nj) + B * i * (i + 1) // 2)
            with eng.Fori(0, B // 2) as c:
                with eng.Fori(0, NB - FARI) as r:
                    u = c * (NB - FARI) + r
                    body(c, r + FARI, NJ, True, u + FARI * (B // 2), u * (2 * NJ) + B * FARI * (FARI + 1) // 2)

        block_of = lambda c, i, v: c * (2 * NB) + i + v // 2 * NB
        even_use = lambda u, v: u * 2 + v // 2

        with nc.Block() as block:

            @block.sync
            def _(sp):
                def body(c, i, nj, far, u, k):
                    for v in range(4):
                        blk, s = block_of(c, i, v), v % 2
                        sp.wait_ge(qx_done[v], u)
                        for part in range(2):
                            sp.dma_start(qe[:, v, part].rearrange("r h t -> r (h t)"),
                                         io["s_q"][part, bass.ds(blk, 1), s * P:(s + 1) * P, :]
                                         .rearrange("o (d h) t -> (o d) (h t)", h=HH).partition_broadcast(G)).then_inc(q_in[v], 16)
                        sp.wait_ge(unit_done[v], u + v // 3)
                        for r, part in enumerate((0, 1, 0, 1)):
                            sp.dma_start(kn[r * D:(r + 1) * D, v, 0:nj, :],
                                         io["s_k"][part, bass.ds(blk - (nj - 1), nj), s * P:(s + 1) * P, :]
                                         .rearrange("j (d h) t -> d j (h t)", h=HH)).then_inc(k_in[v], 16)
                        for r, part in enumerate((0, 1)):
                            sp.dma_start(qs[r * 2 * D:(r + 1) * 2 * D, v].rearrange("r h t -> r (h t)"),
                                         io["s_q"][part, bass.ds(blk, 1), s * P:(s + 1) * P, :]
                                         .rearrange("o (d h) t -> (o d) (h t)", h=HH).partition_broadcast(2)).then_inc(k_in[v], 16)
                        sp.dma_start(qs[4 * D:KR, v].rearrange("r h t -> r (h t)"),
                                     io["s_m"][bass.ds(blk, 1), s * HH:(s + 1) * HH, :].rearrange("o h t -> o (h t)")).then_inc(k_in[v], 16)
                        sp.dma_start(vn[:, v, 0:nj].rearrange("p j h d -> p j (h d)"),
                                     io["s_v"][bass.ds(blk - (nj - 1), nj), :, s * HH:(s + 1) * HH, :]
                                     .rearrange("j p h d -> p j (h d)")).then_inc(k_in[v], 16)
                        if far:
                            sp.wait_ge(on_done[s], even_use(u, v) - 1)
                            sp.dma_start(fo[:, v], io["s_of"][bass.ds(blk, 1), 2 * s:2 * s + 2, :, :]
                                         .rearrange("o c r t -> r (o c) t")).then_inc(f_in[v], 16)
                levels(sp, body)

            @block.gpsimd
            def _(pool):
                def body(c, i, nj, far, u, k):
                    for v in range(4):
                        pool.wait_ge(q_in[v], u * 32 + 32)
                        pool.wait_ge(unit_done[v], u + v // 3)
                        for part in range(2):
                            last = pool.tensor_tensor(qx[:, v, part], qe[:, v, part].rearrange("p h (g i) -> p g h i", i=G),
                                                      keep["mask_i"][:, :].unsqueeze(1).unsqueeze(1).broadcast_to([P, NG, HH, G]), ALU.mult)
                        last.then_inc(qx_done[v], 1)
                levels(pool, body)

            @block.vector
            def _(dve):
                dve.memset(kn[4 * D:KR, :, :, :], -1.0).then_inc(ones, 1)

                def body(c, i, nj, far, u, k):
                    for v in range(4):
                        n, s = nj * v + nj - 1, v % 2
                        dve.wait_ge(p_free[n % 2], k + n // 2 + 1)
                        dve.wait_ge(on_out[s], even_use(u, v) * 16)
                        if far:
                            dve.wait_ge(f_in[v], (u - FARI * (B // 2)) * 16 + 16)
                            dve.tensor_tensor(on[:, s], po[s][:, :, :], fo[:, v], ALU.add).then_inc(on_done[s], 1)
                        else:
                            dve.tensor_copy(on[:, s], po[s][:, :, :]).then_inc(on_done[s], 1)
                levels(dve, body)

            @block.scalar
            def _(act):
                def body(c, i, nj, far, u, k):
                    def store(v):
                        s = v % 2
                        act.wait_ge(on_done[s], even_use(u, v) + 1)
                        act.dma_start(io["s_o"][bass.ds(block_of(c, i, v), 1), 2 * s:2 * s + 2, :, :]
                                      .rearrange("o c r t -> r (o c) t"), on[:, s]).then_inc(on_out[s], 16)
                    for v in range(4):
                        for j in range(nj):
                            n = nj * v + j
                            act.wait_ge(p_free[n % 2], k + n // 2)
                            act.wait_ge(s_full[n % 2], k + n // 2 + 1)
                            act.activation(pt[:, n % 2].rearrange("p h (x t) -> p x h t", x=2), ps[n % 2][:, :, :, :],
                                           ACT.Exp, scale=SCALE).then_inc(p_full[n % 2], 1)
                        if v:
                            store(v - 1)
                    store(3)
                levels(act, body)
                for s in range(2):
                    act.wait_ge(on_out[s], NB * B * 16)

            @block.tensor
            def _(pe):
                pe.wait_ge(ones, 1)

                def body(c, i, nj, far, u, k):
                    steps = [(v, j) for v in range(4) for j in range(nj)]

                    def pv(n):
                        v, j = steps[n]
                        s = v % 2
                        if j == 0:
                            pe.wait_ge(on_done[s], even_use(u, v))
                        pe.wait_ge(p_full[n % 2], k + n // 2 + 1)
                        for h in range(HH):
                            last = pe.matmul(po[s][32 * (h % 4):32 * (h % 4) + 32, h // 4, :], vn[:, v, nj - 1 - j, h, :],
                                             pt[:, n % 2, h, :], start=(j == 0 and h < 4), stop=(j == nj - 1 and h >= 4),
                                             skip_group_check=True)
                            if j == h == 0:
                                last.then_inc(unit_done[(v - 1) % 4], 1)
                        last.then_inc(p_free[n % 2], 1)

                    for n, (v, j) in enumerate(steps):
                        if j == 0:
                            pe.wait_ge(k_in[v], u * NIN + NIN)
                            pe.wait_ge(qx_done[v], u + 1)
                        pe.wait_ge(p_full[n % 2], k + n // 2)
                        for x in range(2):
                            bank = ps[n % 2][:, x]
                            for h in range(HH):
                                pe.matmul(bank[:, h, :], kn[:, v, nj - 1 - j, h * P:(h + 1) * P], qs[:, v, h, x * 64:x * 64 + 64],
                                          start=(h == 0), stop=False, skip_group_check=True)
                            if j == 0:
                                pe.matmul(bank[:, :, :], keep["ident_m"][:, :],
                                          keep["mask_n"][:, x * 64:x * 64 + 64].unsqueeze(1).broadcast_to([P, HH, 64]),
                                          start=False, stop=False, skip_group_check=True)
                            for g in range(NG // 2):
                                y = TAB0 - j * P - (x * 64 + g * G)
                                out = bank[:, :, g * G:g * G + G]
                                for part, qpart in ((0, 0), (0, 1), (1, 0)):
                                    last = pe.matmul(out, keep["table"][:, part, y:y + P], qx[:, v, qpart, x * (NG // 2) + g],
                                                     start=False, stop=(g == NG // 2 - 1 and part == 1), skip_group_check=True)
                        last.then_inc(s_full[n % 2], 1)
                        if nj == 1:
                            pv(n)
                        elif n:
                            pv(n - 1)
                    if nj > 1:
                        pv(len(steps) - 1)
                levels(pe, body)


def phase_ffn(nc, io, keep):
    JT = CH // P
    NK = B * CPB
    with PhaseMemory(nc, "ffn") as a:
        wo = a.sb("wo", [P, 4, E])
        gw = a.sb("gw", [P, EH, NX])
        gbias = a.sb("gbias", [P, NX])
        b3 = a.sb("b3", [NX, E])
        bo = a.sb("bo", [P, E])
        gbo = a.sb("gbo", [P, B, E])
        w_f = a.sb("w_f", [P, 2, 3, EH, E])
        w_s = a.sb("w_s", [P, 2, NX, 3, EH, E], F16)
        b1, b2 = (a.sb(n, [P, NX, EH]) for n in ("b1", "b2"))
        gbo_now, gb_now = a.sb("gbo_now", [P, 1, E]), a.sb("gb_now", [P, 1, E])
        mod_now = a.sb("mod_now", [P, 2, EH])
        x = a.sb("x", [P, 2, JT, E])
        heads = a.sb("heads", [P, 2, JT * 4, P])
        sums_of = a.sb("sums_of", [P, 2, JT * 4, P])
        nrm = a.sb("nrm", [P, JT, 4, P])
        att = a.sb("att", [P, JT, E])
        x1 = a.sb("x1", [P, JT, E])
        xn = att
        stats, mv = a.sb("stats", [P, JT, 6]), a.sb("mv", [P, JT, 2])
        tick = a.sb("tick", [P, 1])
        ve, sd, r1, r2, rstd = (a.sb(n, [P, JT]) for n in ("ve", "sd", "r1", "r2", "rstd"))
        lg, sh, ex, pr, o1, o2, g1, g2 = (a.sb(n, [P, JT, NX]) for n in ("lg", "sh", "ex", "pr", "o1", "o2", "g1", "g2"))
        top, topf = a.sb("top", [P, JT, 8]), a.sb("topf", [P, JT, 8])
        topi = a.sb("topi", [P, JT, 8], U32)
        mxs, sums, rsum = (a.sb(n, [P, JT]) for n in ("mxs", "sums", "rsum"))
        cwT = a.sb("cwT", [NX, CH])
        wb = a.sb("wb", [P, 2, 2, E])
        hT = a.sb("hT", [P, 2, EH, CH])
        cw = a.sb("cw", [P, 2, JT, NX])
        base = a.sb("base", [P, 2, JT, E])
        hT_s = a.sb("hT_s", [P, 2, 2, EH, CH], F16)
        h1_f, h2_f = a.sb("h1_f", [P, EH, CH]), a.sb("h2_f", [P, EH, CH])
        h1_s, h2_s = (a.sb(n, [P, 2, 2, EH, CH], F16) for n in ("h1_s", "h2_s"))
        y = a.sb("y", [P, 2, JT, E])
        p1 = [a.ps(f"p1{i}", [P, CH]) for i in range(EH)]
        p2 = [a.ps(f"p2{i}", [P, CH]) for i in range(EH)]
        p3 = [a.ps(f"p3{i}", [P, 2, E]) for i in range(2)]
        px = [a.ps(f"px{i}", [P, CH]) for i in range(2)]
        halves = lambda bank: bank[:, :].rearrange("p (j e) -> p j e", e=E)

        zeroed, weights, once, gbo_set, gb_set, mod_set = (
            a.sem(n) for n in ("zeroed", "weights", "once", "gbo_set", "gb_set", "mod_set"))
        w_in, w_hi, w_split = a.sems("w_in", 2), a.sem("w_hi"), a.sem("w_split")
        hT_split, h1_split, h2_split = a.sem("hT_split"), a.sems("h1_split", 2), a.sems("h2_split", 2)
        x_in, heads_in, out_done, out_sent = (a.sems(n, 2) for n in ("x_in", "heads_in", "out_done", "out_sent"))
        rec_done, nrm_done = a.sem("rec_done"), a.sem("nrm_done")
        wo_full, att_done, bp_full, wb_done, base_done = (
            a.sems(n, 2) for n in ("wo_full", "att_done", "bp_full", "wb_done", "base_done"))
        xb_done, x1_done, ln_step, var_done, sd_done, xn_done, tp_done, hT_done = (
            a.sem(n) for n in ("xb_done", "x1_done", "ln_step", "var_done", "sd_done", "xn_done", "tp_done", "hT_done"))
        lg_full, route_step, sh_done, ex_done, cw_done, cp_full, cwT_done = (
            a.sem(n) for n in ("lg_full", "route_step", "sh_done", "ex_done", "cw_done", "cp_full", "cwT_done"))
        p1_full, h1_done, p2_full, h2_done, p3_full, p3_free = (
            a.sems(n, 2) for n in ("p1_full", "h1_done", "p2_full", "h2_done", "p3_full", "p3_free"))
        NW = 9 * 16
        LN, RS = 6, 11
        NS = CPB * NX
        LAG = 2

        def order(eng, piece, step, weights, piece_first=True):
            for n in range(NX):
                piece(0, 0, 0, n)
                for e in (2 * n - NX, 2 * n - NX + 1) if n >= NX // 2 else ():
                    weights(e)

            def batch(b, last):
                for k in range(NS + LAG):
                    prepare = k < NS and not (last and k >= NS - NX)
                    nb, nc_ = (b, k // NX + 1) if k // NX + 1 < CPB else (b + 1, 0)
                    if prepare and piece_first:
                        piece(nb, nc_, b * CPB + k // NX + 1, k % NX)
                    step(b, k)
                    if prepare and not piece_first:
                        piece(nb, nc_, b * CPB + k // NX + 1, k % NX)
            with eng.Fori(0, B - 1) as b:
                batch(b, False)
            batch(B - 1, True)

        with nc.Block() as block:

            @block.sync
            def _(sp):
                sp.wait_ge(zeroed, 1)
                for q in range(4):
                    sp.dma_start(wo[32 * q:32 * q + D, :, :], io["wo"].rearrange("(g q d) n -> q d g n", q=4, d=D)[q]).then_inc(weights, 16)
                sp.dma_start(bo[:, :], io["bo"].partition_broadcast(P)).then_inc(weights, 16)
                sp.dma_start(gbias[:, :], io["gate_b"].partition_broadcast(P)).then_inc(weights, 16)
                sp.dma_start(b3[:, :], io["b3"]).then_inc(weights, 16)
                for eh in range(EH):
                    sp.dma_start(gw[:, eh, :], io["gwT"][eh * P:(eh + 1) * P, :]).then_inc(weights, 16)
                xv = io["x"].rearrange("b (c j p) e -> (b c) p j e", j=JT, p=P)

                def load(u, s):
                    it = u * 2 + s
                    sp.dma_start(x[:, s], xv[bass.ds(it, 1)].rearrange("o p j e -> p (o j) e")).then_inc(x_in[s], 16)
                    for j in range(JT):
                        sp.dma_start(heads[:, s, 4 * j:4 * j + 4], io["s_o"][bass.ds(it * JT + j, 1)].rearrange("i o r t -> r (i o) t")).then_inc(heads_in[s], 16)
                    for q in range(4):
                        sp.dma_start(sums_of[32 * q:32 * q + D, s], io["s_o"][bass.ds(it * JT, JT), :, 32 * q + D:32 * q + 2 * D, :]
                                     .rearrange("i o r t -> r (i o) t")).then_inc(heads_in[s], 16)
                load(0, 0)
                load(0, 1)
                for e in range(NX):
                    if e >= 2:
                        sp.wait_ge(w_split, e - 1)
                    for i, name in enumerate(("w1", "w2", "w3")):
                        sp.dma_start(w_f[:, e % 2, i], io[name][e].rearrange("(k p) n -> p k n", p=P)).then_inc(w_in[e % 2], 16)
                    for w, name in ((b1, "b1"), (b2, "b2")):
                        sp.dma_start(w[:, e, :], io[name][e]).then_inc(w_in[e % 2], 16)
                with sp.Fori(0, NK // 2 - 1) as u:
                    for s in range(2):
                        sp.wait_ge(x1_done, u * 2 + (s + 1))
                        load(u + 1, s)

            @block.gpsimd
            def _(pool):
                pool.memset(sums_of[:, :, :, :], 1.0)
                pool.memset(wo[:, :, :], 0.0).then_inc(zeroed, 1)
                pool.wait_ge(once, 1)

                def piece(b, c, it, n):
                    s = c % 2
                    if n == 0:
                        if c == 0:
                            pool.tensor_copy(gbo_now[:, :, :], gbo[:, bass.ds(b, 1), :]).then_inc(gbo_set, 1)
                            pool.wait_ge(gbo_set, b + 1)
                        pool.wait_ge(x_in[s], (b * (CPB // 2) + c // 2) * 16 + 16)
                        pool.tensor_tensor(x[:, s], x[:, s], gbo_now[:, :, :].broadcast_to([P, JT, E]), ALU.add).then_inc(xb_done, 1)
                    if n == 7:
                        pool.wait_ge(out_sent[s], (b * (CPB // 2) + c // 2) * 16)
                        for m in range(2):
                            pool.wait_ge(wb_done[m], it + 1)
                            pool.tensor_tensor(base[:, s, 2 * m:2 * m + 2, :], wb[:, m], x1[:, 2 * m:2 * m + 2, :], ALU.add).then_inc(base_done[m], 1)

                def step(b, k):
                    if k < NS:
                        pool.wait_ge(p2_full[EH - 1], b * NS + max(k - 1, 0))
                        for eh in range(EH):
                            pool.wait_ge(h1_done[eh], b * NS + k + 1)
                            pool.tensor_tensor(h1_s[:, k % 2, 1, eh, :], h1_f[:, eh, :], h1_s[:, k % 2, 0, eh, :], ALU.subtract).then_inc(h1_split[eh], 1)
                    if k % NX != LAG - 1 or k < NX:
                        return
                    c = k // NX - 1
                    s, it, u = c % 2, b * CPB + c, b * (CPB // 2) + c // 2
                    if c == 0:
                        pool.tensor_copy(gb_now[:, :, :], keep["gates"][:, 1, bass.ds(b, 1), :]).then_inc(gb_set, 1)
                        pool.wait_ge(gb_set, b + 1)
                    for m in range(2):
                        pool.wait_ge(p3_free[m], it * NX + NX)
                    pool.tensor_tensor(y[:, s], y[:, s], gb_now[:, :, :].broadcast_to([P, JT, E]), ALU.mult).then_inc(out_done[s], 1)
                    pool.wait_ge(out_done[s], u * 2 + 1)
                    for m in range(2):
                        pool.wait_ge(base_done[m], it + 1)
                    pool.tensor_tensor(base[:, s], y[:, s], base[:, s], ALU.add).then_inc(out_done[s], 1)
                    pool.wait_ge(out_done[s], u * 2 + 2)
                    pool.dma_start(io["out"][bass.ds(b, 1), c * CH:(c + 1) * CH, :]
                                   .rearrange("o (j p) e -> p (o j) e", p=P), base[:, s]).then_inc(out_sent[s], 16)
                order(pool, piece, step, lambda e: None)
                for s in range(2):
                    pool.wait_ge(out_sent[s], NK // 2 * 16)

            @block.vector
            def _(dve):
                dve.wait_ge(weights, NW)
                dve.tensor_tensor(gbo[:, :, :], keep["gates"][:, 0, :, :], bo[:, :].unsqueeze(1).broadcast_to([P, B, E]), ALU.mult).then_inc(once, 1)

                def split_weights(e):
                    dve.wait_ge(w_hi, e + 1)
                    dve.tensor_tensor(w_s[:, 1, e], w_f[:, e % 2], w_s[:, 0, e], ALU.subtract).then_inc(w_split, 1)

                wide = lambda t: t.unsqueeze(2).broadcast_to([P, JT, NX])
                gate = lambda kind, b: keep["gates"][:, kind, bass.ds(b, 1), :].broadcast_to([P, 2, E])

                def normalise_heads(b, c, it, j):
                    s, u = c % 2, b * (CPB // 2) + c // 2
                    if j == 0:
                        dve.wait_ge(heads_in[s], (u * 16 + 16) * 2 * JT)
                        dve.wait_ge(wo_full[1], it)
                    v = sums_of[:, s, 4 * j:4 * j + 4, :]
                    dve.reciprocal(v, v).then_inc(rec_done, 1)
                    dve.wait_ge(rec_done, it * JT + j + 1)
                    dve.tensor_tensor(nrm[:, j], heads[:, s, 4 * j:4 * j + 4, :], v, ALU.mult).then_inc(nrm_done, 1)

                def residual_and_norm(b, c, it):
                    s = c % 2
                    dve.wait_ge(tp_done, it)
                    for m in range(2):
                        dve.wait_ge(wo_full[m], it + 1)
                        dve.tensor_tensor(att[:, 2 * m:2 * m + 2, :], halves(px[m]), gate(0, b), ALU.mult).then_inc(att_done[m], 1)
                    dve.wait_ge(xb_done, it + 1)
                    for m in range(2):
                        dve.wait_ge(att_done[m], it + 1)
                        dve.wait_ge(base_done[m], it)
                        last = dve.tensor_tensor(x1[:, 2 * m:2 * m + 2, :], att[:, 2 * m:2 * m + 2, :], x[:, s, 2 * m:2 * m + 2, :], ALU.add)
                    last.then_inc(x1_done, 1)
                    dve.wait_ge(x1_done, it + 1)
                    dve.memset(tick[:, :], 0.0)
                    for j in range(JT):
                        last = dve.bn_stats(stats[:, j, :], x1[:, j, :])
                    last.then_inc(ln_step, 1)
                    dve.wait_ge(ln_step, it * LN + 1)
                    dve.memset(tick[:, :], 0.0)
                    for j in range(JT):
                        last = dve.bn_aggr(mv[:, j, :], stats[:, j, :])
                    last.then_inc(ln_step, 1)
                    dve.wait_ge(ln_step, it * LN + 2)
                    dve.tensor_scalar(ve[:, :], mv[:, :, 1], EPS, None, ALU.add).then_inc(var_done, 1)
                    dve.wait_ge(sd_done, it + 1)
                    inverse_root(dve, rstd[:, :], sd[:, :], ve[:, :], r1[:, :], r2[:, :], ln_step, it * LN + 2)
                    for j in range(JT):
                        last = dve.tensor_scalar(xn[:, j, :], x1[:, j, :], mv[:, j, 0:1], rstd[:, j:j + 1],
                                                 ALU.subtract, ALU.mult)
                    last.then_inc(xn_done, 1)

                def route(b, c, it):
                    n = [0]

                    def link(ins):
                        n[0] += 1
                        ins.then_inc(route_step, 1)
                        dve.wait_ge(route_step, it * RS + n[0])
                    dve.wait_ge(lg_full, it + 1)
                    link(dve.tensor_tensor(lg[:, :, :], px[0][:, 0:JT * NX].rearrange("p (j n) -> p j n", n=NX),
                                           gbias[:, :].unsqueeze(1).broadcast_to([P, JT, NX]), ALU.add))
                    link(dve.reduce_max(mxs[:, :], lg[:, :, :], AX.X))
                    dve.tensor_tensor(sh[:, :, :], lg[:, :, :], wide(mxs[:, :]), ALU.subtract).then_inc(sh_done, 1)
                    dve.wait_ge(ex_done, it + 1)
                    link(dve.reduce_sum(sums[:, :], ex[:, :, :], AX.X))
                    link(dve.reciprocal(rsum[:, :], sums[:, :]))
                    link(dve.tensor_tensor(pr[:, :, :], ex[:, :, :], wide(rsum[:, :]), ALU.mult))
                    dve.memset(tick[:, :], 0.0)
                    for j in range(JT):
                        last = dve.max(out=top[:, j, :], in_=pr[:, j, :])
                    link(last)
                    dve.memset(tick[:, :], 0.0)
                    for j in range(JT):
                        last = dve.max_index(out=topi[:, j, :], in_max=top[:, j, :], in_values=pr[:, j, :])
                    link(last)
                    link(dve.tensor_copy(topf[:, :, :], topi[:, :, :]))
                    iota = keep["iota8"][:, :].unsqueeze(1).broadcast_to([P, JT, NX])
                    dve.tensor_tensor(o1[:, :, :], iota, wide(topf[:, :, 0]), ALU.is_equal)
                    link(dve.tensor_tensor(o2[:, :, :], iota, wide(topf[:, :, 1]), ALU.is_equal))
                    dve.tensor_tensor(g1[:, :, :], o1[:, :, :], wide(pr[:, :, 0]), ALU.mult)
                    link(dve.tensor_tensor(g2[:, :, :], o2[:, :, :], wide(pr[:, :, 1]), ALU.mult))
                    dve.tensor_tensor(cw[:, c % 2], g1[:, :, :], g2[:, :, :], ALU.add).then_inc(cw_done, 1)
                    link(dve.memset(tick[:, :], 0.0))
                    assert n[0] == RS

                def piece(b, c, it, n):
                    for j in ((0, 1), (2,), (3,))[n] if n < 3 else ():
                        normalise_heads(b, c, it, j)
                    if n == 3:
                        residual_and_norm(b, c, it)
                    if n == 5:
                        route(b, c, it)
                    if n == 5:
                        dve.wait_ge(hT_done, it + 1)
                        dve.tensor_tensor(hT_s[:, c % 2, 1], hT[:, c % 2], hT_s[:, c % 2, 0], ALU.subtract).then_inc(hT_split, 1)
                    if n == 7:
                        for m in range(2):
                            dve.wait_ge(bp_full[m], it + 1)
                            dve.wait_ge(base_done[m], it)
                            dve.tensor_tensor(wb[:, m], halves(px[m]), gate(1, b), ALU.mult).then_inc(wb_done[m], 1)

                def step(b, k):
                    if 1 <= k <= NS:
                        dve.wait_ge(p3_full[1], b * NS + max(k - LAG, 0))
                        n = k - 1
                        for eh in range(EH):
                            dve.wait_ge(h2_done[eh], b * NS + n + 1)
                            dve.tensor_tensor(h2_s[:, n % 2, 1, eh, :], h2_f[:, eh, :], h2_s[:, n % 2, 0, eh, :], ALU.subtract).then_inc(h2_split[eh], 1)
                    k -= LAG
                    if k < 0:
                        return
                    c, e = k // NX, k % NX
                    s, g = c % 2, b * NS + k
                    if e == 0:
                        dve.wait_ge(out_done[s], (b * (CPB // 2) + c // 2) * 2)
                        dve.wait_ge(cw_done, b * CPB + c + 1)
                    for m in range(2):
                        if e:
                            dve.wait_ge(p3_free[m], g)
                        dve.wait_ge(p3_full[m], g + 1)
                        for j in (2 * m, 2 * m + 1):
                            w = cw[:, s, j, e:e + 1]
                            if e == 0:
                                last = dve.tensor_scalar(y[:, s, j, :], p3[m][:, j % 2, :], w, None, ALU.mult)
                            else:
                                last = dve.scalar_tensor_tensor(out=y[:, s, j, :], in0=p3[m][:, j % 2, :], scalar=w,
                                                                in1=y[:, s, j, :], op0=ALU.mult, op1=ALU.add)
                        last.then_inc(p3_free[m], 1)
                order(dve, piece, step, split_weights)

            @block.scalar
            def _(act):
                def hi_weights(e):
                    act.wait_ge(w_in[e % 2], (e // 2 + 1) * 5 * 16)
                    act.activation(w_s[:, 0, e], w_f[:, e % 2], ACT.Copy).then_inc(w_hi, 1)

                def relu(hi, whole, src, bias, full, split, done, b, k):
                    for eh in range(EH):
                        act.wait_ge(full[eh], b * NS + k + 1)
                        act.activation(hi[:, k % 2, 0, eh, :], src[eh][:, :], ACT.Relu, bias=bias[:, k % NX, eh:eh + 1])
                        act.wait_ge(split[eh], b * NS + k)
                        act.activation(whole[:, eh, :], src[eh][:, :], ACT.Relu,
                                       bias=bias[:, k % NX, eh:eh + 1]).then_inc(done[eh], 1)

                def piece(b, c, it, n):
                    if n == 3:
                        if c == 0:
                            for k, name in enumerate(("shift_b", "scale_b")):
                                act.activation(mod_now[:, k, :].unsqueeze(2), keep[name][:, :, bass.ds(b, 1)], ACT.Copy).then_inc(mod_set, 1)
                            act.wait_ge(mod_set, b * 2 + 2)
                        act.wait_ge(var_done, it + 1)
                        act.activation(sd[:, :], ve[:, :], ACT.Sqrt).then_inc(sd_done, 1)
                    if n == 4:
                        act.wait_ge(lg_full, it)
                        act.wait_ge(tp_done, it + 1)
                        for dst in (hT_s[:, c % 2, 0], hT[:, c % 2]):
                            for eh in range(EH):
                                last = act.activation(dst[:, eh, :], px[eh][:, :], ACT.Identity, bias=mod_now[:, 0, eh:eh + 1],
                                                      scale=mod_now[:, 1, eh:eh + 1])
                        last.then_inc(hT_done, 1)
                    if n == 5:
                        act.wait_ge(sh_done, it + 1)
                        act.activation(ex[:, :, :], sh[:, :, :], ACT.Exp).then_inc(ex_done, 1)
                    if n == 6:
                        act.wait_ge(cp_full, it + 1)
                        act.activation(cwT[:, :], px[1][0:NX, :], ACT.Copy).then_inc(cwT_done, 1)

                def step(b, k):
                    if k < NS:
                        act.wait_ge(p2_full[EH - 1], b * NS + max(k - 1, 0))
                        relu(h1_s, h1_f, p1, b1, p1_full, h1_split, h1_done, b, k)
                    if 1 <= k <= NS:
                        act.wait_ge(p3_full[1], b * NS + max(k - LAG, 0))
                        relu(h2_s, h2_f, p2, b2, p2_full, h2_split, h2_done, b, k - 1)
                order(act, piece, step, hi_weights)

            @block.tensor
            def _(pe):
                pe.wait_ge(weights, NW)

                PARTS = ((0, 0), (0, 1), (1, 0))

                def layer(b, k, i, src, dst, full, free):
                    for eh in range(EH):
                        pe.wait_ge(free[eh], b * NS + k)
                        for n, (pw, px_) in enumerate(PARTS):
                            for ki in range(EH):
                                last = pe.matmul(dst[eh][:, :], w_s[:, pw, k % NX, i, ki, eh * P:(eh + 1) * P], src[:, px_, ki, :],
                                                 start=(n == ki == 0), stop=(n == 2 and ki == EH - 1))
                        last.then_inc(full[eh], 1)

                def step(b, k):
                    if k < NS:
                        if k % NX == 0:
                            pe.wait_ge(hT_split, b * CPB + k // NX + 1)
                        pe.wait_ge(w_split, k + 1 if k < NX else NX)
                        layer(b, k, 0, hT_s[:, k // NX % 2], p1, p1_full, h1_done)
                    if 1 <= k <= NS:
                        for eh in range(EH):
                            pe.wait_ge(h1_split[eh], b * NS + k)
                        layer(b, k - 1, 1, h1_s[:, (k - 1) % 2], p2, p2_full, h2_done)
                    if k >= LAG:
                        k -= LAG
                        for eh in range(EH):
                            pe.wait_ge(h2_split[eh], b * NS + k + 1)
                        for m in range(2):
                            pe.wait_ge(p3_free[m], b * NS + k)
                            for j in range(2):
                                for n, (ph, pw) in enumerate(PARTS):
                                    for ki in range(EH):
                                        last = pe.matmul(p3[m][:, j, :], h2_s[:, k % 2, ph, ki, (2 * m + j) * P:(2 * m + j + 1) * P],
                                                         w_s[:, pw, k % NX, 2, ki, :], start=(n == ki == 0), stop=(n == 2 and ki == EH - 1))
                            last.then_inc(p3_full[m], 1)

                def piece(b, c, it, n):
                    s = c % 2
                    if n == 2:
                        for m in range(2):
                            pe.wait_ge(wb_done[m], it)
                        pe.wait_ge(nrm_done, it * JT + JT)
                        for m in range(2):
                            for j in (2 * m, 2 * m + 1):
                                for g in range(4):
                                    last = pe.matmul(halves(px[m])[:, j % 2, :], nrm[:, j, g, :], wo[:, g, :], start=(g == 0), stop=(g == 3))
                            last.then_inc(wo_full[m], 1)
                    if n == 3:
                        pe.wait_ge(xn_done, it + 1)
                        for eh in range(EH):
                            for j in range(JT):
                                last = pe.transpose(px[eh][:, j * P:(j + 1) * P], xn[:, j, eh * P:(eh + 1) * P], keep["ident"][:, :])
                        last.then_inc(tp_done, 1)
                    if n == 4:
                        pe.wait_ge(hT_done, it + 1)
                        for j in range(JT):
                            for eh in range(EH):
                                last = pe.matmul(px[0][:, j * NX:(j + 1) * NX], hT[:, s, eh, j * P:(j + 1) * P], gw[:, eh, :],
                                                 start=(eh == 0), stop=(eh == EH - 1))
                        last.then_inc(lg_full, 1)
                    if n == 5:
                        pe.wait_ge(cw_done, it + 1)
                        for j in range(JT):
                            last = pe.transpose(px[1][0:NX, j * P:(j + 1) * P], cw[:, s, j, :], keep["ident"][:, :])
                        last.then_inc(cp_full, 1)
                    if n == 6:
                        pe.wait_ge(cwT_done, it + 1)
                        for m in range(2):
                            for j in range(2):
                                last = pe.matmul(halves(px[m])[:, j, :], cwT[:, (2 * m + j) * P:(2 * m + j + 1) * P], b3[:, :],
                                                 start=True, stop=True)
                            last.then_inc(bp_full[m], 1)
                order(pe, piece, step, lambda e: None, piece_first=False)


SCRATCH = {
    "s_rel": ([2, D, TAB + 2 * G], F16),
    "s_q": ([2, B * NB, EH * P, P], F16),
    "s_k": ([2, B * NB, EH * P, P], F16),
    "s_v": ([B * NB, P, H, 2 * D], F32),
    "s_m": ([B * NB, H, P], F16),
    "s_of": ([B * NB, 4, P, P], F32),
    "s_o": ([B * NB, 4, P, P], F32),
}

KEEP = {
    "ident": ([P, P], F32), "mask_h": ([P, HH], F16), "mask_i": ([P, G], F16),
    "ident_s": ([G, H, G], F16), "mask_f": ([G, P], F16), "iota8": ([P, NX], F32),
    "ident_m": ([P, P], F16), "mask_n": ([P, P], F16),
    "table": ([P, 2, TAB], F16),
    "shift_a": ([P, EH, B], F32), "scale_a": ([P, EH, B], F32),
    "shift_b": ([P, EH, B], F32), "scale_b": ([P, EH, B], F32), "gates": ([P, 2, B, E], F32),
}


def adaln_moe_layer(nc, **io):
    for name, (shape, dt) in SCRATCH.items():
        io[name] = nc.dram_tensor(name, shape, dt).ap()
    with ExitStack() as ctx:
        keep = {name: ctx.enter_context(nc.sbuf_tensor(name, shape, dt)) for name, (shape, dt) in KEEP.items()}
        phase_modulation(nc, io, keep)
        phase_project(nc, io, keep)
        phase_row_max(nc, io, keep)
        phase_far(nc, io, keep)
        phase_near(nc, io, keep)
        phase_ffn(nc, io, keep)


def kernel(**inputs):
    import numpy as _np
    import concourse.bacc as _bacc
    from concourse import mybir as _mybir
    from concourse.bass_utils import run_bass_kernel_spmd as _run

    def heads_inside(w):
        return w.reshape(-1, EH, HH, D).transpose(0, 1, 3, 2).reshape(w.shape)

    def on_partitions(v):
        return v.reshape(v.shape[:-1] + (EH, P)).swapaxes(-1, -2)

    get = {name: _np.asarray(v) for name, v in inputs.items()}
    r0 = _np.broadcast_to(get["L0_attn_rel_key"][0][None, :, None], (EH, D, HH)).reshape(E)
    laid = {
        "x": get["L0_attn_x"], "wq": heads_inside(get["L0_attn_Wq"]), "wk": heads_inside(get["L0_attn_Wk"]),
        "wv": get["L0_attn_Wv"], "wo": get["L0_attn_Wo"], "bv": get["L0_attn_bv"], "bo": get["L0_attn_bo"],
        "bq": on_partitions(heads_inside(get["L0_attn_bq"])), "bk": on_partitions(heads_inside(get["L0_attn_bk"])),
        "r0": on_partitions(r0), "relT": get["L0_attn_rel_key"].T, "cT": get["L0_c"].T, "wmod": get["L0_wmod"],
        "gwT": get["L0_ffn_gate_w"].T, "gate_b": get["L0_ffn_gate_b"],
        "w1": get["L0_ffn_w1"], "w2": get["L0_ffn_w2"], "w3": get["L0_ffn_w3"],
        "b1": on_partitions(get["L0_ffn_b1"]), "b2": on_partitions(get["L0_ffn_b2"]), "b3": get["L0_ffn_b3"],
    }
    nc = _bacc.Bacc("TRN2", target_bir_lowering=False, num_devices=1)
    arrays, io = {}, {}
    for name, v in laid.items():
        v = _np.ascontiguousarray(v)
        arrays[f"in_{name}"] = v
        io[name] = nc.dram_tensor(f"in_{name}", v.shape, _mybir.dt.from_np(v.dtype), kind="ExternalInput").ap()
    io["out"] = nc.dram_tensor("out_0", (B, S, E), _mybir.dt.from_np(_np.dtype("float32")), kind="ExternalOutput").ap()
    adaln_moe_layer(nc, **io)
    r = _run(nc, [arrays], core_ids=[0])
    return r.results[0]["out_0"]
```
